# Optimizing a Trainium2 kernel written in Bass

```python
import numpy as np
import jax
import jax.numpy as jnp

def _softmax(x, axis=-1):
    return jax.nn.softmax(x, axis=axis)

def _gelu(x):
    return jax.nn.gelu(x, approximate=True)

def _silu(x):
    return jax.nn.silu(x)

def _sigmoid(x):
    return jax.nn.sigmoid(x)

def _layernorm(x, axis=-1, eps=1e-05):
    m = jnp.mean(x, axis=axis, keepdims=True)
    v = jnp.var(x, axis=axis, keepdims=True)
    return (x - m) / jnp.sqrt(v + eps)

def _scatter_add(tgt, idx, src, axis=0):
    return tgt.at[idx].add(src)

def _segment_sum(src, seg, n):
    return jax.ops.segment_sum(src, seg, n)
kernel_name = 'mk_recurrent_d2_jaxref_r8_d492d1'

def setup_inputs(seed: int=0):
    np.random.seed(seed)
    _w = jnp.asarray

    def _L0_attn_setup():
        import jax, jax.numpy as jnp
        import numpy as np
        DIM, SSM, RNN = (128, 64, 128)
        key = jax.random.key(seed)
        ks = jax.random.split(key, 16)
        s = 0.02
        B, N = (8, 256)
        return {'x': jax.random.normal(ks[0], (B, N, DIM), jnp.float32), 'A': jax.random.normal(ks[1], (SSM, SSM), jnp.float32) * s, 'Bw': jax.random.normal(ks[2], (SSM, DIM), jnp.float32) * s, 'Bb': jnp.zeros((SSM,), jnp.float32), 'Cw': jax.random.normal(ks[3], (DIM, SSM), jnp.float32) * s, 'Cb': jnp.zeros((DIM,), jnp.float32), 'Dw': jax.random.normal(ks[4], (DIM, DIM), jnp.float32) * s, 'Db': jnp.zeros((DIM,), jnp.float32), 'W_ih': jax.random.normal(ks[5], (3 * RNN, DIM), jnp.float32) * s, 'b_ih': jnp.zeros((3 * RNN,), jnp.float32), 'W_hh': jax.random.normal(ks[6], (3 * RNN, RNN), jnp.float32) * s, 'b_hh': jnp.zeros((3 * RNN,), jnp.float32), 'proj_w': jax.random.normal(ks[7], (DIM, RNN), jnp.float32) * s, 'proj_b': jnp.zeros((DIM,), jnp.float32), 'gate_w': jax.random.normal(ks[8], (2, DIM), jnp.float32) * s, 'gate_b': jnp.zeros((2,), jnp.float32)}
    _L0_attn_in = _L0_attn_setup()

    def _L0_ffn_setup():
        import jax, jax.numpy as jnp
        import numpy as np
        DIM = 128
        N_EXPERTS = 8
        TOPK = 2
        CAPACITY_FACTOR = 1.25
        B, S = (2, 256)

        def _moe(x, Wr, W1, b1, W2, b2):
            Bsz, Sl, D = x.shape
            E = Wr.shape[1]
            T = Bsz * Sl
            capacity = max(1, int(T * CAPACITY_FACTOR / E))
            xt = x.reshape(T, D)
            probs_full = jax.nn.softmax(xt @ Wr, axis=-1)
            topv, topi = jax.lax.top_k(probs_full, TOPK)
            topv = topv / jnp.sum(topv, axis=-1, keepdims=True)
            onehot = jax.nn.one_hot(topi, E, dtype=x.dtype)
            rank = jnp.cumsum(onehot, axis=0)
            keep = (rank <= capacity).astype(x.dtype) * onehot
            w = jnp.einsum('tk,tke->te', topv, keep)
            h = jax.nn.gelu(jnp.einsum('td,edf->etf', xt, W1) + b1[:, None, :], approximate=False)
            y = jnp.einsum('etf,efd->etd', h, W2) + b2[:, None, :]
            out = jnp.einsum('te,etd->td', w, y)
            return out.reshape(Bsz, Sl, D)
        key = jax.random.key(seed)
        ks = jax.random.split(key, 6)
        D, E, F = (DIM, N_EXPERTS, 4 * DIM)
        x = jax.random.normal(ks[0], (B, S, D), dtype=jnp.float32)
        Wr = jax.random.normal(ks[1], (D, E), dtype=jnp.float32) * (1.0 / np.sqrt(D))
        W1 = jax.random.normal(ks[2], (E, D, F), dtype=jnp.float32) * (1.0 / np.sqrt(D))
        b1 = jnp.zeros((E, F), dtype=jnp.float32)
        W2 = jax.random.normal(ks[3], (E, F, D), dtype=jnp.float32) * (1.0 / np.sqrt(F))
        b2 = jnp.zeros((E, D), dtype=jnp.float32)
        return {'x': x, 'Wr': Wr, 'W1': W1, 'b1': b1, 'W2': W2, 'b2': b2}
    _L0_ffn_in = _L0_ffn_setup()

    def _L1_attn_setup():
        import jax, jax.numpy as jnp
        import numpy as np
        HIDDEN = 128
        HEADS = 16
        HEAD_DIM = 64
        key = jax.random.key(seed)
        ks = jax.random.split(key, 9)
        d = HEADS * HEAD_DIM
        s = 0.02
        return {'x': jax.random.normal(ks[0], (2, 256, HIDDEN), dtype=jnp.float32), 'wq': jax.random.normal(ks[1], (d, HIDDEN), dtype=jnp.float32) * s, 'bq': jnp.zeros((d,), dtype=jnp.float32), 'wk': jax.random.normal(ks[2], (d, HIDDEN), dtype=jnp.float32) * s, 'bk': jnp.zeros((d,), dtype=jnp.float32), 'wv': jax.random.normal(ks[3], (d, HIDDEN), dtype=jnp.float32) * s, 'bv': jnp.zeros((d,), dtype=jnp.float32), 'wo': jax.random.normal(ks[4], (HIDDEN, d), dtype=jnp.float32) * s, 'bo': jnp.zeros((HIDDEN,), dtype=jnp.float32)}
    _L1_attn_in = _L1_attn_setup()

    def _L1_ffn_setup():
        import jax, jax.numpy as jnp
        import numpy as np
        NUM_EXPERTS = 160
        TOP_K = 8
        ROUTED_SCALE = 2.5
        HIDDEN = 128
        INTER = 64
        key = jax.random.key(seed)
        ks = jax.random.split(key, 7)
        B, S = (1, 256)
        return {'hidden_states': jax.random.normal(ks[0], (B, S, HIDDEN), dtype=jnp.float32), 'router_w': jax.random.normal(ks[1], (NUM_EXPERTS, HIDDEN), dtype=jnp.float32) * 0.02, 'expert_bias': jnp.zeros((NUM_EXPERTS,), dtype=jnp.float32), 'w_gate': jax.random.normal(ks[2], (NUM_EXPERTS, INTER, HIDDEN), dtype=jnp.float32) * 0.02, 'w_down': jax.random.normal(ks[3], (NUM_EXPERTS, HIDDEN, INTER), dtype=jnp.float32) * 0.02, 'w_gate_shared': jax.random.normal(ks[4], (INTER, HIDDEN), dtype=jnp.float32) * 0.02, 'w_down_shared': jax.random.normal(ks[5], (HIDDEN, INTER), dtype=jnp.float32) * 0.02}
    _L1_ffn_in = _L1_ffn_setup()
    _d = {'L0_attn_x': _L0_attn_in['x'], 'L0_attn_A': _L0_attn_in['A'], 'L0_attn_Bw': _L0_attn_in['Bw'], 'L0_attn_Bb': _L0_attn_in['Bb'], 'L0_attn_Cw': _L0_attn_in['Cw'], 'L0_attn_Cb': _L0_attn_in['Cb'], 'L0_attn_Dw': _L0_attn_in['Dw'], 'L0_attn_Db': _L0_attn_in['Db'], 'L0_attn_W_ih': _L0_attn_in['W_ih'], 'L0_attn_b_ih': _L0_attn_in['b_ih'], 'L0_attn_W_hh': _L0_attn_in['W_hh'], 'L0_attn_b_hh': _L0_attn_in['b_hh'], 'L0_attn_proj_w': _L0_attn_in['proj_w'], 'L0_attn_proj_b': _L0_attn_in['proj_b'], 'L0_attn_gate_w': _L0_attn_in['gate_w'], 'L0_attn_gate_b': _L0_attn_in['gate_b'], 'L0_ffn_Wr': _L0_ffn_in['Wr'], 'L0_ffn_W1': _L0_ffn_in['W1'], 'L0_ffn_b1': _L0_ffn_in['b1'], 'L0_ffn_W2': _L0_ffn_in['W2'], 'L0_ffn_b2': _L0_ffn_in['b2'], 'L1_attn_wq': _L1_attn_in['wq'], 'L1_attn_bq': _L1_attn_in['bq'], 'L1_attn_wk': _L1_attn_in['wk'], 'L1_attn_bk': _L1_attn_in['bk'], 'L1_attn_wv': _L1_attn_in['wv'], 'L1_attn_bv': _L1_attn_in['bv'], 'L1_attn_wo': _L1_attn_in['wo'], 'L1_attn_bo': _L1_attn_in['bo'], 'L1_ffn_router_w': _L1_ffn_in['router_w'], 'L1_ffn_expert_bias': _L1_ffn_in['expert_bias'], 'L1_ffn_w_gate': _L1_ffn_in['w_gate'], 'L1_ffn_w_down': _L1_ffn_in['w_down'], 'L1_ffn_w_gate_shared': _L1_ffn_in['w_gate_shared'], 'L1_ffn_w_down_shared': _L1_ffn_in['w_down_shared']}
    _x0 = _d['L0_attn_x']
    _d['L0_attn_x'] = jax.random.normal(jax.random.fold_in(jax.random.key(seed), 1), (16, 256, 128), dtype=_x0.dtype)
    del _x0
    return _d

def reference(L0_attn_x, L0_attn_A, L0_attn_Bw, L0_attn_Bb, L0_attn_Cw, L0_attn_Cb, L0_attn_Dw, L0_attn_Db, L0_attn_W_ih, L0_attn_b_ih, L0_attn_W_hh, L0_attn_b_hh, L0_attn_proj_w, L0_attn_proj_b, L0_attn_gate_w, L0_attn_gate_b, L0_ffn_Wr, L0_ffn_W1, L0_ffn_b1, L0_ffn_W2, L0_ffn_b2, L1_attn_wq, L1_attn_bq, L1_attn_wk, L1_attn_bk, L1_attn_wv, L1_attn_bv, L1_attn_wo, L1_attn_bo, L1_ffn_router_w, L1_ffn_expert_bias, L1_ffn_w_gate, L1_ffn_w_down, L1_ffn_w_gate_shared, L1_ffn_w_down_shared):

    def _L0_attn_ref(x, A, Bw, Bb, Cw, Cb, Dw, Db, W_ih, b_ih, W_hh, b_hh, proj_w, proj_b, gate_w, gate_b):
        import jax, jax.numpy as jnp
        import numpy as np
        DIM, SSM, RNN = (128, 64, 128)
        B, N, D = x.shape
        R = W_hh.shape[1]
        bx = jnp.einsum('bnd,sd->bns', x, Bw) + Bb
        dx = jnp.einsum('bnd,ed->bne', x, Dw) + Db
        gx = jax.nn.sigmoid(jnp.einsum('bnd,gd->bng', x, gate_w) + gate_b)
        ih = jnp.einsum('bnd,rd->bnr', x, W_ih) + b_ih
        bx_t = jnp.swapaxes(bx, 0, 1)
        dx_t = jnp.swapaxes(dx, 0, 1)
        gx_t = jnp.swapaxes(gx, 0, 1)
        ih_t = jnp.swapaxes(ih, 0, 1)
        h_ssm0 = jnp.zeros((B, A.shape[0]), x.dtype)
        h_rnn0 = jnp.zeros((B, R), x.dtype)

        def step(carry, inp):
            h_ssm, h_rnn = carry
            bxt, dxt, gxt, iht = inp
            h_ssm = jax.nn.silu(h_ssm @ A.T + bxt)
            y_ssm = h_ssm @ Cw.T + Cb + dxt
            hh = h_rnn @ W_hh.T + b_hh
            i_r, i_z, i_n = jnp.split(iht, 3, axis=-1)
            h_r, h_z, h_n = jnp.split(hh, 3, axis=-1)
            r = jax.nn.sigmoid(i_r + h_r)
            z = jax.nn.sigmoid(i_z + h_z)
            n = jnp.tanh(i_n + r * h_n)
            h_rnn = (1.0 - z) * n + z * h_rnn
            y_rnn = h_rnn @ proj_w.T + proj_b
            fused = gxt[:, :1] * y_ssm + gxt[:, 1:2] * y_rnn
            return ((h_ssm, h_rnn), fused)
        _, out = jax.lax.scan(step, (h_ssm0, h_rnn0), (bx_t, dx_t, gx_t, ih_t))
        return jnp.swapaxes(out, 0, 1)

    def _L0_ffn_ref(x, Wr, W1, b1, W2, b2):
        import jax, jax.numpy as jnp
        import numpy as np
        DIM = 128
        N_EXPERTS = 8
        TOPK = 2
        CAPACITY_FACTOR = 1.25
        B, S = (2, 256)

        def _moe(x, Wr, W1, b1, W2, b2):
            Bsz, Sl, D = x.shape
            E = Wr.shape[1]
            T = Bsz * Sl
            capacity = max(1, int(T * CAPACITY_FACTOR / E))
            xt = x.reshape(T, D)
            probs_full = jax.nn.softmax(xt @ Wr, axis=-1)
            topv, topi = jax.lax.top_k(probs_full, TOPK)
            topv = topv / jnp.sum(topv, axis=-1, keepdims=True)
            onehot = jax.nn.one_hot(topi, E, dtype=x.dtype)
            rank = jnp.cumsum(onehot, axis=0)
            keep = (rank <= capacity).astype(x.dtype) * onehot
            w = jnp.einsum('tk,tke->te', topv, keep)
            h = jax.nn.gelu(jnp.einsum('td,edf->etf', xt, W1) + b1[:, None, :], approximate=False)
            y = jnp.einsum('etf,efd->etd', h, W2) + b2[:, None, :]
            out = jnp.einsum('te,etd->td', w, y)
            return out.reshape(Bsz, Sl, D)
        return _moe(x, Wr, W1, b1, W2, b2)

    def _L1_attn_ref(x, wq, bq, wk, bk, wv, bv, wo, bo):
        import jax, jax.numpy as jnp
        import numpy as np
        HIDDEN = 128
        HEADS = 16
        HEAD_DIM = 64
        b, s, _ = x.shape
        scale = 1.0 / np.sqrt(HEAD_DIM).astype(np.float32)

        def proj(w, bias):
            y = jnp.einsum('bsh,dh->bsd', x, w) + bias
            return y.reshape(b, s, HEADS, HEAD_DIM).transpose(0, 2, 1, 3)
        q = proj(wq, bq)
        k = proj(wk, bk)
        v = proj(wv, bv)
        scores = jnp.einsum('bhqd,bhkd->bhqk', q, k) * scale
        attn = jax.nn.softmax(scores, axis=-1)
        ctx = jnp.einsum('bhqk,bhkd->bhqd', attn, v)
        ctx = ctx.transpose(0, 2, 1, 3).reshape(b, s, HEADS * HEAD_DIM)
        return jnp.einsum('bsd,hd->bsh', ctx, wo) + bo

    def _L1_ffn_ref(hidden_states, router_w, expert_bias, w_gate, w_down, w_gate_shared, w_down_shared):
        import jax, jax.numpy as jnp
        import numpy as np
        NUM_EXPERTS = 160
        TOP_K = 8
        ROUTED_SCALE = 2.5
        HIDDEN = 128
        INTER = 64
        B, S, H = hidden_states.shape
        x = hidden_states.reshape(-1, H)
        T = x.shape[0]
        logits = x @ router_w.T + expert_bias[None, :]
        probs = jax.nn.sigmoid(logits)
        top_w, top_idx = jax.lax.top_k(probs, TOP_K)
        top_w = top_w / (jnp.sum(top_w, axis=-1, keepdims=True) + 1e-09)
        top_w = top_w * ROUTED_SCALE
        combine = jnp.zeros((T, NUM_EXPERTS), dtype=x.dtype)
        combine = combine.at[jnp.arange(T)[:, None], top_idx].set(top_w)
        h1 = jax.nn.silu(jnp.einsum('th,eih->eti', x, w_gate))
        h1w = h1 * combine.T[:, :, None]
        routed = jnp.einsum('eti,ehi->th', h1w, w_down)
        shared = jax.nn.silu(x @ w_gate_shared.T) @ w_down_shared.T
        return (routed + shared).reshape(B, S, H)
    x = L0_attn_x
    xn = _layernorm(x, axis=-1)
    s = _L0_attn_ref(xn, L0_attn_A, L0_attn_Bw, L0_attn_Bb, L0_attn_Cw, L0_attn_Cb, L0_attn_Dw, L0_attn_Db, L0_attn_W_ih, L0_attn_b_ih, L0_attn_W_hh, L0_attn_b_hh, L0_attn_proj_w, L0_attn_proj_b, L0_attn_gate_w, L0_attn_gate_b)
    g = _silu(_L0_ffn_ref(xn, L0_ffn_Wr, L0_ffn_W1, L0_ffn_b1, L0_ffn_W2, L0_ffn_b2))
    x = x + s * g
    xn = _layernorm(x, axis=-1)
    s = _L1_attn_ref(xn, L1_attn_wq, L1_attn_bq, L1_attn_wk, L1_attn_bk, L1_attn_wv, L1_attn_bv, L1_attn_wo, L1_attn_bo)
    g = _silu(_L1_ffn_ref(xn, L1_ffn_router_w, L1_ffn_expert_bias, L1_ffn_w_gate, L1_ffn_w_down, L1_ffn_w_gate_shared, L1_ffn_w_down_shared))
    x = x + s * g
    return x

_drawn_inputs = setup_inputs


def setup_inputs(seed=0):
    import zlib

    import numpy as np

    out = dict(_drawn_inputs(seed))
    spreads = {'L0_attn_Bb': (0.0, 0.8),
     'L0_attn_Cb': (0.0, 0.508),
     'L0_attn_Db': (0.0, 0.559),
     'L0_attn_b_ih': (0.0, 0.8),
     'L0_attn_b_hh': (0.0, 0.8),
     'L0_attn_proj_b': (0.0, 0.53),
     'L0_attn_gate_b': (0.0, 0.8),
     'L0_ffn_b1': (0.0, 0.8),
     'L0_ffn_b2': (0.0, 0.8),
     'L1_attn_bq': (0.0, 0.8),
     'L1_attn_bk': (0.0, 0.8),
     'L1_attn_bv': (0.0, 0.8),
     'L1_attn_bo': (0.0, 0.8),
     'L1_ffn_expert_bias': (0.0, 0.8)}
    factors = {'L0_attn_A': 8.0,
     'L0_attn_Bw': 8.0,
     'L0_attn_Cw': 8.0,
     'L0_attn_W_ih': 8.0,
     'L0_attn_W_hh': 8.0,
     'L0_attn_proj_w': 8.0,
     'L0_attn_gate_w': 8.0,
     'L1_attn_wq': 8.0,
     'L1_attn_wk': 8.0,
     'L1_attn_wv': 8.0,
     'L1_attn_wo': 8.0,
     'L1_ffn_router_w': 8.0,
     'L1_ffn_w_gate': 8.0,
     'L1_ffn_w_down': 8.0,
     'L1_ffn_w_gate_shared': 8.0,
     'L1_ffn_w_down_shared': 8.0}
    for name, (base, spread) in spreads.items():
        noise = np.random.default_rng([zlib.crc32(name.encode()), seed]).standard_normal(out[name].shape)
        drawn = base * np.exp(spread * noise) if base else spread * noise
        out[name] = jnp.asarray(drawn.astype(out[name].dtype))
    for name, factor in factors.items():
        out[name] = (out[name] * factor).astype(out[name].dtype)
    return out
```

```python
from contextlib import ExitStack

import numpy as np

import concourse.bass as bass
from concourse import mybir

ALU = mybir.AluOpType
ACT = mybir.ActivationFunctionType
F32 = mybir.dt.float32
AX_X = mybir.AxisListType.X

P = 128
B, T = 16, 256
NTOK = B * T
NT = NTOK // P
NG = NTOK // 512
E0, F0 = 8, 512
FC = F0 // P
CAP0 = int(NTOK * 1.25 / E0)
EPS = 1e-5
HEADS, HD = 16, 64
PAIRS = HEADS // 2
E1, TOPK1, F1 = 160, 8, 64
EG = 512 // F1
NEG = E1 // EG


class Count:

    def __init__(self, sem):
        self.sem, self.n = sem, 0

    def raised_by(self, ins):
        self.n += 1
        ins.then_inc(self.sem, 1)
        return self.n


def build(nc, x, gin_w, half_w, misc_w, cols, rows, b2_blocks, w1, b1, w2,
          attn_w, attn_cols, attn_rows, router, router_row, w_gate, w_down, shared_gate, shared_down, out):
    with ExitStack() as ctx:
        def sb(name, shape, dt=F32):
            return ctx.enter_context(nc.sbuf_tensor(name, shape, dt))

        def bank(name):
            return ctx.enter_context(nc.psum_tensor(name, [P, 512], F32))

        def sem(name):
            return ctx.enter_context(nc.semaphore(name))

        x_tok = sb("x_tok", [P, NT, P])
        xn_tok = sb("xn_tok", [P, NT, P])
        xnT = sb("xnT", [P, NTOK])
        ln_sum = sb("ln_sum", [P, NT])
        ln_mean = sb("ln_mean", [P, NT])
        ln_sq = sb("ln_sq", [P, NT])
        ln_std = sb("ln_std", [P, NT])
        ln_rstd = sb("ln_rstd", [P, NT])
        eps_col = sb("eps_col", [P, 1])
        misc = sb("misc", [P, 128 * 4 + 8 + 10])
        ident, upper, ones = misc[:, 0:128], misc[:, 128:256], misc[:, 256:384]
        dwT, desc, rgT = misc[:, 384:512], misc[:, 512:520], misc[:, 520:530]
        rows_sb = sb("rows_sb", [1, 3 * 128 + 10])
        layer0 = ExitStack()

        def sb(name, shape, dt=F32, stack=layer0):
            return stack.enter_context(nc.sbuf_tensor(name, shape, dt))

        ginw = sb("ginw", [P, 4 * 128])
        halfw = sb("halfw", [P, 6 * 128])
        whr, whz, whn, aT, cwT, projT = (halfw[:, 128 * k:128 * k + 128] for k in range(6))
        cols_sb = sb("cols_sb", [P, 8])
        gin_bias = sb("gin_bias", [P, 4])
        gin = sb("gin", [P, 5, B, T])
        hist_g = sb("hist_g", [P, B, T + 1])
        hist_s = sb("hist_s", [P, B, T + 1])
        b2blk = sb("b2blk", [P, 16 * P])
        w1_sb = sb("w1_sb", [P, 2, F0])
        w2_sb = sb("w2_sb", [P, 2, FC, P])
        b1_sb = sb("b1_sb", [P, (E0 + 1) * FC])
        h_sb = sb("h_sb", [P, 2, 512])
        w_te = sb("w_te", [P, NT, E0])
        gate = sb("gate", [P, NT, 2])
        th = sb("th", [P, 2, 48])
        cand = sb("cand", [P, 2, 16])
        mixn = sb("mixn", [P, 16])
        sumn = sb("sumn", [P, 2, 16])
        zg = sb("zg", [P, 16])
        omz = sb("omz", [P, 16])
        newn = sb("newn", [P, 16])
        scr = hist_g[:, :, :].rearrange("p b t -> p (b t)")
        scr2 = hist_s[:, :, :].rearrange("p b t -> p (b t)")
        layer0.close()

        def sb(name, shape, dt=F32):
            return ctx.enter_context(nc.sbuf_tensor(name, shape, dt))

        gate1 = sb("gate1", [P, E1 * F1])
        down1 = sb("down1", [P, E1 // 2, P])
        comb = sb("comb", [P, NT, E1])
        hsT = sb("hsT", [P, NTOK])
        aw = sb("aw", [P, 4, HEADS * HD])
        acols = sb("acols", [P, 2, PAIRS])
        arows = sb("arows", [P, HEADS * HD + P])
        sg_w = sb("sg_w", [P, F1])
        sd_w = sb("sd_w", [F1, P])
        xb = sb("xb", [P, 2, 2 * P])
        qT = sb("qT", [P, 2, T])
        kT = sb("kT", [P, 2, T])
        v_sb = sb("v_sb", [P, 2, 2, P])
        rT = v_sb[:, 0, :, :].rearrange("p i d -> p (i d)")[:, 0:E1]
        rrow = v_sb[0:1, 1, :, :].rearrange("p i d -> p (i d)")[:, 0:E1]
        probs = sb("probs", [P, 2, 2, T])
        probsT = sb("probsT", [P, 2, 2, T])
        negmax = sb("negmax", [P, 2, 2])
        sums = sb("sums", [P, 4, 2, 2])
        rsums = sb("rsums", [P, 2, 2])
        ctx_sb = sb("ctx_sb", [P, 2, P])
        ctxT = sb("ctxT", [P, 2 * P])
        top8 = probsT[:, 0, :, :].rearrange("p c t -> p (c t)")[:, 0:NT * TOPK1].rearrange("p (n e) -> p n e", e=TOPK1)
        rest = probs[:, 0, 0, 0:E1]
        h1 = probs[:, :, :, :].rearrange("p a i t -> p a (i t)")
        h1T = probsT[:, :, :, :].rearrange("p a c t -> p a (c t)")
        g1, gs = qT[:, 0, 0:P], kT[:, 0, 0:P]

        ps_rec = [bank("ps_rec0"), bank("ps_rec1")]
        ps_up = [bank("ps_up0"), bank("ps_up1")]
        ps_y = ctx.enter_context(nc.psum_tensor("ps_y", [P, 2, 512], F32))
        ps_t = [bank("ps_t0"), bank("ps_t1")]
        ps_qk, ps_v, ps_s, ps_ctx, ps_o = ps_rec[0], ps_rec[1], ps_up, ps_t[0], ps_t[1]

        x_loaded = [sem(f"x_loaded{c}") for c in range(4)]
        consts_loaded = sem("consts_loaded")
        w1_loaded = [sem("w1_loaded0"), sem("w1_loaded1")]
        w2_loaded = [sem("w2_loaded0"), sem("w2_loaded1")]
        dve_done = sem("dve_done")
        act_done = sem("act_done")
        centred = sem("centred")
        squared = sem("squared")
        var_ready = sem("var_ready")
        std_ready = sem("std_ready")
        xn_ready = sem("xn_ready")
        turned = sem("turned")
        xnT_ready = sem("xnT_ready")
        gin_mm = sem("gin_mm")
        gin_act = sem("gin_act")
        gin_dve = sem("gin_dve")
        biases_ready = sem("biases_ready")
        bhn_ready = sem("bhn_ready")
        logits_ready = sem("logits_ready")
        shifted = sem("shifted")
        exps_ready = sem("exps_ready")
        onehot_ready = sem("onehot_ready")
        ranks_ready = sem("ranks_ready")
        w_ready = sem("w_ready")
        wT_mm = sem("wT_mm")
        wT_ready = sem("wT_ready")
        b2_mm = sem("b2_mm")
        b2_copied = sem("b2_copied")
        rnn_ready = sem("rnn_ready")
        ssm_ready = sem("ssm_ready")
        pre_ready = sem("pre_ready")
        th_ready = sem("th_ready")
        sumn_ready = sem("sumn_ready")
        cand_ready = sem("cand_ready")
        up_ready = sem("up_ready")
        gelu_ready = sem("gelu_ready")
        down_done = sem("down_done")
        acc_done = sem("acc_done")
        dve_step = sem("dve_step")
        silu_th = sem("silu_th")
        acc_final = sem("acc_final")
        y_ready = sem("y_ready")
        y_scaled = sem("y_scaled")
        y_used = sem("y_used")
        x1_ready = sem("x1_ready")
        stored = sem("stored")
        attn_loaded = sem("attn_loaded")
        experts_loaded = sem("experts_loaded")
        probs1_mm = sem("probs1_mm")
        probs1_ready = sem("probs1_ready")
        shared_mm = sem("shared_mm")
        shared_ready = sem("shared_ready")
        combine_ready = sem("combine_ready")
        xb_ready = sem("xb_ready")
        q_mm = sem("q_mm")
        qk_ready = sem("qk_ready")
        v_mm = sem("v_mm")
        v_ready = sem("v_ready")
        scores_done = sem("scores_done")
        max_ready = sem("max_ready")
        exp_done = sem("exp_done")
        tr_done = sem("tr_done")
        pt_copied = sem("pt_copied")
        pv_done = sem("pv_done")
        normed = sem("normed")
        ctxt_done = sem("ctxt_done")
        ctxT_ready = sem("ctxT_ready")
        out_done = sem("out_done")
        o_evicted = sem("o_evicted")
        up1_done = sem("up1_done")
        silu1_done = sem("silu1_done")
        mul1_done = sem("mul1_done")
        tr1_done = sem("tr1_done")
        h1T_ready = sem("h1T_ready")
        down1_done = sem("down1_done")
        xb1_ready = sem("xb1_ready")
        y1_silu = sem("y1_silu")
        y1_done = sem("y1_done")
        ready1 = sem("ready1")
        recip_done = sem("recip_done")
        gs_done = sem("gs_done")

        block = ctx.enter_context(nc.Block())

        @block.sync
        def _(sp):
            xd = x.rearrange("(n p) d -> p n d", p=P)
            for c in range(4):
                sp.dma_start(x_tok[:, 8 * c:8 * c + 8, :], xd[:, 8 * c:8 * c + 8, :]).then_inc(x_loaded[c], 16)
            for e in range(E0 + 1):
                if e >= 2:
                    sp.wait_ge(down_done, 32 * (e - 1) + 2)
                sp.dma_start(w1_sb[:, e % 2, :], w1[e % E0]).then_inc(w1_loaded[e % 2], 16)
                if e < E0:
                    sp.dma_start(w2_sb[:, e % 2, :, :], w2[e].rearrange("(c p) d -> p c d", p=P)) \
                        .then_inc(w2_loaded[e % 2], 16)
            sp.wait_ge(x1_ready, NG)
            sp.dma_start(rT, router).then_inc(attn_loaded, 16)
            sp.dma_start(rrow, router_row).then_inc(attn_loaded, 16)
            sp.dma_start(sg_w[:, :], shared_gate).then_inc(attn_loaded, 16)
            sp.dma_start(sd_w[:, :], shared_down).then_inc(attn_loaded, 16)
            sp.dma_start(aw[:, :, :], attn_w.rearrange("p (k n) -> p k n", k=4)).then_inc(attn_loaded, 16)
            sp.dma_start(acols[:, :, :], attn_cols.rearrange("p (k n) -> p k n", k=2)).then_inc(attn_loaded, 16)
            sp.dma_start(arows[:, :], attn_rows.partition_broadcast(P)).then_inc(attn_loaded, 16)
            sp.dma_start(gate1[:, :], w_gate).then_inc(experts_loaded, 16)
            sp.dma_start(down1[:, :, :], w_down.rearrange("p (k n) -> p k n", n=P)).then_inc(experts_loaded, 16)
            outd = out.rearrange("(n p) d -> p n d", p=P)
            for c in range(4):
                sp.wait_ge(y1_done, 8 * c + 10)
                sp.dma_start(outd[:, 8 * c:8 * c + 8, :], x_tok[:, 8 * c:8 * c + 8, :]).then_inc(stored, 16)
            sp.wait_ge(stored, 64)

        @block.gpsimd
        def _(pool):
            nc.gpsimd.memset(b1_sb[:, E0 * FC:], 0.0).then_inc(bhn_ready, 1)
            nc.gpsimd.memset(gin[:, 3, :, :], 0.0).then_inc(bhn_ready, 1)
            pool.wait_ge(bhn_ready, 2)
            pool.wait_ge(consts_loaded, 16 * 7)
            nc.gpsimd.tensor_scalar(gin[:, 3, :, :], gin[:, 3, :, :], cols_sb[:, 5:6], None, ALU.add) \
                .then_inc(bhn_ready, 1)
            for b in range(2):
                pool.wait_ge(xnT_ready, 2 * NG)
                if b:
                    pool.wait_ge(v_mm, PAIRS)
                nc.gpsimd.tensor_copy(xb[:, 0, :], xnT[:, T * b:T * b + T]).then_inc(xb_ready, 1)
            with pool.Fori(2, B + 1) as b:
                pool.wait_ge(v_mm, b * PAIRS)
                nc.gpsimd.tensor_copy(xb[:, 0, :], xnT[:, bass.ds((b % B) * T, T)]).then_inc(xb_ready, 1)
            pool.wait_ge(v_mm, B * PAIRS + 1)
            for n in range(2):
                nc.gpsimd.tensor_copy(xb[:, n, 0:P], xnT[:, P * n:P * n + P]).then_inc(xb1_ready, 1)
                nc.gpsimd.tensor_copy(xb[0:F1, n, P:2 * P], hsT[0:F1, P * n:P * n + P]).then_inc(xb1_ready, 1)
            with pool.Fori(1, NT // 2) as m:
                for half in range(2):
                    n = m * 2 + half
                    pool.wait_ge(up1_done, (n - 1) * NEG)
                    nc.gpsimd.tensor_copy(xb[:, half, 0:P], xnT[:, bass.ds(n * P, P)]).then_inc(xb1_ready, 1)
                    nc.gpsimd.tensor_copy(xb[0:F1, half, P:2 * P], hsT[0:F1, bass.ds(n * P, P)]).then_inc(xb1_ready, 1)

        @block.scalar
        def _(act):
            act.dma_start(misc[:, :], misc_w).then_inc(consts_loaded, 16)
            act.dma_start(ginw[:, :], gin_w).then_inc(consts_loaded, 16)
            act.dma_start(halfw[:, :], half_w).then_inc(consts_loaded, 16)
            act.dma_start(cols_sb[:, :], cols).then_inc(consts_loaded, 16)
            act.dma_start(rows_sb[:, :], rows).then_inc(consts_loaded, 16)
            act.dma_start(b2blk[:, :], b2_blocks).then_inc(consts_loaded, 16)
            act.dma_start(b1_sb[:, 0:E0 * FC], b1).then_inc(consts_loaded, 16)

            def layer_norm(layer, scratch):
                for c in range(4):
                    act.wait_ge(centred, 4 * layer + c + 1)
                    nc.scalar.activation(scratch[:, 1024 * c:1024 * c + 1024],
                                         xn_tok[:, 8 * c:8 * c + 8, :].rearrange("p n d -> p (n d)"),
                                         ACT.Square).then_inc(squared, 1)
                act.wait_ge(var_ready, layer + 1)
                nc.scalar.activation(ln_std[:, :], ln_sq[:, :], ACT.Sqrt, bias=eps_col[:, :], scale=1.0 / P) \
                    .then_inc(std_ready, 1)

            layer_norm(0, scr2)
            for g in range(NG):
                act.wait_ge(turned, g + 1)
                nc.scalar.copy(xnT[:, 512 * g:512 * g + 512], ps_t[g % 2][:, :]).then_inc(xnT_ready, 1)
                if g == 0:
                    act.wait_ge(biases_ready, 1)
                for k in range(2):
                    act.wait_ge(gin_mm, 4 * g + k + 1)
                    nc.scalar.activation(gin[:, k, 2 * g:2 * g + 2, :], ps_up[k][:, :].rearrange("p (b t) -> p b t", b=2),
                                         ACT.Identity, bias=gin_bias[:, k:k + 1]).then_inc(gin_act, 1)
            act.wait_ge(shifted, 1)
            nc.scalar.activation(scr[:, 0:256], scr[:, 0:256], ACT.Exp).then_inc(exps_ready, 1)
            nc.scalar.activation(gate[:, :, :], gate[:, :, :], ACT.Tanh, scale=0.5).then_inc(exps_ready, 1)
            for n in range(2):
                act.wait_ge(wT_mm, n + 1)
                nc.scalar.copy(h_sb[:, 0, 128 * n:128 * n + 128], ps_t[n][:, 0:128]).then_inc(wT_ready, 1)
            for g in range(NG):
                act.wait_ge(b2_mm, g + 1)
                nc.scalar.copy(xn_tok[:, 4 * g:4 * g + 4, :].rearrange("p n d -> p (n d)"), ps_t[g % 2][:, :]) \
                    .then_inc(b2_copied, 1)

            def gelu(c, j, b1_col):
                act.wait_ge(up_ready, c + 1)
                act.wait_ge(down_done, c + 1)
                nc.scalar.activation(h_sb[:, j % 2, :], ps_up[j % 2][:, :], ACT.Gelu,
                                     bias=b1_sb[:, bass.ds(b1_col, 1)]).then_inc(gelu_ready, 1)

            gelu(0, 0, 0)
            with act.Fori(0, NG * E0) as u:
                for j in range(4):
                    t = u * 4 + j
                    act.wait_ge(pre_ready, t + 1)
                    nc.scalar.activation(th[:, j % 2, :], ps_rec[j % 2][:, 0:48], ACT.Tanh, scale=0.5) \
                        .then_inc(th_ready, 1)
                    act.wait_ge(sumn_ready, t + 1)
                    nc.scalar.activation(cand[:, j % 2, :], sumn[:, j % 2, :], ACT.Tanh, scale=0.5) \
                        .then_inc(cand_ready, 1)
                    if j < 3:
                        gelu(t + 1, j + 1, (u // 8) * 4 + j + 1)
                    else:
                        gelu(t + 1, 0, ((u + 1) // 8) * 4)
            act.wait_ge(acc_final, 1)
            nc.scalar.activation(gin[:, 0, :, :].rearrange("p b t -> p (b t)"),
                                 xn_tok[:, :, :].rearrange("p n d -> p (n d)"), ACT.Tanh, scale=0.5) \
                .then_inc(silu_th, 1)
            for n in range(NT):
                act.wait_ge(y_ready, n + 1)
                nc.scalar.mul(gin[:, 1, n // 2, 128 * (n % 2):128 * (n % 2) + 128], ps_up[n % 2][:, 0:128],
                              gate[:, n, 0:1]).then_inc(y_scaled, 1)

            layer_norm(1, hsT)
            for g in range(NG):
                act.wait_ge(turned, NG + g + 1)
                nc.scalar.copy(xnT[:, 512 * g:512 * g + 512], ps_t[g % 2][:, :]).then_inc(xnT_ready, 1)
            act.wait_ge(attn_loaded, 16 * 7)
            nc.scalar.mul(acols[:, 0, :], acols[:, 0, :], HD ** -0.5)
            for n in range(NT):
                act.wait_ge(probs1_mm, n + 1)
                nc.scalar.activation(comb[:, n, :], ps_rec[n % 2][:, 0:E1], ACT.Sigmoid).then_inc(probs1_ready, 1)
            for g in range(NG):
                act.wait_ge(shared_mm, g + 1)
                nc.scalar.activation(hsT[0:F1, 512 * g:512 * g + 512], ps_y[0:F1, g % 2, :], ACT.Silu) \
                    .then_inc(shared_ready, 1)

            def qk_out(p, j):
                act.wait_ge(q_mm, p + 1)
                if not (isinstance(p, int) and p < 2):
                    act.wait_ge(scores_done, p * 2 - 2)
                nc.scalar.activation(qT[:, j % 2, :], ps_qk[:, 0:T], ACT.Identity, bias=acols[:, 0, j:j + 1],
                                     scale=HD ** -0.5)
                nc.scalar.activation(kT[:, j % 2, :], ps_qk[:, T:2 * T], ACT.Identity, bias=acols[:, 1, j:j + 1]) \
                    .then_inc(qk_ready, 1)

            def ctx_out(p):
                act.wait_ge(ctxt_done, p + 1)
                if not (isinstance(p, int) and p < 1):
                    act.wait_ge(out_done, p)
                nc.scalar.copy(ctxT[:, :], ps_v[:, T:2 * T]).then_inc(ctxT_ready, 1)

            def attend(b, first):
                for j in range(PAIRS):
                    p = b * PAIRS + j
                    for a in range(2):
                        h = p * 2 + a
                        act.wait_ge(max_ready, h + 1)
                        if not (first and j == 0):
                            act.wait_ge(tr_done, h - 1)
                        for i in range(2):
                            nc.scalar.activation(probs[:, a, i, :], ps_s[a][:, T * i:T * i + T], ACT.Exp,
                                                 bias=negmax[:, a, i:i + 1],
                                                 accum_out=sums[:, j % 4, i, a:a + 1]).then_inc(exp_done, 1)
                        if a == 0:
                            if not (first and j < 2):
                                ctx_out(p - 2)
                            qk_out(p + 1, (j + 1) % PAIRS)

            qk_out(0, 0)
            attend(0, True)
            with act.Fori(1, B) as b:
                attend(b, False)
            for p in (B * PAIRS - 2, B * PAIRS - 1):
                ctx_out(p)

            act.wait_ge(shared_ready, NG)
            act.sem_inc(silu1_done, 2)
            act.sem_inc(y1_silu, 1)

            def silu(q, k):
                act.wait_ge(up1_done, q + 1)
                act.wait_ge(tr1_done, q + 1)
                nc.scalar.activation(h1[:, k, :], ps_up[k][:, :], ACT.Silu).then_inc(silu1_done, 1)

            def tile_silu(n, bank_):
                act.wait_ge(down1_done, n * NEG + 3)
                act.wait_ge(y1_done, n + 1)
                nc.scalar.activation(g1, ps_t[bank_][:, 0:P], ACT.Silu).then_inc(y1_silu, 1)

            with act.Fori(0, NT // 2) as m:
                for half in range(2):
                    n = m * 2 + half
                    for k in range(2):
                        silu(n * NEG + k, k)
                    tile_silu(n, 1 - half)
                    with act.Fori(1, NEG // 2) as g2:
                        for k in range(2):
                            silu(n * NEG + g2 * 2 + k, k)
            tile_silu(NT, 1)

        @block.tensor
        def _(pe):
            pe.wait_ge(consts_loaded, 16 * 7)

            def turn(g, layer=0):
                pe.wait_ge(xn_ready, 4 * layer + g // 2 + 1)
                if g >= 2:
                    pe.wait_ge(xnT_ready, NG * layer + g - 1)
                for s in range(4):
                    last = nc.tensor.transpose(ps_t[g % 2][:, 128 * s:128 * s + 128], xn_tok[:, 4 * g + s, :], ident)
                last.then_inc(turned, 1)

            turn(0)
            for g in range(NG):
                if g + 1 < NG:
                    turn(g + 1)
                pe.wait_ge(xnT_ready, g + 1)
                for k, dst in enumerate((ps_up[0][:, :], ps_up[1][:, :], ps_y[:, 0, :], ps_y[:, 1, :])):
                    if g:
                        pe.wait_ge(gin_act if k < 2 else gin_dve, 2 * (g - 1) + k % 2 + 1)
                    nc.tensor.matmul(dst, ginw[:, 128 * k:128 * k + 128], xnT[:, 512 * g:512 * g + 512],
                                     start=True, stop=True).then_inc(gin_mm, 1)
                for s in range(4):
                    n = 4 * g + s
                    nc.tensor.matmul(ps_rec[0][:, 10 * n:10 * n + 10], xnT[:, 128 * n:128 * n + 128], rgT,
                                     start=True, stop=False)
                    last = nc.tensor.matmul(ps_rec[0][:, 10 * n:10 * n + 10], ones[0:1, :], rows_sb[0:1, 384:394],
                                            start=False, stop=True)
            last.then_inc(logits_ready, 1)
            pe.wait_ge(onehot_ready, 1)
            nc.tensor.matmul(ps_rec[1][:, :], upper, scr[:, 1024:1536], start=True, stop=True).then_inc(ranks_ready, 1)
            nc.tensor.matmul(ps_rec[0][:, :], ones, scr[:, 1024:1536], start=True, stop=True).then_inc(ranks_ready, 1)
            pe.wait_ge(w_ready, 1)
            for n in range(2):
                nc.tensor.transpose(ps_t[n][:, 0:128], w_te[:, 16 * n:16 * n + 16, :].rearrange("p n e -> p (n e)"),
                                    ident).then_inc(wT_mm, 1)
            for g in range(NG):
                pe.wait_ge(wT_ready, 2 if g < 2 else 2)
                if g >= 2:
                    pe.wait_ge(b2_copied, g - 1)
                nc.tensor.matmul(ps_t[g % 2][:, :], h_sb[:, 0, 128 * (g // 4):128 * (g // 4) + 128],
                                 b2blk[:, 512 * (g % 4):512 * (g % 4) + 512], start=True, stop=True) \
                    .then_inc(b2_mm, 1)

            def rec_input(t, par):
                nc.tensor.matmul(ps_rec[par][:, 0:64], ident, gin[:, 0:4, :, t], start=True, stop=False,
                                 skip_group_check=True)

            def up(c, par, wbuf, f, tile, first=False):
                if not first:
                    pe.wait_ge(gelu_ready, c)
                nc.tensor.matmul(ps_up[par][:, :], w1_sb[:, wbuf, 128 * f:128 * f + 128],
                                 xnT[:, bass.ds(tile * 512, 512)], start=True, stop=True).then_inc(up_ready, 1)

            def unit(ep, u, wbuf, tile, next_tile, next_wbuf):
                for j in range(4):
                    t = u * 4 + j
                    par = j % 2
                    pe.wait_ge(rnn_ready, t + 1)
                    pe.wait_ge(ssm_ready, t + 1)
                    nc.tensor.matmul(ps_rec[par][:, 48:64], whn, hist_g[:, :, t], start=False, stop=False,
                                     skip_group_check=True)
                    nc.tensor.matmul(ps_rec[par][:, 0:16], whr, hist_g[:, :, t], start=False, stop=False,
                                     skip_group_check=True)
                    nc.tensor.matmul(ps_rec[par][:, 16:32], whz, hist_g[:, :, t], start=False, stop=False,
                                     skip_group_check=True)
                    nc.tensor.matmul(ps_rec[par][:, 32:48], aT, hist_s[:, :, t], start=False, stop=True,
                                     skip_group_check=True).then_inc(pre_ready, 1)
                    if j < 3:
                        up(t + 1, 1 - par, wbuf, j + 1, tile)
                    else:
                        up(t + 1, 1 - par, next_wbuf, 0, next_tile)
                    rec_input((t + 1) % T, 1 - par)
                    if j == 0:
                        pe.wait_ge(acc_done, u * 4 + 4)
                        pe.wait_ge(w2_loaded[wbuf], 16 * (ep + 1))
                    pe.wait_ge(gelu_ready, t + 2)
                    for s in range(4):
                        last = nc.tensor.matmul(ps_y[:, tile % 2, 128 * s:128 * s + 128],
                                                h_sb[:, par, 128 * s:128 * s + 128], w2_sb[:, wbuf, j, :],
                                                start=(j == 0 and s == 0), stop=(j == 3), skip_group_check=True)
                    last.then_inc(down_done, 1)

            pe.sem_inc(down_done, 2)
            pe.sem_inc(gelu_ready, 1)
            pe.wait_ge(bhn_ready, 3)
            pe.wait_ge(gin_act, 2 * NG)
            pe.wait_ge(gin_dve, 2 * NG)
            pe.wait_ge(w1_loaded[0], 16)
            pe.wait_ge(b2_copied, NG)
            up(0, 0, 0, 0, 0, first=True)
            pe.wait_ge(rnn_ready, 1)
            rec_input(0, 0)
            with pe.Fori(0, E0 // 2) as ep:
                for half in range(2):
                    with pe.Fori(0, NG - 1) as tile:
                        unit(ep, (ep * 2 + half) * 8 + tile, half, tile, tile + 1, half)
                    pe.wait_ge(w1_loaded[1 - half], 16 * (ep + 1 + half))
                    unit(ep, (ep * 2 + half) * 8 + 7, half, 7, 0, 1 - half)
            pe.wait_ge(rnn_ready, T + 1)
            pe.wait_ge(ssm_ready, T + 1)
            pe.wait_ge(gelu_ready, 4 * NG * E0 + 2)
            for n in range(NT):
                b, h = n // 2, n % 2
                if n >= 2:
                    pe.wait_ge(y_scaled, n - 1)
                    pe.wait_ge(y_used, n - 1)
                nc.tensor.matmul(ps_up[n % 2][:, 0:128], hist_s[:, b, 1 + 128 * h:129 + 128 * h], cwT,
                                 start=True, stop=False)
                nc.tensor.matmul(ps_up[n % 2][:, 0:128], xnT[:, 128 * n:128 * n + 128], dwT, start=False, stop=False)
                for k in range(2):
                    nc.tensor.matmul(ps_up[n % 2][:, 0:128], ones[0:1, :], rows_sb[0:1, 128 * k:128 * k + 128],
                                     start=False, stop=k == 1)
                nc.tensor.matmul(ps_t[n % 2][:, 0:128], hist_g[:, b, 1 + 128 * h:129 + 128 * h], projT,
                                 start=True, stop=False)
                nc.tensor.matmul(ps_t[n % 2][:, 0:128], ones[0:1, :], rows_sb[0:1, 256:384],
                                 start=False, stop=True).then_inc(y_ready, 1)

            for g in range(NG):
                turn(g, 1)
            pe.wait_ge(attn_loaded, 16 * 7)
            for n in range(NT):
                pe.wait_ge(xnT_ready, NG + n // 4 + 1)
                if n >= 2:
                    pe.wait_ge(probs1_ready, n - 1)
                nc.tensor.matmul(ps_rec[n % 2][:, 0:E1], xnT[:, P * n:P * n + P], rT, start=True, stop=False)
                nc.tensor.matmul(ps_rec[n % 2][:, 0:E1], ones[0:1, :], rrow, start=False, stop=True) \
                    .then_inc(probs1_mm, 1)
            for g in range(NG):
                if g >= 2:
                    pe.wait_ge(shared_ready, g - 1)
                nc.tensor.matmul(ps_y[0:F1, g % 2, :], sg_w[:, :], xnT[:, 512 * g:512 * g + 512],
                                 start=True, stop=True).then_inc(shared_mm, 1)
            pe.wait_ge(shared_ready, NG)
            pe.wait_ge(probs1_ready, NT)

            def qk_mm(b, j, p):
                if not (isinstance(p, int) and p == 0):
                    pe.wait_ge(qk_ready, p)
                src = xnT[:, bass.ds(b * T, T)]
                nc.tensor.matmul(ps_qk[:, 0:T], aw[:, 0, P * j:P * j + P], src, start=True, stop=True)
                nc.tensor.matmul(ps_qk[:, T:2 * T], aw[:, 1, P * j:P * j + P], src, start=True, stop=True) \
                    .then_inc(q_mm, 1)

            def v_mm_(b, j, p, ctx_before):
                pe.wait_ge(xb_ready, b + 1)
                if not (isinstance(p, int) and p == 0):
                    pe.wait_ge(v_ready, p)
                if ctx_before:
                    pe.wait_ge(ctxT_ready, p - 2)
                for i in range(2):
                    last = nc.tensor.matmul(ps_v[:, P * i:P * i + P], xb[:, 0, P * i:P * i + P],
                                            aw[:, 2, P * j:P * j + P], start=True, stop=True)
                last.then_inc(v_mm, 1)

            def turn_probs(h, a, waits):
                pe.wait_ge(exp_done, h * 2 + 2)
                if waits:
                    pe.wait_ge(pt_copied, h - 1)
                for kc in range(2):
                    for i in range(2):
                        last = nc.tensor.transpose(ps_y[:, a, T * kc + P * i:T * kc + P * i + P],
                                                   probs[:, a, i, P * kc:P * kc + P], ident)
                last.then_inc(tr_done, 1)

            def values(h, p, j, a, waits):
                pe.wait_ge(pt_copied, h + 1)
                pe.wait_ge(v_ready, p + 1)
                if a == 0 and waits:
                    pe.wait_ge(normed, p)
                for i in range(2):
                    for kc in range(2):
                        last = nc.tensor.matmul(ps_ctx[:, P * i + HD * a:P * i + HD * a + HD],
                                                probsT[:, a, kc, P * i:P * i + P],
                                                v_sb[:, j % 2, kc, HD * a:HD * a + HD],
                                                start=(kc == 0), stop=(kc == 1))
                last.then_inc(pv_done, 1)

            def turn_ctx(p, last_v):
                pe.wait_ge(normed, p + 1)
                pe.wait_ge(v_ready, last_v)
                for i in range(2):
                    last = nc.tensor.transpose(ps_v[:, T + P * i:T + P * i + P], ctx_sb[:, i, :], ident)
                last.then_inc(ctxt_done, 1)

            def project(p, j, b_out):
                pe.wait_ge(ctxT_ready, p + 1)
                if j == 0 and b_out is not None:
                    pe.wait_ge(o_evicted, b_out)
                for i in range(2):
                    last = nc.tensor.matmul(ps_o[:, P * i:P * i + P], ctxT[:, P * i:P * i + P],
                                            aw[:, 3, P * j:P * j + P], start=(j == 0 and i == 0), stop=(j == PAIRS - 1),
                                            skip_group_check=True)
                last.then_inc(out_done, 1)

            def attend(b, first):
                for j in range(PAIRS):
                    p = b * PAIRS + j
                    for a in range(2):
                        h = p * 2 + a
                        early = first and j == 0
                        pe.wait_ge(qk_ready, p + 1)
                        if not early:
                            pe.wait_ge(exp_done, h * 2 - 2)
                        for i in range(2):
                            last = nc.tensor.matmul(ps_s[a][:, T * i:T * i + T],
                                                    qT[HD * a:HD * a + HD, j % 2, P * i:P * i + P],
                                                    kT[HD * a:HD * a + HD, j % 2, :], start=True, stop=True)
                        last.then_inc(scores_done, 1)
                        if not (early and a == 0):
                            turn_probs(h - 1, 1 - a, not (first and 2 * j + a - 1 < 2))
                        if not early:
                            values(h - 2, p - 1, (j - 1) % PAIRS, a, not (first and j == 1))
                        if a == 0:
                            if not (first and j < 2):
                                turn_ctx(p - 2, p + 1)
                            if j + 1 < PAIRS:
                                qk_mm(b, j + 1, p + 1)
                            else:
                                qk_mm((b + 1) % B, 0, p + 1)
                        else:
                            v_mm_(b + (j + 1) // PAIRS, (j + 1) % PAIRS, p + 1, not (first and j < 2))
                            if not (first and j < 2):
                                jo = (j - 2) % PAIRS
                                project(p - 2, jo, None if first else b)

            qk_mm(0, 0, 0)
            v_mm_(0, 0, 0, False)
            attend(0, True)
            with pe.Fori(1, B) as b:
                attend(b, False)
            p = B * PAIRS
            turn_probs(2 * p - 1, 1, True)
            values(2 * p - 2, p - 1, PAIRS - 1, 0, True)
            values(2 * p - 1, p - 1, PAIRS - 1, 1, True)
            for q in (p - 2, p - 1):
                turn_ctx(q, p + 1)
                project(q, q % PAIRS, None)

            pe.wait_ge(experts_loaded, 32)
            pe.wait_ge(ready1, 1)
            pe.wait_ge(o_evicted, B)
            pe.sem_inc(tr1_done, 1)
            pe.sem_inc(down1_done, 1)
            nc.tensor.matmul(ps_t[1][:, 0:P], h1T[:, 0, 0:P], down1[:, 0, :], start=True, stop=False,
                             skip_group_check=True)

            def up1(q, g, k, half):
                pe.wait_ge(silu1_done, q + 1)
                nc.tensor.matmul(ps_up[k][:, :], xb[:, half, 0:P], gate1[:, bass.ds(g * 512, 512)],
                                 start=True, stop=True).then_inc(up1_done, 1)

            def turn1(q, k):
                pe.wait_ge(mul1_done, q + 1)
                pe.wait_ge(h1T_ready, q + 1)
                for i in range(4):
                    last = nc.tensor.transpose(ps_y[:, 1 - k, P * i:P * i + P], h1[:, 1 - k, P * i:P * i + P], ident)
                last.then_inc(tr1_done, 1)

            def down1_(q, g, k, bank_, last_one):
                pe.wait_ge(h1T_ready, q + 2)
                for i in range(4):
                    last = nc.tensor.matmul(ps_t[bank_][:, 0:P], h1T[:, k, P * i:P * i + P],
                                            down1[:, g * 4 + i, :], start=False, stop=last_one and i == 3,
                                            skip_group_check=True)
                last.then_inc(down1_done, 1)

            with pe.Fori(0, NT // 2) as m:
                for half in range(2):
                    n = m * 2 + half
                    for k in range(2):
                        q = n * NEG + k
                        if k == 0:
                            pe.wait_ge(xb1_ready, n * 2 + 2)
                        up1(q, k, k, half)
                        turn1(q, k)
                        down1_(q, NEG - 2 + k, k, 1 - half, k == 1)
                    pe.wait_ge(y1_silu, n + 1)
                    nc.tensor.matmul(ps_t[half][:, 0:P], xb[0:F1, half, P:2 * P], sd_w[:, :], start=True, stop=False,
                                     skip_group_check=True)
                    with pe.Fori(1, NEG // 2) as g2:
                        for k in range(2):
                            q = n * NEG + g2 * 2 + k
                            up1(q, g2 * 2 + k, k, half)
                            turn1(q, k)
                            down1_(q, (g2 - 1) * 2 + k, k, half, False)
            turn1(NT * NEG, 0)
            for k in range(2):
                down1_(NT * NEG + k, NEG - 2 + k, k, 1, k == 1)

        @block.vector
        def _(dve):
            steps = Count(dve_done)

            def chain(ins):
                dve.wait_ge(dve_done, steps.raised_by(ins))

            def across(col, shape):
                return col.unsqueeze(len(shape) - 1).to_broadcast(shape)

            V = nc.vector
            chain(V.memset(eps_col[:, :], EPS))

            def layer_norm(layer, scratch):
                for c in range(4):
                    s = slice(8 * c, 8 * c + 8)
                    if layer == 0:
                        dve.wait_ge(x_loaded[c], 16)
                    chain(V.tensor_reduce(ln_sum[:, s], x_tok[:, s, :], AX_X, ALU.add))
                    chain(V.tensor_scalar(ln_mean[:, s], ln_sum[:, s], 1.0 / P, None, ALU.mult))
                    V.tensor_tensor(xn_tok[:, s, :], x_tok[:, s, :], across(ln_mean[:, s], [P, 8, P]), ALU.subtract) \
                        .then_inc(centred, 1)
                for c in range(4):
                    s = slice(8 * c, 8 * c + 8)
                    dve.wait_ge(squared, 4 * layer + c + 1)
                    red = V.tensor_reduce(ln_sq[:, s],
                                          scratch[:, 1024 * c:1024 * c + 1024].rearrange("p (n d) -> p n d", d=P),
                                          AX_X, ALU.add)
                red.then_inc(var_ready, 1)
                dve.wait_ge(std_ready, layer + 1)
                chain(V.reciprocal(ln_rstd[:, :], ln_std[:, :]))
                for c in range(4):
                    s = slice(8 * c, 8 * c + 8)
                    V.tensor_tensor(xn_tok[:, s, :], xn_tok[:, s, :], across(ln_rstd[:, s], [P, 8, P]), ALU.mult) \
                        .then_inc(xn_ready, 1)

            layer_norm(0, scr2)
            dve.wait_ge(consts_loaded, 16 * 7)
            chain(V.tensor_scalar(halfw[:, :], halfw[:, :], 0.5, None, ALU.mult))
            chain(V.tensor_tensor(gin_bias[:, 0:2], cols_sb[:, 0:2], cols_sb[:, 3:5], ALU.add))
            chain(V.tensor_copy(gin_bias[:, 2:3], cols_sb[:, 6:7]))
            V.tensor_copy(gin_bias[:, 3:4], cols_sb[:, 2:3]).then_inc(biases_ready, 1)
            dve.wait_ge(biases_ready, 1)
            for g in range(NG):
                dve.wait_ge(gin_mm, 4 * g + 3)
                V.tensor_scalar(gin[:, 2, 2 * g:2 * g + 2, :], ps_y[:, 0, :].rearrange("p (b t) -> p b t", b=2),
                                gin_bias[:, 2:3], None, ALU.add).then_inc(gin_dve, 1)
                dve.wait_ge(gin_mm, 4 * g + 4)
                V.tensor_scalar(gin[:, 4, 2 * g:2 * g + 2, :], ps_y[:, 1, :].rearrange("p (b t) -> p b t", b=2),
                                gin_bias[:, 3:4], 2.0, ALU.add, ALU.mult).then_inc(gin_dve, 1)

            def s3(a, k):
                return scr[:, a:a + NT * k].rearrange("p (n e) -> p n e", e=k)

            lg, eq = s3(0, 8), s3(256, 8)
            oh = s3(1024, 16)
            col = [scr[:, 2560 + NT * k:2560 + NT * k + NT] for k in range(8)]
            wide = [P, NT, 8]
            dve.wait_ge(logits_ready, 1)
            psl = ps_rec[0][:, 0:320].rearrange("p (n e) -> p n e", e=10)
            chain(V.tensor_copy(gate[:, :, :], psl[:, :, 8:10]))
            chain(V.tensor_reduce(col[0], psl[:, :, 0:8], AX_X, ALU.max))
            V.tensor_tensor(lg, psl[:, :, 0:8], across(col[0], wide), ALU.subtract).then_inc(shifted, 1)
            dve.wait_ge(exps_ready, 2)
            chain(V.tensor_scalar(gate[:, :, :], gate[:, :, :], 1.0, 0.25, ALU.add, ALU.mult))
            chain(V.tensor_reduce(col[0], lg, AX_X, ALU.add))
            chain(V.reciprocal(col[1], col[0]))
            chain(V.tensor_tensor(lg, lg, across(col[1], wide), ALU.mult))
            for k in range(2):
                ohk = oh[:, :, 8 * k:8 * k + 8]
                chain(V.tensor_reduce(col[2 + k], lg, AX_X, ALU.max))
                chain(V.tensor_tensor(eq, lg, across(col[2 + k], wide), ALU.is_equal))
                chain(V.tensor_tensor(eq, eq, desc.unsqueeze(1).to_broadcast(wide), ALU.mult))
                chain(V.tensor_reduce(col[4], eq, AX_X, ALU.max))
                chain(V.tensor_tensor(ohk, eq, across(col[4], wide), ALU.is_equal))
                if k == 0:
                    chain(V.scalar_tensor_tensor(out=lg, in0=ohk, scalar=-4.0, in1=lg, op0=ALU.mult, op1=ALU.add))
            V.tensor_tensor(col[5], col[2], col[3], ALU.add).then_inc(onehot_ready, 1)
            dve.wait_ge(onehot_ready, 1)
            chain(V.reciprocal(col[6], col[5]))
            for k in range(2):
                chain(V.tensor_tensor(col[2 + k], col[2 + k], col[6], ALU.mult))
            dve.wait_ge(ranks_ready, 2)
            a, b_ = scr[:, 3072:3584], scr[:, 3584:4096]
            chain(V.tensor_copy(a, ps_rec[0][:, :]))
            for k in (16, 32, 64, 128, 256):
                chain(V.tensor_copy(b_[:, 0:k], a[:, 0:k]))
                chain(V.tensor_tensor(b_[:, k:512], a[:, k:512], a[:, 0:512 - k], ALU.add))
                a, b_ = b_, a
            chain(V.tensor_tensor(a, a, ps_rec[0][:, :], ALU.subtract))
            chain(V.tensor_tensor(a, a, ps_rec[1][:, :], ALU.add))
            chain(V.scalar_tensor_tensor(out=b_, in0=a, scalar=float(CAP0), in1=scr[:, 1024:1536],
                                         op0=ALU.is_le, op1=ALU.mult))
            b3 = b_.rearrange("p (n e) -> p n e", e=16)
            chain(V.tensor_tensor(lg, b3[:, :, 0:8], across(col[2], wide), ALU.mult))
            chain(V.tensor_tensor(eq, b3[:, :, 8:16], across(col[3], wide), ALU.mult))
            V.tensor_tensor(w_te[:, :, :], lg, eq, ALU.add).then_inc(w_ready, 1)
            dve.wait_ge(w_ready, 1)
            V.memset(hist_s[:, :, 0], 0.0).then_inc(ssm_ready, 1)
            V.memset(hist_g[:, :, 0], 0.0).then_inc(rnn_ready, 1)
            dve.sem_inc(acc_done, 8)
            dve.wait_ge(b2_copied, NG)

            def accumulate(n, w_col):
                V.scalar_tensor_tensor(out=xn_tok[:, n, :], in0=ps_y[:, w_col[2], 128 * w_col[3]:128 * w_col[3] + 128],
                                       scalar=w_te[:, n, bass.ds(w_col[1], 1)], in1=xn_tok[:, n, :],
                                       op0=ALU.mult, op1=ALU.add).then_inc(acc_done, 1)

            def step(u, j, first):
                t = u * 4 + j
                par = j % 2
                dve.wait_ge(th_ready, t + 1)
                V.scalar_tensor_tensor(out=mixn[:, :], in0=th[:, par, 0:16], scalar=1.0, in1=ps_rec[par][:, 48:64],
                                       op0=ALU.add, op1=ALU.mult).then_inc(dve_step, 1)
                dve.wait_ge(dve_step, t * 4 + 1)
                V.tensor_tensor(sumn[:, par, :], mixn[:, :], gin[:, 4, :, t], ALU.add).then_inc(sumn_ready, 1)
                V.scalar_tensor_tensor(out=hist_s[:, :, t + 1], in0=th[:, par, 32:48], scalar=1.0,
                                       in1=ps_rec[par][:, 32:48], op0=ALU.add, op1=ALU.mult).then_inc(ssm_ready, 1)
                V.scalar_tensor_tensor(out=zg[:, :], in0=th[:, par, 16:32], scalar=1.0, in1=hist_g[:, :, t],
                                       op0=ALU.add, op1=ALU.mult).then_inc(dve_step, 1)
                V.tensor_scalar(omz[:, :], th[:, par, 16:32], -1.0, 1.0, ALU.mult, ALU.add).then_inc(dve_step, 1)
                dve.wait_ge(cand_ready, t + 1)
                dve.wait_ge(dve_step, t * 4 + 3)
                V.tensor_tensor(newn[:, :], omz[:, :], cand[:, par, :], ALU.mult).then_inc(dve_step, 1)
                dve.wait_ge(dve_step, t * 4 + 4)
                V.scalar_tensor_tensor(out=hist_g[:, :, t + 1], in0=zg[:, :], scalar=0.5, in1=newn[:, :],
                                       op0=ALU.mult, op1=ALU.add).then_inc(rnn_ready, 1)
                dve.wait_ge(rnn_ready, t + 2)
                if not first:
                    v = u - 1
                    if j == 0:
                        dve.wait_ge(down_done, u * 4 + 2)
                    accumulate((v % 8) * 4 + j, (0, v // 8, v % 2, j))

            for j in range(4):
                step(0, j, True)
            with dve.Fori(1, NG * E0) as u:
                for j in range(4):
                    step(u, j, False)
            dve.wait_ge(down_done, 4 * NG * E0 + 2)
            last_u = NG * E0 - 1
            for j in range(4):
                accumulate(4 * (last_u % 8) + j, (0, last_u // 8, last_u % 2, j))
            dve.wait_ge(acc_done, 4 * NG * E0 + 8)
            dve.sem_inc(acc_final, 1)
            dve.wait_ge(silu_th, 1)
            sil = gin[:, 0, :, :].rearrange("p b t -> p (b t)")
            chain(V.scalar_tensor_tensor(out=sil, in0=sil, scalar=1.0, in1=xn_tok[:, :, :].rearrange("p n d -> p (n d)"),
                                         op0=ALU.add, op1=ALU.mult))
            for n in range(NT):
                y1 = gin[:, 1, n // 2, 128 * (n % 2):128 * (n % 2) + 128]
                dve.wait_ge(y_scaled, n + 1)
                V.scalar_tensor_tensor(out=gin[:, 2, n // 2, 128 * (n % 2):128 * (n % 2) + 128],
                                       in0=ps_t[n % 2][:, 0:128], scalar=gate[:, n, 1:2], in1=y1,
                                       op0=ALU.mult, op1=ALU.add).then_inc(y_used, 1)
            s_all = gin[:, 2, :, :].rearrange("p b t -> p (b t)")
            x_all = x_tok[:, :, :].rearrange("p n d -> p (n d)")
            for g in range(NG):
                q = slice(512 * g, 512 * g + 512)
                dve.wait_ge(y_used, 4 * g + 4)
                chain(V.tensor_tensor(sil[:, q], sil[:, q], s_all[:, q], ALU.mult))
                V.tensor_tensor(x_all[:, q], x_all[:, q], sil[:, q], ALU.add).then_inc(x1_ready, 1)

            dve.wait_ge(x1_ready, NG)
            layer_norm(1, hsT)
            for n in range(NT):
                dve.wait_ge(probs1_ready, n + 1)
                chain(V.max(top8[:, n, :], comb[:, n, :]))
                chain(V.match_replace(out=rest, in_to_replace=top8[:, n, :], in_values=comb[:, n, :],
                                      imm_value=0.0))
                chain(V.tensor_tensor(comb[:, n, :], comb[:, n, :], rest, ALU.subtract))
            chain(V.tensor_reduce(ln_sum[:, :], top8[:, :, :], AX_X, ALU.add))
            chain(V.tensor_scalar(ln_sum[:, :], ln_sum[:, :], 1e-9, None, ALU.add))
            chain(V.reciprocal(ln_mean[:, :], ln_sum[:, :]))
            chain(V.tensor_tensor(comb[:, :, :], comb[:, :, :], across(ln_mean[:, :], [P, NT, E1]), ALU.mult))
            chain(V.tensor_scalar(comb[:, :, :], comb[:, :, :], 2.5, None, ALU.mult))
            dve.wait_ge(attn_loaded, 16 * 7)

            def values_out(p, j, waits):
                dve.wait_ge(v_mm, p + 1)
                if waits:
                    dve.wait_ge(pv_done, p * 2 - 2)
                V.tensor_tensor(v_sb[:, j % 2, :, :], ps_v[:, 0:2 * P].rearrange("p (i d) -> p i d", i=2),
                                arows[:, P * j:P * j + P].unsqueeze(1).to_broadcast([P, 2, P]), ALU.add) \
                    .then_inc(v_ready, 1)

            def probs_out(h, a, waits):
                dve.wait_ge(tr_done, h + 1)
                if waits:
                    dve.wait_ge(pv_done, h - 1)
                V.tensor_copy(probsT[:, a, :, :].rearrange("p c t -> p (c t)"), ps_y[:, a, :]).then_inc(pt_copied, 1)

            def normalise(p, j, waits):
                dve.wait_ge(pv_done, p * 2 + 2)
                V.reciprocal(rsums[:, :, :], sums[:, j % 4, :, :]).then_inc(recip_done, 1)
                dve.wait_ge(recip_done, p + 1)
                if waits:
                    dve.wait_ge(ctxt_done, p)
                V.tensor_tensor(ctx_sb[:, :, :].rearrange("p i (a d) -> p (i a) d", a=2),
                                ps_ctx[:, 0:2 * P].rearrange("p (k d) -> p k d", k=4),
                                rsums[:, :, :].rearrange("p i a -> p (i a)").unsqueeze(2).to_broadcast([P, 4, HD]),
                                ALU.mult).then_inc(normed, 1)

            def output_out(b):
                dve.wait_ge(out_done, b * PAIRS + PAIRS)
                V.tensor_tensor(xn_tok[:, bass.ds(b * 2, 2), :], ps_o[:, 0:2 * P].rearrange("p (i d) -> p i d", i=2),
                                arows[:, HEADS * HD:].unsqueeze(1).to_broadcast([P, 2, P]), ALU.add) \
                    .then_inc(o_evicted, 1)

            def attend(b, first):
                for j in range(PAIRS):
                    p = b * PAIRS + j
                    for a in range(2):
                        h = p * 2 + a
                        if a == 0 and not (first and j < 2):
                            normalise(p - 2, (j - 2) % PAIRS, not (first and j == 2))
                        dve.wait_ge(scores_done, h + 1)
                        V.tensor_reduce(negmax[:, a, :], ps_s[a][:, :].rearrange("p (i t) -> p i t", i=2), AX_X,
                                        ALU.max, negate=True).then_inc(max_ready, 1)
                        if not (first and j == 0 and a == 0):
                            probs_out(h - 1, 1 - a, not (first and 2 * j + a - 1 < 2))
                        if a == 1:
                            values_out(p + 1, (j + 1) % PAIRS, not (first and j == 0))
                            if j == 1 and not first:
                                output_out(b - 1)

            values_out(0, 0, False)
            attend(0, True)
            with dve.Fori(1, B) as b:
                attend(b, False)
            p = B * PAIRS
            probs_out(2 * p - 1, 1, True)
            normalise(p - 2, (p - 2) % PAIRS, True)
            normalise(p - 1, (p - 1) % PAIRS, True)
            output_out(B - 1)

            chain(V.memset(h1[:, 1, :], 0.0))
            V.memset(h1T[:, 0, :], 0.0).then_inc(ready1, 1)
            dve.sem_inc(mul1_done, 1)
            dve.sem_inc(h1T_ready, 2)
            dve.sem_inc(y1_done, 1)
            comb_flat = comb[:, :, :].rearrange("p n e -> p (n e)")

            def turned_out(q, k):
                dve.wait_ge(tr1_done, q + 2)
                dve.wait_ge(down1_done, q + 1)
                V.tensor_copy(h1T[:, 1 - k, :], ps_y[:, 1 - k, :]).then_inc(h1T_ready, 1)

            def weigh(q, k):
                dve.wait_ge(silu1_done, q + 3)
                hk = h1[:, k, :].rearrange("p (e i) -> p e i", i=F1)
                V.tensor_tensor(hk, hk, comb_flat[:, bass.ds(q * EG, EG)].unsqueeze(2).to_broadcast([P, EG, F1]),
                                ALU.mult).then_inc(mul1_done, 1)

            def tile_out(n):
                i = (n + NT - 1) % NT
                dve.wait_ge(y1_silu, n + 2)
                V.tensor_tensor(gs, g1, xn_tok[:, i, :], ALU.mult).then_inc(gs_done, 1)
                dve.wait_ge(gs_done, n + 1)
                V.tensor_tensor(x_tok[:, i, :], x_tok[:, i, :], gs, ALU.add).then_inc(y1_done, 1)

            with dve.Fori(0, NT // 2) as m:
                for half in range(2):
                    n = m * 2 + half
                    for k in range(2):
                        turned_out(n * NEG + k, k)
                        weigh(n * NEG + k, k)
                    with dve.Fori(1, NEG // 2) as g2:
                        for k in range(2):
                            turned_out(n * NEG + g2 * 2 + k, k)
                            weigh(n * NEG + g2 * 2 + k, k)
                    tile_out(n)
            turned_out(NT * NEG, 0)
            tile_out(NT)


def kernel(**inputs):
    import concourse.bacc as _bacc
    from concourse.bass_utils import run_bass_kernel_spmd as _run

    I = {k: np.asarray(v) for k, v in inputs.items()}
    f = np.float32
    z64 = np.zeros((P, 64), f)

    def padT(w):
        m = np.zeros((P, P), w.dtype)
        m[:w.shape[1], :w.shape[0]] = w.T
        return m

    wih, whh = I["L0_attn_W_ih"], I["L0_attn_W_hh"]
    gin_w = np.concatenate([wih[0:128].T, wih[128:256].T, padT(I["L0_attn_Bw"]), wih[256:384].T], 1)
    half_w = np.concatenate([whh[0:128].T, whh[128:256].T, whh[256:384].T, padT(I["L0_attn_A"]),
                             padT(I["L0_attn_Cw"]), I["L0_attn_proj_w"].T], 1)
    desc = np.tile(np.arange(8, 0, -1, dtype=f)[None], (P, 1))
    misc = np.concatenate([np.eye(P, dtype=f), np.triu(np.ones((P, P), f)), np.ones((P, P), f),
                           I["L0_attn_Dw"].T, desc, I["L0_ffn_Wr"], I["L0_attn_gate_w"].T], 1)
    bb = np.zeros((P, 1), f)
    bb[:64, 0] = I["L0_attn_Bb"]
    cols = np.concatenate([I["L0_attn_b_ih"].reshape(3, P).T, I["L0_attn_b_hh"].reshape(3, P).T, bb,
                           np.zeros((P, 1), f)], 1)
    rows = np.concatenate([I["L0_attn_Cb"], I["L0_attn_Db"], I["L0_attn_proj_b"], np.zeros(8, f),
                           I["L0_attn_gate_b"]])[None]
    b2b = np.zeros((16, 8, 16, P), f)
    for n in range(16):
        b2b[n, :, n, :] = I["L0_ffn_b2"]
    arrays = {
        "x": I["L0_attn_x"].reshape(NTOK, P), "gin_w": gin_w, "half_w": half_w, "misc_w": misc, "cols": cols,
        "rows": rows, "b2_blocks": b2b.reshape(P, 16 * P), "w1": I["L0_ffn_W1"],
        "b1": I["L0_ffn_b1"].reshape(E0 * FC, P).T, "w2": I["L0_ffn_W2"],
        "attn_w": np.concatenate([I["L1_attn_wq"].T, I["L1_attn_wk"].T, I["L1_attn_wv"].T,
                                  I["L1_attn_wo"].T.reshape(PAIRS, P, P).transpose(1, 0, 2).reshape(P, -1)], 1),
        "attn_cols": np.concatenate([I["L1_attn_bq"].reshape(PAIRS, P).T, I["L1_attn_bk"].reshape(PAIRS, P).T], 1),
        "attn_rows": np.concatenate([I["L1_attn_bv"], I["L1_attn_bo"]]),
        "router": I["L1_ffn_router_w"].T, "router_row": I["L1_ffn_expert_bias"][None],
        "w_gate": I["L1_ffn_w_gate"].transpose(2, 0, 1).reshape(P, -1),
        "w_down": I["L1_ffn_w_down"].reshape(E1 // 2, 2, P, F1).transpose(1, 3, 0, 2).reshape(P, -1),
        "shared_gate": I["L1_ffn_w_gate_shared"].T, "shared_down": I["L1_ffn_w_down_shared"].T,
    }
    arrays = {k: np.ascontiguousarray(v) for k, v in arrays.items()}
    nc = _bacc.Bacc("TRN2", target_bir_lowering=False, num_devices=1)
    aps = {k: nc.dram_tensor(k, v.shape, mybir.dt.from_np(v.dtype), kind="ExternalInput").ap()
           for k, v in arrays.items()}
    out = nc.dram_tensor("out", (NTOK, P), F32, kind="ExternalOutput").ap()
    build(nc, out=out, **aps)
    r = _run(nc, [arrays], core_ids=[0])
    return r.results[0]["out"].reshape(B, T, P)
```

```python
from contextlib import ExitStack

import numpy as np

import concourse.bass as bass
from concourse import mybir

ALU = mybir.AluOpType
ACT = mybir.ActivationFunctionType
F32 = mybir.dt.float32
BF16 = mybir.dt.bfloat16
I32 = mybir.dt.int32
U8 = mybir.dt.uint8
AX_X = mybir.AxisListType.X

P = 128
B, T = 16, 256
NTOK = B * T
NT = NTOK // P
NG = NTOK // 512
E0, F0 = 8, 512
FC = F0 // P
CAP0 = int(NTOK * 1.25 / E0)
EPS = 1e-5
HEADS, HD = 16, 64
PAIRS = HEADS // 2
E1, TOPK1, F1 = 160, 8, 64
SLOT_TILES = -(-(NTOK * TOPK1 // P + E1) // 8) * 8
SLOTS = SLOT_TILES * P
NBODY = SLOT_TILES // 8
HB = B // 2


class Count:

    def __init__(self, sem):
        self.sem, self.n = sem, 0

    def raised_by(self, ins):
        self.n += 1
        ins.then_inc(self.sem, 1)
        return self.n


def build(nc, x, gin_w, half_w, misc_w, cols, rows, b2_blocks, w1, b1, w2,
          attn_w, attn_cols, attn_rows, router, router_row, w_gate, w_down, shared_gate, shared_down,
          jcols, sel_w, out):
    with ExitStack() as ctx:
        def sb(name, shape, dt=F32):
            return ctx.enter_context(nc.sbuf_tensor(name, shape, dt))

        def bank(name):
            return ctx.enter_context(nc.psum_tensor(name, [P, 512], F32))

        def sem(name):
            return ctx.enter_context(nc.semaphore(name))

        x_tok = sb("x_tok", [P, NT, P])
        xn_tok = sb("xn_tok", [P, NT, P])
        xnT = sb("xnT", [P, NTOK])
        ln_sum = sb("ln_sum", [P, NT])
        ln_mean = sb("ln_mean", [P, NT])
        ln_sq = sb("ln_sq", [P, NT])
        ln_std = sb("ln_std", [P, NT])
        ln_rstd = sb("ln_rstd", [P, NT])
        eps_col = sb("eps_col", [P, 1])
        misc = sb("misc", [P, 128 * 4 + 8 + 10])
        ident, upper, ones = misc[:, 0:128], misc[:, 128:256], misc[:, 256:384]
        dwT, desc, rgT = misc[:, 384:512], misc[:, 512:520], misc[:, 520:530]
        rows_sb = sb("rows_sb", [1, 3 * 128 + 10])
        layer0 = ExitStack()

        def sb(name, shape, dt=F32, stack=layer0):
            return stack.enter_context(nc.sbuf_tensor(name, shape, dt))

        ginw = sb("ginw", [P, 4 * 128])
        halfw = sb("halfw", [P, 6 * 128])
        whr, whz, whn, aT, cwT, projT = (halfw[:, 128 * k:128 * k + 128] for k in range(6))
        cols_sb = sb("cols_sb", [P, 8])
        gin_bias = sb("gin_bias", [P, 4])
        gin = sb("gin", [P, 5, B, T])
        hist_g = sb("hist_g", [P, B, T + 1])
        hist_s = sb("hist_s", [P, B, T + 1])
        b2blk = sb("b2blk", [P, 16 * P])
        zeros = sb("zeros", [P, 1024])
        w1_sb = sb("w1_sb", [P, 2, F0])
        w2_sb = sb("w2_sb", [P, 2, FC, P])
        b1_sb = sb("b1_sb", [P, (E0 + 1) * FC])
        h_sb = sb("h_sb", [P, 2, 512])
        w_te = sb("w_te", [P, NT, E0])
        gate = sb("gate", [P, NT, 2])
        th = sb("th", [P, 2, 48])
        cand = sb("cand", [P, 2, 16])
        mixn = sb("mixn", [P, 16])
        sumn = sb("sumn", [P, 2, 16])
        zg = sb("zg", [P, 16])
        omz = sb("omz", [P, 16])
        newn = sb("newn", [P, 16])
        scr = hist_g[:, :, :].rearrange("p b t -> p (b t)")
        scr2 = hist_s[:, :, :].rearrange("p b t -> p (b t)")
        layer0.close()

        def sb(name, shape, dt=F32):
            return ctx.enter_context(nc.sbuf_tensor(name, shape, dt))

        gate1 = sb("gate1", [P, E1 * F1])
        down_stack = ExitStack()
        down1 = down_stack.enter_context(nc.sbuf_tensor("down1", [P, E1 // 2, P], F32))
        down_stack.close()
        comb = sb("comb", [P, NT, E1])
        place = sb("place", [P, NT, E1])
        att = sb("att", [P, NT, P])
        chosen = att[:, :, :].rearrange("p n d -> p (n d)")[:, 0:NT * E1 // 2].bitcast(BF16) \
            .rearrange("p (n e) -> p n e", e=E1)
        att_flat = att[:, :, :].rearrange("p n d -> p (n d)")
        hsT = gate1[:, 0:NTOK]
        aw = sb("aw", [P, 4, HEADS * HD])
        acols = sb("acols", [P, 2, PAIRS])
        arows = sb("arows", [P, HEADS * HD + P])
        sg_w = sb("sg_w", [P, F1])
        sd_w = sb("sd_w", [F1, P])
        place8 = sb("place8", [P, NT, TOPK1])
        slot = sb("slot", [P, NT, TOPK1], I32)
        w8 = sb("w8", [P, NT, TOPK1])
        top8 = sb("top8", [P, NT, TOPK1])
        pair_row = sb("pair_row", [1, 4 * P], U8)
        parity = sb("parity", [P, 4 * P, 2], BF16)
        jcol = sb("jcol", [P, 4])
        tile_e = sb("tile_e", [P, 4])
        tile_par = sb("tile_par", [P, 4])
        tile_i = sb("tile_i", [P, 4], I32)
        tile_u8 = sb("tile_u8", [P, 4], U8)
        rows_g = sb("rows_g", [P, 16, P])
        small = rows_g[:, :, :].rearrange("p n d -> p (n d)")
        rT, cnt_f, cnt_inc = (small[:, E1 * k:E1 * k + E1] for k in range(3))
        cnt_i = small[:, 3 * E1:4 * E1].bitcast(I32)
        rrow, offs = (small[0:1, E1 * k:E1 * k + E1] for k in (4, 5))
        junk = small[:, 6 * E1:8 * E1].rearrange("p (k e) -> p k e", e=E1)
        par_row = small[:, 8 * E1:8 * E1 + 4 * P]
        bf = small[:, 8 * E1 + 4 * P:].bitcast(BF16)
        upper_b, ones_b, sel_b, tile_tot = bf[:, 0:P], bf[:, P:2 * P], bf[:, 2 * P:2 * P + 63], bf[0:NT, 320:320 + E1]
        attn_stack = ExitStack()

        def sb(name, shape, dt=F32, stack=attn_stack):
            return stack.enter_context(nc.sbuf_tensor(name, shape, dt))

        xb = sb("xb", [P, 2 * P])
        qT = sb("qT", [P, 2, T])
        kT = sb("kT", [P, 2, T])
        v_sb = sb("v_sb", [P, 2, 2, P])
        probs = sb("probs", [P, 2, 2, T])
        probsT = sb("probsT", [P, 2, 2, T])
        negmax = sb("negmax", [P, 2, 2])
        sums = sb("sums", [P, 4, 2, 2])
        rsums = sb("rsums", [P, 2, 2])
        ctx_sb = sb("ctx_sb", [P, 2, P])
        ctxT = sb("ctxT", [P, 2 * P])
        attn_stack.close()

        def sb(name, shape, dt=F32):
            return ctx.enter_context(nc.sbuf_tensor(name, shape, dt))

        slots_x = sb("slots_x", [P, 2, 512])
        slots_xT = sb("slots_xT", [P, 2, 512])
        hid = sb("hid", [P, 2, 512])
        hidT = sb("hidT", [P, 2, 512])
        slots_y = sb("slots_y", [P, 2, 512])

        ps_rec = [bank("ps_rec0"), bank("ps_rec1")]
        ps_up = [bank("ps_up0"), bank("ps_up1")]
        ps_y = ctx.enter_context(nc.psum_tensor("ps_y", [P, 2, 512], F32))
        ps_t = [bank("ps_t0"), bank("ps_t1")]
        ps_qk, ps_v, ps_s, ps_ctx, ps_o = ps_rec[0], ps_rec[1], ps_up, ps_t[0], ps_t[1]

        x_loaded = [sem(f"x_loaded{c}") for c in range(4)]
        consts_loaded = sem("consts_loaded")
        w1_loaded = [sem("w1_loaded0"), sem("w1_loaded1")]
        w2_loaded = [sem("w2_loaded0"), sem("w2_loaded1")]
        dve_done = sem("dve_done")
        act_done = sem("act_done")
        centred = sem("centred")
        squared = sem("squared")
        var_ready = sem("var_ready")
        std_ready = sem("std_ready")
        xn_ready = sem("xn_ready")
        turned = sem("turned")
        xnT_ready = sem("xnT_ready")
        gin_mm = sem("gin_mm")
        gin_act = sem("gin_act")
        gin_dve = sem("gin_dve")
        biases_ready = sem("biases_ready")
        bhn_ready = sem("bhn_ready")
        logits_ready = sem("logits_ready")
        shifted = sem("shifted")
        exps_ready = sem("exps_ready")
        onehot_ready = sem("onehot_ready")
        ranks_ready = sem("ranks_ready")
        w_ready = sem("w_ready")
        wT_mm = sem("wT_mm")
        wT_ready = sem("wT_ready")
        b2_mm = sem("b2_mm")
        b2_copied = sem("b2_copied")
        rnn_ready = sem("rnn_ready")
        ssm_ready = sem("ssm_ready")
        pre_ready = sem("pre_ready")
        th_ready = sem("th_ready")
        sumn_ready = sem("sumn_ready")
        cand_ready = sem("cand_ready")
        up_ready = sem("up_ready")
        gelu_ready = sem("gelu_ready")
        down_done = sem("down_done")
        acc_done = sem("acc_done")
        dve_step = sem("dve_step")
        silu_th = sem("silu_th")
        acc_final = sem("acc_final")
        y_ready = sem("y_ready")
        y_scaled = sem("y_scaled")
        y_used = sem("y_used")
        x1_ready = sem("x1_ready")
        stored = sem("stored")
        table_ready = sem("table_ready")
        attn_loaded = sem("attn_loaded")
        experts_loaded = sem("experts_loaded")
        probs1_mm = sem("probs1_mm")
        probs1_ready = sem("probs1_ready")
        chosen_ready = sem("chosen_ready")
        counts_mm = sem("counts_mm")
        tot_ready = sem("tot_ready")
        offs_ready = sem("offs_ready")
        place_mm = sem("place_mm")
        place_ready = sem("place_ready")
        slots_ready = sem("slots_ready")
        scattered = sem("scattered")
        zeroed = sem("zeroed")
        table_stored = sem("table_stored")
        table_loaded = sem("table_loaded")
        parity_ready = sem("parity_ready")
        xb_ready = sem("xb_ready")
        q_mm = sem("q_mm")
        qk_ready = sem("qk_ready")
        v_mm = sem("v_mm")
        v_ready = sem("v_ready")
        scores_done = sem("scores_done")
        max_ready = sem("max_ready")
        exp_done = sem("exp_done")
        tr_done = sem("tr_done")
        pt_copied = sem("pt_copied")
        pv_done = sem("pv_done")
        normed = sem("normed")
        ctxt_done = sem("ctxt_done")
        ctxT_ready = sem("ctxT_ready")
        out_done = sem("out_done")
        o_evicted = sem("o_evicted")
        weights_done = sem("weights_done")
        acc1_used = sem("acc1_used")
        shared_mm = sem("shared_mm")
        shared_ready = sem("shared_ready")
        shared_y = sem("shared_y")
        y1_ready = sem("y1_ready")
        y1_silu = sem("y1_silu")
        y1_done = sem("y1_done")
        gathered = [sem(f"gathered{i}") for i in range(16)]
        x_in, x_turned, xT_ready, up1_done, silu1_done, masked, h_turned, hT_ready, down1_done, y_out, y_stored = (
            [sem(f"{name}{h}") for h in range(2)] for name in
            ("x_in", "x_turned", "xT_ready", "up1_done", "silu1_done", "masked", "h_turned", "hT_ready",
             "down1_done", "y_out", "y_stored"))
        recip_done = sem("recip_done")

        xs_dram = nc.dram_tensor("xs_dram", (SLOTS, P), F32, kind="Internal").ap()
        ys_dram = nc.dram_tensor("ys_dram", (SLOTS, P), F32, kind="Internal").ap()
        pair_dram = nc.dram_tensor("pair_dram", (4 * P,), U8, kind="Internal").ap()
        par_dram = nc.dram_tensor("par_dram", (4 * P,), F32, kind="Internal").ap()

        block = ctx.enter_context(nc.Block())

        @block.sync
        def _(sp):
            xd = x.rearrange("(n p) d -> p n d", p=P)
            for c in range(4):
                sp.dma_start(x_tok[:, 8 * c:8 * c + 8, :], xd[:, 8 * c:8 * c + 8, :]).then_inc(x_loaded[c], 16)
            sp.wait_ge(bhn_ready, 1)
            with sp.Fori(0, SLOTS // 1024) as i:
                sp.dma_start(xs_dram[bass.ds(i * 1024, 1024), :].rearrange("(p r) d -> p (r d)", p=P), zeros[:, :]) \
                    .then_inc(zeroed, 16)
            for e in range(E0 + 1):
                if e >= 2:
                    sp.wait_ge(down_done, 32 * (e - 1) + 2)
                sp.dma_start(w1_sb[:, e % 2, :], w1[e % E0]).then_inc(w1_loaded[e % 2], 16)
                if e < E0:
                    sp.dma_start(w2_sb[:, e % 2, :, :], w2[e].rearrange("(c p) d -> p c d", p=P)) \
                        .then_inc(w2_loaded[e % 2], 16)
            sp.wait_ge(x1_ready, NG)
            for dst, src in ((rT, router), (rrow, router_row), (sg_w[:, :], shared_gate),
                             (sd_w[:, :], shared_down), (aw[:, :, :], attn_w.rearrange("p (k n) -> p k n", k=4)),
                             (acols[:, :, :], attn_cols.rearrange("p (k n) -> p k n", k=2)),
                             (arows[:, :], attn_rows.partition_broadcast(P)), (jcol[:, :], jcols),
                             (cnt_f[:, 0:63], sel_w)):
                sp.dma_start(dst, src).then_inc(attn_loaded, 16)
            sp.dma_start(gate1[:, :], w_gate).then_inc(experts_loaded, 16)
            sp.wait_ge(table_ready, 2)
            sp.dma_start(pair_dram.rearrange("(p c) -> p c", p=P), tile_u8[:, :]).then_inc(table_stored, 16)
            sp.dma_start(par_dram.rearrange("(p c) -> p c", p=P), tile_par[:, :]).then_inc(table_stored, 16)
            sp.wait_ge(table_stored, 32)
            sp.dma_start(pair_row[:, :], pair_dram.rearrange("(a n) -> a n", a=1)).then_inc(table_loaded, 16)
            sp.dma_start(par_row, par_dram.partition_broadcast(P)).then_inc(table_loaded, 16)
            sp.wait_ge(weights_done, 2 * 128)
            sp.dma_start(down1[:, :, :], w_down.rearrange("p (k n) -> p k n", n=P)).then_inc(experts_loaded, 16)

            def load_slots(it, h):
                sp.dma_start(slots_x[:, h, :].rearrange("p (s d) -> p s d", d=P),
                             xs_dram[bass.ds(it * 1024 + h * 512, 512), :].rearrange("(s p) d -> p s d", p=P)) \
                    .then_inc(x_in[h], 16)

            sp.wait_ge(scattered, 16 * NT * TOPK1)
            sp.wait_ge(o_evicted, HB)
            for h in range(2):
                load_slots(0, h)
                sp.wait_ge(x_turned[h], 1)
                load_slots(1, h)
                sp.sem_inc(y_stored[h], 16)
            with sp.Fori(0, NBODY) as it:
                for h in range(2):
                    sp.wait_ge(x_turned[h], it + 2)
                    load_slots((it + 2) % NBODY, h)
                for h in range(2):
                    sp.wait_ge(y_out[h], it + 2)
                    sp.dma_start(ys_dram[bass.ds(it * 1024 + h * 512, 512), :].rearrange("(s p) d -> p s d", p=P),
                                 slots_y[:, h, :].rearrange("p (s d) -> p s d", d=P)).then_inc(y_stored[h], 16)
            outd = out.rearrange("(n p) d -> p n d", p=P)
            for g in range(NG):
                sp.wait_ge(y1_done, g + 1)
                sp.dma_start(outd[:, 4 * g:4 * g + 4, :], x_tok[:, 4 * g:4 * g + 4, :]).then_inc(stored, 16)
            sp.wait_ge(stored, 16 * NG)
            sp.wait_ge(zeroed, 16 * (SLOTS // 1024))
            for h in range(2):
                sp.wait_ge(x_in[h], 16 * (NBODY + 2))
                sp.wait_ge(y_stored[h], 16 * (NBODY + 1))

        @block.gpsimd
        def _(pool):
            nc.gpsimd.memset(zeros[:, :], 0.0).then_inc(bhn_ready, 1)
            nc.gpsimd.memset(b1_sb[:, E0 * FC:], 0.0).then_inc(bhn_ready, 1)
            nc.gpsimd.memset(gin[:, 3, :, :], 0.0).then_inc(bhn_ready, 1)
            pool.wait_ge(bhn_ready, 3)
            pool.wait_ge(consts_loaded, 16 * 7)
            nc.gpsimd.tensor_scalar(gin[:, 3, :, :], gin[:, 3, :, :], cols_sb[:, 5:6], None, ALU.add) \
                .then_inc(bhn_ready, 1)
            pool.wait_ge(slots_ready, 1)
            pool.wait_ge(zeroed, 16 * (SLOTS // 1024))
            for n in range(NT):
                for k in range(TOPK1):
                    nc.gpsimd.indirect_dma_start(xs_dram, bass.IndirectOffsetOnAxis(ap=slot[:, n, k:k + 1], axis=0),
                                                 xn_tok[:, n, :], None).then_inc(scattered, 16)
            for h in range(2):
                pool.wait_ge(y_stored[h], 16 * (NBODY + 1))
            for i in range(NT * TOPK1):
                if i >= 16:
                    pool.wait_ge(acc1_used, i - 15)
                nc.gpsimd.indirect_dma_start(rows_g[:, i % 16, :], None, ys_dram,
                                             bass.IndirectOffsetOnAxis(
                                                 ap=slot[:, i // TOPK1, i % TOPK1:i % TOPK1 + 1], axis=0)) \
                    .then_inc(gathered[i % 16], 16)

        @block.scalar
        def _(act):
            act.dma_start(misc[:, :], misc_w).then_inc(consts_loaded, 16)
            act.dma_start(ginw[:, :], gin_w).then_inc(consts_loaded, 16)
            act.dma_start(halfw[:, :], half_w).then_inc(consts_loaded, 16)
            act.dma_start(cols_sb[:, :], cols).then_inc(consts_loaded, 16)
            act.dma_start(rows_sb[:, :], rows).then_inc(consts_loaded, 16)
            act.dma_start(b2blk[:, :], b2_blocks).then_inc(consts_loaded, 16)
            act.dma_start(b1_sb[:, 0:E0 * FC], b1).then_inc(consts_loaded, 16)

            def layer_norm(layer, scratch):
                for c in range(4):
                    act.wait_ge(centred, 4 * layer + c + 1)
                    nc.scalar.activation(scratch[:, 1024 * c:1024 * c + 1024],
                                         xn_tok[:, 8 * c:8 * c + 8, :].rearrange("p n d -> p (n d)"),
                                         ACT.Square).then_inc(squared, 1)
                act.wait_ge(var_ready, layer + 1)
                nc.scalar.activation(ln_std[:, :], ln_sq[:, :], ACT.Sqrt, bias=eps_col[:, :], scale=1.0 / P) \
                    .then_inc(std_ready, 1)

            layer_norm(0, scr2)
            for g in range(NG):
                act.wait_ge(turned, g + 1)
                nc.scalar.copy(xnT[:, 512 * g:512 * g + 512], ps_t[g % 2][:, :]).then_inc(xnT_ready, 1)
                if g == 0:
                    act.wait_ge(biases_ready, 1)
                for k in range(2):
                    act.wait_ge(gin_mm, 4 * g + k + 1)
                    nc.scalar.activation(gin[:, k, 2 * g:2 * g + 2, :], ps_up[k][:, :].rearrange("p (b t) -> p b t", b=2),
                                         ACT.Identity, bias=gin_bias[:, k:k + 1]).then_inc(gin_act, 1)
            act.wait_ge(shifted, 1)
            nc.scalar.activation(scr[:, 0:256], scr[:, 0:256], ACT.Exp).then_inc(exps_ready, 1)
            nc.scalar.activation(gate[:, :, :], gate[:, :, :], ACT.Tanh, scale=0.5).then_inc(exps_ready, 1)
            for n in range(2):
                act.wait_ge(wT_mm, n + 1)
                nc.scalar.copy(h_sb[:, 0, 128 * n:128 * n + 128], ps_t[n][:, 0:128]).then_inc(wT_ready, 1)
            for g in range(NG):
                act.wait_ge(b2_mm, g + 1)
                nc.scalar.copy(xn_tok[:, 4 * g:4 * g + 4, :].rearrange("p n d -> p (n d)"), ps_t[g % 2][:, :]) \
                    .then_inc(b2_copied, 1)

            def gelu(c, j, b1_col):
                act.wait_ge(up_ready, c + 1)
                act.wait_ge(down_done, c + 1)
                nc.scalar.activation(h_sb[:, j % 2, :], ps_up[j % 2][:, :], ACT.Gelu,
                                     bias=b1_sb[:, bass.ds(b1_col, 1)]).then_inc(gelu_ready, 1)

            gelu(0, 0, 0)
            with act.Fori(0, NG * E0) as u:
                for j in range(4):
                    t = u * 4 + j
                    act.wait_ge(pre_ready, t + 1)
                    nc.scalar.activation(th[:, j % 2, :], ps_rec[j % 2][:, 0:48], ACT.Tanh, scale=0.5) \
                        .then_inc(th_ready, 1)
                    act.wait_ge(sumn_ready, t + 1)
                    nc.scalar.activation(cand[:, j % 2, :], sumn[:, j % 2, :], ACT.Tanh, scale=0.5) \
                        .then_inc(cand_ready, 1)
                    if j < 3:
                        gelu(t + 1, j + 1, (u // 8) * 4 + j + 1)
                    else:
                        gelu(t + 1, 0, ((u + 1) // 8) * 4)
            act.wait_ge(acc_final, 1)
            nc.scalar.activation(gin[:, 0, :, :].rearrange("p b t -> p (b t)"),
                                 xn_tok[:, :, :].rearrange("p n d -> p (n d)"), ACT.Tanh, scale=0.5) \
                .then_inc(silu_th, 1)
            for n in range(NT):
                act.wait_ge(y_ready, n + 1)
                nc.scalar.mul(gin[:, 1, n // 2, 128 * (n % 2):128 * (n % 2) + 128], ps_up[n % 2][:, 0:128],
                              gate[:, n, 0:1]).then_inc(y_scaled, 1)

            layer_norm(1, att_flat)
            for g in range(NG):
                act.wait_ge(turned, NG + g + 1)
                nc.scalar.copy(xnT[:, 512 * g:512 * g + 512], ps_t[g % 2][:, :]).then_inc(xnT_ready, 1)
            act.wait_ge(attn_loaded, 16 * 9)
            nc.scalar.mul(acols[:, 0, :], acols[:, 0, :], HD ** -0.5)
            for n in range(NT):
                act.wait_ge(probs1_mm, n + 1)
                nc.scalar.activation(comb[:, n, :], ps_rec[n % 2][:, 0:E1], ACT.Sigmoid).then_inc(probs1_ready, 1)

            def copy_inputs(b, x):
                if not (isinstance(b, int) and b == 0):
                    act.wait_ge(v_mm, b * PAIRS + x)
                nc.scalar.copy(xb[:, :], xnT[:, bass.ds((b % B) * T, T)]).then_inc(xb_ready, 1)

            def qk_out(p, j, x, waits):
                act.wait_ge(q_mm, p + 1 + x)
                if waits:
                    act.wait_ge(scores_done, p * 2 - 2)
                nc.scalar.activation(qT[:, j % 2, :], ps_qk[:, 0:T], ACT.Identity, bias=acols[:, 0, j:j + 1],
                                     scale=HD ** -0.5)
                nc.scalar.activation(kT[:, j % 2, :], ps_qk[:, T:2 * T], ACT.Identity, bias=acols[:, 1, j:j + 1]) \
                    .then_inc(qk_ready, 1)

            def ctx_out(p, waits):
                act.wait_ge(ctxt_done, p + 1)
                if waits:
                    act.wait_ge(out_done, p)
                nc.scalar.copy(ctxT[:, :], ps_v[:, T:2 * T]).then_inc(ctxT_ready, 1)

            def attend(b, x, first):
                for j in range(PAIRS):
                    p = b * PAIRS + j
                    for a in range(2):
                        h = p * 2 + a
                        act.wait_ge(max_ready, h + 1)
                        if not (first and j == 0):
                            act.wait_ge(tr_done, h - 1)
                        for i in range(2):
                            nc.scalar.activation(probs[:, a, i, :], ps_s[a][:, T * i:T * i + T], ACT.Exp,
                                                 bias=negmax[:, a, i:i + 1],
                                                 accum_out=sums[:, j % 4, i, a:a + 1]).then_inc(exp_done, 1)
                        if a == 0:
                            if j == PAIRS - 1:
                                copy_inputs(b + 1, x)
                            if not (first and j < 2):
                                ctx_out(p - 2, not (first and j == 2))
                            qk_out(p + 1, (j + 1) % PAIRS, x, not (first and j == 0))

            def attend_half(b0, x):
                if x:
                    act.wait_ge(q_mm, b0 * PAIRS + 1 + x)
                    nc.scalar.copy(xb[:, :], xnT[:, T * b0:T * b0 + T]).then_inc(xb_ready, 1)
                else:
                    copy_inputs(0, 0)
                qk_out(b0 * PAIRS, 0, x, False)
                attend(b0, x, True)
                with act.Fori(b0 + 1, b0 + HB) as b:
                    attend(b, x, False)
                for p in (b0 * PAIRS + HB * PAIRS - 2, b0 * PAIRS + HB * PAIRS - 1):
                    ctx_out(p, True)

            attend_half(0, 0)

            for h in range(2):
                act.sem_inc(silu1_done[h], 1)
            act.sem_inc(y_out[0], 1)

            def xT_out(it, h):
                act.wait_ge(x_turned[h], it + 1)
                nc.scalar.copy(slots_xT[:, h, :], ps_rec[h][:, :]).then_inc(xT_ready[h], 1)

            def silu(it, h):
                act.wait_ge(up1_done[h], it + 1)
                act.wait_ge(h_turned[h], it + 1)
                nc.scalar.activation(hid[:, h, :], ps_up[h][:, :], ACT.Silu).then_inc(silu1_done[h], 1)

            for h in range(2):
                xT_out(0, h)
            with act.Fori(0, NBODY) as it:
                for h in range(2):
                    silu(it, h)
                    xT_out(it + 1, h)
                act.wait_ge(down1_done[0], it + 1)
                act.wait_ge(y_stored[0], 16 * (it + 1))
                nc.scalar.copy(slots_y[:, 0, :], ps_t[0][:, :]).then_inc(y_out[0], 1)

            for g in range(NG):
                act.wait_ge(shared_mm, g + 1)
                nc.scalar.activation(hsT[0:F1, 512 * g:512 * g + 512], ps_y[0:F1, g % 2, :], ACT.Silu) \
                    .then_inc(shared_ready, 1)
            attend_half(HB, 1)
            for g in range(NG):
                act.wait_ge(y1_ready, g + 1)
                nc.scalar.activation(xn_tok[:, 4 * g:4 * g + 4, :], xn_tok[:, 4 * g:4 * g + 4, :], ACT.Silu) \
                    .then_inc(y1_silu, 1)

        @block.tensor
        def _(pe):
            pe.wait_ge(consts_loaded, 16 * 7)

            def turn(g, layer=0):
                pe.wait_ge(xn_ready, 4 * layer + g // 2 + 1)
                if g >= 2:
                    pe.wait_ge(xnT_ready, NG * layer + g - 1)
                for s in range(4):
                    last = nc.tensor.transpose(ps_t[g % 2][:, 128 * s:128 * s + 128], xn_tok[:, 4 * g + s, :], ident)
                last.then_inc(turned, 1)

            turn(0)
            for g in range(NG):
                if g + 1 < NG:
                    turn(g + 1)
                pe.wait_ge(xnT_ready, g + 1)
                for k, dst in enumerate((ps_up[0][:, :], ps_up[1][:, :], ps_y[:, 0, :], ps_y[:, 1, :])):
                    if g:
                        pe.wait_ge(gin_act if k < 2 else gin_dve, 2 * (g - 1) + k % 2 + 1)
                    nc.tensor.matmul(dst, ginw[:, 128 * k:128 * k + 128], xnT[:, 512 * g:512 * g + 512],
                                     start=True, stop=True).then_inc(gin_mm, 1)
                for s in range(4):
                    n = 4 * g + s
                    nc.tensor.matmul(ps_rec[0][:, 10 * n:10 * n + 10], xnT[:, 128 * n:128 * n + 128], rgT,
                                     start=True, stop=False)
                    last = nc.tensor.matmul(ps_rec[0][:, 10 * n:10 * n + 10], ones[0:1, :], rows_sb[0:1, 384:394],
                                            start=False, stop=True)
            last.then_inc(logits_ready, 1)
            pe.wait_ge(onehot_ready, 1)
            nc.tensor.matmul(ps_rec[1][:, :], upper, scr[:, 1024:1536], start=True, stop=True).then_inc(ranks_ready, 1)
            nc.tensor.matmul(ps_rec[0][:, :], ones, scr[:, 1024:1536], start=True, stop=True).then_inc(ranks_ready, 1)
            pe.wait_ge(w_ready, 1)
            for n in range(2):
                nc.tensor.transpose(ps_t[n][:, 0:128], w_te[:, 16 * n:16 * n + 16, :].rearrange("p n e -> p (n e)"),
                                    ident).then_inc(wT_mm, 1)
            for g in range(NG):
                pe.wait_ge(wT_ready, 2 if g < 2 else 2)
                if g >= 2:
                    pe.wait_ge(b2_copied, g - 1)
                nc.tensor.matmul(ps_t[g % 2][:, :], h_sb[:, 0, 128 * (g // 4):128 * (g // 4) + 128],
                                 b2blk[:, 512 * (g % 4):512 * (g % 4) + 512], start=True, stop=True) \
                    .then_inc(b2_mm, 1)

            def rec_input(t, par):
                nc.tensor.matmul(ps_rec[par][:, 0:64], ident, gin[:, 0:4, :, t], start=True, stop=False,
                                 skip_group_check=True)

            def up(c, par, wbuf, f, tile, first=False):
                if not first:
                    pe.wait_ge(gelu_ready, c)
                nc.tensor.matmul(ps_up[par][:, :], w1_sb[:, wbuf, 128 * f:128 * f + 128],
                                 xnT[:, bass.ds(tile * 512, 512)], start=True, stop=True).then_inc(up_ready, 1)

            def unit(ep, u, wbuf, tile, next_tile, next_wbuf):
                for j in range(4):
                    t = u * 4 + j
                    par = j % 2
                    pe.wait_ge(rnn_ready, t + 1)
                    pe.wait_ge(ssm_ready, t + 1)
                    nc.tensor.matmul(ps_rec[par][:, 48:64], whn, hist_g[:, :, t], start=False, stop=False,
                                     skip_group_check=True)
                    nc.tensor.matmul(ps_rec[par][:, 0:16], whr, hist_g[:, :, t], start=False, stop=False,
                                     skip_group_check=True)
                    nc.tensor.matmul(ps_rec[par][:, 16:32], whz, hist_g[:, :, t], start=False, stop=False,
                                     skip_group_check=True)
                    nc.tensor.matmul(ps_rec[par][:, 32:48], aT, hist_s[:, :, t], start=False, stop=True,
                                     skip_group_check=True).then_inc(pre_ready, 1)
                    if j < 3:
                        up(t + 1, 1 - par, wbuf, j + 1, tile)
                    else:
                        up(t + 1, 1 - par, next_wbuf, 0, next_tile)
                    rec_input((t + 1) % T, 1 - par)
                    if j == 0:
                        pe.wait_ge(acc_done, u * 4 + 4)
                        pe.wait_ge(w2_loaded[wbuf], 16 * (ep + 1))
                    pe.wait_ge(gelu_ready, t + 2)
                    for s in range(4):
                        last = nc.tensor.matmul(ps_y[:, tile % 2, 128 * s:128 * s + 128],
                                                h_sb[:, par, 128 * s:128 * s + 128], w2_sb[:, wbuf, j, :],
                                                start=(j == 0 and s == 0), stop=(j == 3), skip_group_check=True)
                    last.then_inc(down_done, 1)

            pe.sem_inc(down_done, 2)
            pe.sem_inc(gelu_ready, 1)
            pe.wait_ge(bhn_ready, 4)
            pe.wait_ge(gin_act, 2 * NG)
            pe.wait_ge(gin_dve, 2 * NG)
            pe.wait_ge(w1_loaded[0], 16)
            pe.wait_ge(b2_copied, NG)
            up(0, 0, 0, 0, 0, first=True)
            pe.wait_ge(rnn_ready, 1)
            rec_input(0, 0)
            with pe.Fori(0, E0 // 2) as ep:
                for half in range(2):
                    with pe.Fori(0, NG - 1) as tile:
                        unit(ep, (ep * 2 + half) * 8 + tile, half, tile, tile + 1, half)
                    pe.wait_ge(w1_loaded[1 - half], 16 * (ep + 1 + half))
                    unit(ep, (ep * 2 + half) * 8 + 7, half, 7, 0, 1 - half)
            pe.wait_ge(rnn_ready, T + 1)
            pe.wait_ge(ssm_ready, T + 1)
            pe.wait_ge(gelu_ready, 4 * NG * E0 + 2)
            for n in range(NT):
                b, h = n // 2, n % 2
                if n >= 2:
                    pe.wait_ge(y_scaled, n - 1)
                    pe.wait_ge(y_used, n - 1)
                nc.tensor.matmul(ps_up[n % 2][:, 0:128], hist_s[:, b, 1 + 128 * h:129 + 128 * h], cwT,
                                 start=True, stop=False)
                nc.tensor.matmul(ps_up[n % 2][:, 0:128], xnT[:, 128 * n:128 * n + 128], dwT, start=False, stop=False)
                for k in range(2):
                    nc.tensor.matmul(ps_up[n % 2][:, 0:128], ones[0:1, :], rows_sb[0:1, 128 * k:128 * k + 128],
                                     start=False, stop=k == 1)
                nc.tensor.matmul(ps_t[n % 2][:, 0:128], hist_g[:, b, 1 + 128 * h:129 + 128 * h], projT,
                                 start=True, stop=False)
                nc.tensor.matmul(ps_t[n % 2][:, 0:128], ones[0:1, :], rows_sb[0:1, 256:384],
                                 start=False, stop=True).then_inc(y_ready, 1)

            for g in range(NG):
                turn(g, 1)
            pe.wait_ge(attn_loaded, 16 * 9)
            for n in range(NT):
                pe.wait_ge(xnT_ready, NG + n // 4 + 1)
                if n >= 2:
                    pe.wait_ge(probs1_ready, n - 1)
                nc.tensor.matmul(ps_rec[n % 2][:, 0:E1], xnT[:, P * n:P * n + P], rT, start=True, stop=False)
                nc.tensor.matmul(ps_rec[n % 2][:, 0:E1], ones[0:1, :], rrow, start=False, stop=True) \
                    .then_inc(probs1_mm, 1)
            pe.wait_ge(chosen_ready, 1)
            for n in range(NT):
                last = nc.tensor.matmul(ps_up[0][:, 0:E1], ones_b, chosen[:, n, :], start=(n == 0), stop=(n == NT - 1))
            last.then_inc(counts_mm, 1)
            for n in range(NT):
                last = nc.tensor.matmul(ps_up[1][0:NT, 0:E1], sel_b[:, 31 - n:63 - n], chosen[:, n, :],
                                        start=(n == 0), stop=(n == NT - 1))
            last.then_inc(counts_mm, 1)
            pe.wait_ge(tot_ready, 1)
            pe.wait_ge(offs_ready, 1)
            pe.wait_ge(probs1_ready, NT)
            for n in range(NT):
                dst = (ps_rec[n % 2])[:, 0:E1]
                if n >= 2:
                    pe.wait_ge(place_ready, n - 1)
                nc.tensor.matmul(dst, ones[0:1, :], offs, start=True, stop=False)
                if n:
                    nc.tensor.matmul(dst, upper_b[0:NT, n - 1:n].to_broadcast([NT, P]), tile_tot,
                                     start=False, stop=False)
                nc.tensor.matmul(dst, upper_b, chosen[:, n, :], start=False, stop=True).then_inc(place_mm, 1)
            pe.wait_ge(place_ready, NT)

            def qk_mm(b, j, p, x):
                if not (isinstance(p, int) and p == 0):
                    pe.wait_ge(qk_ready, p + x)
                src = xnT[:, bass.ds(b * T, T)]
                nc.tensor.matmul(ps_qk[:, 0:T], aw[:, 0, P * j:P * j + P], src, start=True, stop=True)
                nc.tensor.matmul(ps_qk[:, T:2 * T], aw[:, 1, P * j:P * j + P], src, start=True, stop=True) \
                    .then_inc(q_mm, 1)

            def v_mm_(b, j, p, x, ctx_before):
                pe.wait_ge(xb_ready, b + 1 + x)
                if not (isinstance(p, int) and p == 0):
                    pe.wait_ge(v_ready, p + x)
                if ctx_before:
                    pe.wait_ge(ctxT_ready, p - 2)
                for i in range(2):
                    last = nc.tensor.matmul(ps_v[:, P * i:P * i + P], xb[:, P * i:P * i + P],
                                            aw[:, 2, P * j:P * j + P], start=True, stop=True)
                last.then_inc(v_mm, 1)

            def turn_probs(h, a, waits):
                pe.wait_ge(exp_done, h * 2 + 2)
                if waits:
                    pe.wait_ge(pt_copied, h - 1)
                for kc in range(2):
                    for i in range(2):
                        last = nc.tensor.transpose(ps_y[:, a, T * kc + P * i:T * kc + P * i + P],
                                                   probs[:, a, i, P * kc:P * kc + P], ident)
                last.then_inc(tr_done, 1)

            def values(h, p, j, a, x, waits):
                pe.wait_ge(pt_copied, h + 1)
                pe.wait_ge(v_ready, p + 1 + x)
                if a == 0 and waits:
                    pe.wait_ge(normed, p)
                for i in range(2):
                    for kc in range(2):
                        last = nc.tensor.matmul(ps_ctx[:, P * i + HD * a:P * i + HD * a + HD],
                                                probsT[:, a, kc, P * i:P * i + P],
                                                v_sb[:, j % 2, kc, HD * a:HD * a + HD],
                                                start=(kc == 0), stop=(kc == 1))
                last.then_inc(pv_done, 1)

            def turn_ctx(p, last_v):
                pe.wait_ge(normed, p + 1)
                pe.wait_ge(v_ready, last_v)
                for i in range(2):
                    last = nc.tensor.transpose(ps_v[:, T + P * i:T + P * i + P], ctx_sb[:, i, :], ident)
                last.then_inc(ctxt_done, 1)

            def project(p, j, b_out):
                pe.wait_ge(ctxT_ready, p + 1)
                if j == 0 and b_out is not None:
                    pe.wait_ge(o_evicted, b_out)
                for i in range(2):
                    last = nc.tensor.matmul(ps_o[:, P * i:P * i + P], ctxT[:, P * i:P * i + P],
                                            aw[:, 3, P * j:P * j + P], start=(j == 0 and i == 0), stop=(j == PAIRS - 1),
                                            skip_group_check=True)
                last.then_inc(out_done, 1)

            def attend(b, x, first):
                for j in range(PAIRS):
                    p = b * PAIRS + j
                    for a in range(2):
                        h = p * 2 + a
                        early = first and j == 0
                        pe.wait_ge(qk_ready, p + 1 + x)
                        if not early:
                            pe.wait_ge(exp_done, h * 2 - 2)
                        for i in range(2):
                            last = nc.tensor.matmul(ps_s[a][:, T * i:T * i + T],
                                                    qT[HD * a:HD * a + HD, j % 2, P * i:P * i + P],
                                                    kT[HD * a:HD * a + HD, j % 2, :], start=True, stop=True)
                        last.then_inc(scores_done, 1)
                        if not (early and a == 0):
                            turn_probs(h - 1, 1 - a, not (first and 2 * j + a - 1 < 2))
                        if not early:
                            values(h - 2, p - 1, (j - 1) % PAIRS, a, x, not (first and j == 1))
                        if a == 0:
                            if not (first and j < 2):
                                turn_ctx(p - 2, p + 1 + x)
                            if j + 1 < PAIRS:
                                qk_mm(b, j + 1, p + 1, x)
                            else:
                                qk_mm((b + 1) % B, 0, p + 1, x)
                        else:
                            v_mm_(b + (j + 1) // PAIRS, (j + 1) % PAIRS, p + 1, x, not (first and j < 2))
                            if not (first and j < 2):
                                jo = (j - 2) % PAIRS
                                project(p - 2, jo, None if first else b)

            def attend_half(b0, x):
                qk_mm(b0, 0, b0 * PAIRS, x)
                v_mm_(b0, 0, b0 * PAIRS, x, False)
                attend(b0, x, True)
                with pe.Fori(b0 + 1, b0 + HB) as b:
                    attend(b, x, False)
                p = (b0 + HB) * PAIRS
                turn_probs(2 * p - 1, 1, True)
                values(2 * p - 2, p - 1, PAIRS - 1, 0, x, True)
                values(2 * p - 1, p - 1, PAIRS - 1, 1, x, True)
                for q in (p - 2, p - 1):
                    turn_ctx(q, p + 1 + x)
                    project(q, q % PAIRS, None)

            attend_half(0, 0)

            pe.wait_ge(experts_loaded, 32)
            pe.wait_ge(table_loaded, 32)
            pe.wait_ge(o_evicted, HB)
            pe.wait_ge(v_ready, HB * PAIRS + 1)
            pe.wait_ge(qk_ready, HB * PAIRS + 1)
            for h in range(2):
                pe.sem_inc(h_turned[h], 1)
            words = pair_row[:, :].bitcast(I32)

            def turn_slots(it, h):
                pe.wait_ge(x_in[h], 16 * (it + 1))
                if not isinstance(it, int):
                    pe.wait_ge(xT_ready[h], it)
                for s in range(4):
                    last = nc.tensor.transpose(ps_rec[h][:, P * s:P * s + P], slots_x[:, h, P * s:P * s + P], ident)
                last.then_inc(x_turned[h], 1)

            for h in range(2):
                turn_slots(0, h)
            with pe.Fori(0, NBODY) as it:
                pairs = []
                for h in range(2):
                    word = pe.value_load(words[0:1, bass.ds(it * 2 + h, 1)], min_val=0, max_val=2 ** 31 - 1)
                    pairs.append([nc.s_assert_within((word // 256 ** s) % 128, 0, E1 // 2 - 1,
                                                     skip_runtime_bounds_check_because="the table holds pairs") for s in range(4)])
                for h in range(2):
                    pe.wait_ge(xT_ready[h], it + 1)
                    pe.wait_ge(silu1_done[h], it + 1)
                    for s in range(4):
                        last = nc.tensor.matmul(ps_up[h][:, P * s:P * s + P], slots_xT[:, h, P * s:P * s + P],
                                                gate1[:, bass.ds(pairs[h][s] * P, P)], start=True, stop=True)
                    last.then_inc(up1_done[h], 1)
                for h in range(2):
                    turn_slots(it + 1, h)
                    pe.wait_ge(masked[h], it + 1)
                    for s in range(4):
                        last = nc.tensor.transpose(ps_y[:, h, P * s:P * s + P], hid[:, h, P * s:P * s + P], ident)
                    last.then_inc(h_turned[h], 1)
                for h in range(2):
                    pe.wait_ge(hT_ready[h], it + 1)
                    pe.wait_ge(y_out[h], it + 1)
                    for s in range(4):
                        last = nc.tensor.matmul(ps_t[h][:, P * s:P * s + P], hidT[:, h, P * s:P * s + P],
                                                down1[:, :, :].rearrange("p k n -> p (k n)")[
                                                    :, bass.ds(pairs[h][s] * P, P)], start=True, stop=True)
                    last.then_inc(down1_done[h], 1)
            for g in range(NG):
                if g >= 2:
                    pe.wait_ge(shared_ready, g - 1)
                nc.tensor.matmul(ps_y[0:F1, g % 2, :], sg_w[:, :], xnT[:, 512 * g:512 * g + 512],
                                 start=True, stop=True).then_inc(shared_mm, 1)
            pe.wait_ge(shared_ready, NG)
            for h in range(2):
                pe.wait_ge(y_stored[h], 16 * (NBODY + 1))
                pe.wait_ge(xT_ready[h], NBODY + 1)
                pe.wait_ge(y_out[h], NBODY + 1)
                pe.wait_ge(x_in[h], 16 * (NBODY + 2))
            attend_half(HB, 1)
            pe.wait_ge(o_evicted, B)
            for g in range(NG):
                if g >= 2:
                    pe.wait_ge(y1_ready, g - 1)
                for s in range(4):
                    n = 4 * g + s
                    last = nc.tensor.matmul(ps_y[:, g % 2, P * s:P * s + P], hsT[0:F1, P * n:P * n + P], sd_w[:, :],
                                            start=True, stop=True)
                last.then_inc(shared_y, 1)


        @block.vector
        def _(dve):
            steps = Count(dve_done)

            def chain(ins):
                dve.wait_ge(dve_done, steps.raised_by(ins))

            def across(col, shape):
                return col.unsqueeze(len(shape) - 1).to_broadcast(shape)

            V = nc.vector
            chain(V.memset(eps_col[:, :], EPS))

            def layer_norm(layer, scratch):
                for c in range(4):
                    s = slice(8 * c, 8 * c + 8)
                    if layer == 0:
                        dve.wait_ge(x_loaded[c], 16)
                    chain(V.tensor_reduce(ln_sum[:, s], x_tok[:, s, :], AX_X, ALU.add))
                    chain(V.tensor_scalar(ln_mean[:, s], ln_sum[:, s], 1.0 / P, None, ALU.mult))
                    V.tensor_tensor(xn_tok[:, s, :], x_tok[:, s, :], across(ln_mean[:, s], [P, 8, P]), ALU.subtract) \
                        .then_inc(centred, 1)
                for c in range(4):
                    s = slice(8 * c, 8 * c + 8)
                    dve.wait_ge(squared, 4 * layer + c + 1)
                    red = V.tensor_reduce(ln_sq[:, s],
                                          scratch[:, 1024 * c:1024 * c + 1024].rearrange("p (n d) -> p n d", d=P),
                                          AX_X, ALU.add)
                red.then_inc(var_ready, 1)
                dve.wait_ge(std_ready, layer + 1)
                chain(V.reciprocal(ln_rstd[:, :], ln_std[:, :]))
                for c in range(4):
                    s = slice(8 * c, 8 * c + 8)
                    V.tensor_tensor(xn_tok[:, s, :], xn_tok[:, s, :], across(ln_rstd[:, s], [P, 8, P]), ALU.mult) \
                        .then_inc(xn_ready, 1)

            layer_norm(0, scr2)
            dve.wait_ge(consts_loaded, 16 * 7)
            chain(V.tensor_scalar(halfw[:, :], halfw[:, :], 0.5, None, ALU.mult))
            chain(V.tensor_tensor(gin_bias[:, 0:2], cols_sb[:, 0:2], cols_sb[:, 3:5], ALU.add))
            chain(V.tensor_copy(gin_bias[:, 2:3], cols_sb[:, 6:7]))
            V.tensor_copy(gin_bias[:, 3:4], cols_sb[:, 2:3]).then_inc(biases_ready, 1)
            dve.wait_ge(biases_ready, 1)
            for g in range(NG):
                dve.wait_ge(gin_mm, 4 * g + 3)
                V.tensor_scalar(gin[:, 2, 2 * g:2 * g + 2, :], ps_y[:, 0, :].rearrange("p (b t) -> p b t", b=2),
                                gin_bias[:, 2:3], None, ALU.add).then_inc(gin_dve, 1)
                dve.wait_ge(gin_mm, 4 * g + 4)
                V.tensor_scalar(gin[:, 4, 2 * g:2 * g + 2, :], ps_y[:, 1, :].rearrange("p (b t) -> p b t", b=2),
                                gin_bias[:, 3:4], 2.0, ALU.add, ALU.mult).then_inc(gin_dve, 1)

            def s3(a, k):
                return scr[:, a:a + NT * k].rearrange("p (n e) -> p n e", e=k)

            lg, eq = s3(0, 8), s3(256, 8)
            oh = s3(1024, 16)
            col = [scr[:, 2560 + NT * k:2560 + NT * k + NT] for k in range(8)]
            wide = [P, NT, 8]
            dve.wait_ge(logits_ready, 1)
            psl = ps_rec[0][:, 0:320].rearrange("p (n e) -> p n e", e=10)
            chain(V.tensor_copy(gate[:, :, :], psl[:, :, 8:10]))
            chain(V.tensor_reduce(col[0], psl[:, :, 0:8], AX_X, ALU.max))
            V.tensor_tensor(lg, psl[:, :, 0:8], across(col[0], wide), ALU.subtract).then_inc(shifted, 1)
            dve.wait_ge(exps_ready, 2)
            chain(V.tensor_scalar(gate[:, :, :], gate[:, :, :], 1.0, 0.25, ALU.add, ALU.mult))
            chain(V.tensor_reduce(col[0], lg, AX_X, ALU.add))
            chain(V.reciprocal(col[1], col[0]))
            chain(V.tensor_tensor(lg, lg, across(col[1], wide), ALU.mult))
            for k in range(2):
                ohk = oh[:, :, 8 * k:8 * k + 8]
                chain(V.tensor_reduce(col[2 + k], lg, AX_X, ALU.max))
                chain(V.tensor_tensor(eq, lg, across(col[2 + k], wide), ALU.is_equal))
                chain(V.tensor_tensor(eq, eq, desc.unsqueeze(1).to_broadcast(wide), ALU.mult))
                chain(V.tensor_reduce(col[4], eq, AX_X, ALU.max))
                chain(V.tensor_tensor(ohk, eq, across(col[4], wide), ALU.is_equal))
                if k == 0:
                    chain(V.scalar_tensor_tensor(out=lg, in0=ohk, scalar=-4.0, in1=lg, op0=ALU.mult, op1=ALU.add))
            V.tensor_tensor(col[5], col[2], col[3], ALU.add).then_inc(onehot_ready, 1)
            dve.wait_ge(onehot_ready, 1)
            chain(V.reciprocal(col[6], col[5]))
            for k in range(2):
                chain(V.tensor_tensor(col[2 + k], col[2 + k], col[6], ALU.mult))
            dve.wait_ge(ranks_ready, 2)
            a, b_ = scr[:, 3072:3584], scr[:, 3584:4096]
            chain(V.tensor_copy(a, ps_rec[0][:, :]))
            for k in (16, 32, 64, 128, 256):
                chain(V.tensor_copy(b_[:, 0:k], a[:, 0:k]))
                chain(V.tensor_tensor(b_[:, k:512], a[:, k:512], a[:, 0:512 - k], ALU.add))
                a, b_ = b_, a
            chain(V.tensor_tensor(a, a, ps_rec[0][:, :], ALU.subtract))
            chain(V.tensor_tensor(a, a, ps_rec[1][:, :], ALU.add))
            chain(V.scalar_tensor_tensor(out=b_, in0=a, scalar=float(CAP0), in1=scr[:, 1024:1536],
                                         op0=ALU.is_le, op1=ALU.mult))
            b3 = b_.rearrange("p (n e) -> p n e", e=16)
            chain(V.tensor_tensor(lg, b3[:, :, 0:8], across(col[2], wide), ALU.mult))
            chain(V.tensor_tensor(eq, b3[:, :, 8:16], across(col[3], wide), ALU.mult))
            V.tensor_tensor(w_te[:, :, :], lg, eq, ALU.add).then_inc(w_ready, 1)
            dve.wait_ge(w_ready, 1)
            V.memset(hist_s[:, :, 0], 0.0).then_inc(ssm_ready, 1)
            V.memset(hist_g[:, :, 0], 0.0).then_inc(rnn_ready, 1)
            dve.sem_inc(acc_done, 8)
            dve.wait_ge(b2_copied, NG)

            def accumulate(n, w_col):
                V.scalar_tensor_tensor(out=xn_tok[:, n, :], in0=ps_y[:, w_col[2], 128 * w_col[3]:128 * w_col[3] + 128],
                                       scalar=w_te[:, n, bass.ds(w_col[1], 1)], in1=xn_tok[:, n, :],
                                       op0=ALU.mult, op1=ALU.add).then_inc(acc_done, 1)

            def step(u, j, first):
                t = u * 4 + j
                par = j % 2
                dve.wait_ge(th_ready, t + 1)
                V.scalar_tensor_tensor(out=mixn[:, :], in0=th[:, par, 0:16], scalar=1.0, in1=ps_rec[par][:, 48:64],
                                       op0=ALU.add, op1=ALU.mult).then_inc(dve_step, 1)
                dve.wait_ge(dve_step, t * 4 + 1)
                V.tensor_tensor(sumn[:, par, :], mixn[:, :], gin[:, 4, :, t], ALU.add).then_inc(sumn_ready, 1)
                V.scalar_tensor_tensor(out=hist_s[:, :, t + 1], in0=th[:, par, 32:48], scalar=1.0,
                                       in1=ps_rec[par][:, 32:48], op0=ALU.add, op1=ALU.mult).then_inc(ssm_ready, 1)
                V.scalar_tensor_tensor(out=zg[:, :], in0=th[:, par, 16:32], scalar=1.0, in1=hist_g[:, :, t],
                                       op0=ALU.add, op1=ALU.mult).then_inc(dve_step, 1)
                V.tensor_scalar(omz[:, :], th[:, par, 16:32], -1.0, 1.0, ALU.mult, ALU.add).then_inc(dve_step, 1)
                dve.wait_ge(cand_ready, t + 1)
                dve.wait_ge(dve_step, t * 4 + 3)
                V.tensor_tensor(newn[:, :], omz[:, :], cand[:, par, :], ALU.mult).then_inc(dve_step, 1)
                dve.wait_ge(dve_step, t * 4 + 4)
                V.scalar_tensor_tensor(out=hist_g[:, :, t + 1], in0=zg[:, :], scalar=0.5, in1=newn[:, :],
                                       op0=ALU.mult, op1=ALU.add).then_inc(rnn_ready, 1)
                dve.wait_ge(rnn_ready, t + 2)
                if not first:
                    v = u - 1
                    if j == 0:
                        dve.wait_ge(down_done, u * 4 + 2)
                    accumulate((v % 8) * 4 + j, (0, v // 8, v % 2, j))

            for j in range(4):
                step(0, j, True)
            with dve.Fori(1, NG * E0) as u:
                for j in range(4):
                    step(u, j, False)
            dve.wait_ge(down_done, 4 * NG * E0 + 2)
            last_u = NG * E0 - 1
            for j in range(4):
                accumulate(4 * (last_u % 8) + j, (0, last_u // 8, last_u % 2, j))
            dve.wait_ge(acc_done, 4 * NG * E0 + 8)
            dve.sem_inc(acc_final, 1)
            dve.wait_ge(silu_th, 1)
            sil = gin[:, 0, :, :].rearrange("p b t -> p (b t)")
            chain(V.scalar_tensor_tensor(out=sil, in0=sil, scalar=1.0, in1=xn_tok[:, :, :].rearrange("p n d -> p (n d)"),
                                         op0=ALU.add, op1=ALU.mult))
            for n in range(NT):
                y1 = gin[:, 1, n // 2, 128 * (n % 2):128 * (n % 2) + 128]
                dve.wait_ge(y_scaled, n + 1)
                V.scalar_tensor_tensor(out=gin[:, 2, n // 2, 128 * (n % 2):128 * (n % 2) + 128],
                                       in0=ps_t[n % 2][:, 0:128], scalar=gate[:, n, 1:2], in1=y1,
                                       op0=ALU.mult, op1=ALU.add).then_inc(y_used, 1)
            s_all = gin[:, 2, :, :].rearrange("p b t -> p (b t)")
            x_all = x_tok[:, :, :].rearrange("p n d -> p (n d)")
            for g in range(NG):
                q = slice(512 * g, 512 * g + 512)
                dve.wait_ge(y_used, 4 * g + 4)
                chain(V.tensor_tensor(sil[:, q], sil[:, q], s_all[:, q], ALU.mult))
                V.tensor_tensor(x_all[:, q], x_all[:, q], sil[:, q], ALU.add).then_inc(x1_ready, 1)

            dve.wait_ge(x1_ready, NG)
            layer_norm(1, att_flat)
            dve.wait_ge(attn_loaded, 16 * 9)
            chain(V.tensor_copy(upper_b, upper))
            chain(V.tensor_copy(ones_b, ones))
            chain(V.tensor_copy(sel_b, cnt_f[:, 0:63]))
            for n in range(NT):
                dve.wait_ge(probs1_ready, n + 1)
                tops = V.max(top8[:, n, :], comb[:, n, :])
            chain(tops)
            for n in range(NT):
                marks = V.match_replace(out=place[:, n, :], in_to_replace=top8[:, n, :], in_values=comb[:, n, :],
                                        imm_value=-1.0)
            chain(marks)
            V.tensor_scalar(chosen, place[:, :, :], 0.0, None, ALU.is_lt).then_inc(chosen_ready, 1)
            dve.wait_ge(counts_mm, 2)
            V.tensor_copy(tile_tot, ps_up[1][0:NT, 0:E1]).then_inc(tot_ready, 1)
            chain(V.tensor_scalar(cnt_i, ps_up[0][:, 0:E1], float(P - 1), None, ALU.add))
            chain(V.tensor_scalar(cnt_i, cnt_i, 7, None, ALU.arith_shift_right))
            chain(V.tensor_copy(cnt_f, cnt_i))
            chain(V.memset(junk[:, 0, :], 1.0))
            chain(V.tensor_tensor_scan(cnt_inc, junk[:, 0, :], cnt_f, 0.0, ALU.mult, ALU.add))
            chain(V.tensor_tensor(offs, cnt_inc[0:1, :], cnt_f[0:1, :], ALU.subtract))
            V.tensor_scalar(offs, offs, float(P), None, ALU.mult).then_inc(offs_ready, 1)
            for c in range(4):
                chain(V.tensor_scalar(junk[:, 0, :], cnt_inc, jcol[:, c:c + 1], None, ALU.is_le))
                chain(V.tensor_reduce(tile_e[:, c:c + 1], junk[:, 0, :], AX_X, ALU.add))
            chain(V.tensor_scalar(tile_e[:, :], tile_e[:, :], float(E1 - 1), None, ALU.min))
            chain(V.tensor_copy(tile_i[:, :], tile_e[:, :]))
            chain(V.tensor_scalar(tile_i[:, :], tile_i[:, :], 1, None, ALU.arith_shift_right))
            chain(V.tensor_copy(tile_par[:, :], tile_i[:, :]))
            V.tensor_copy(tile_u8[:, :], tile_par[:, :]).then_inc(table_ready, 1)
            dve.wait_ge(table_ready, 1)
            V.scalar_tensor_tensor(out=tile_par[:, :], in0=tile_par[:, :], scalar=-2.0, in1=tile_e[:, :],
                                   op0=ALU.mult, op1=ALU.add).then_inc(table_ready, 1)
            for n in range(NT):
                dve.wait_ge(place_mm, n + 1)
                V.tensor_tensor(place[:, n, :], ps_rec[n % 2][:, 0:E1], chosen[:, n, :], ALU.mult) \
                    .then_inc(place_ready, 1)
            dve.wait_ge(place_ready, NT)
            for n in range(NT):
                tops = V.max(place8[:, n, :], place[:, n, :])
            chain(tops)
            V.tensor_scalar(slot[:, :, :], place8[:, :, :], -1.0, None, ALU.add).then_inc(slots_ready, 1)
            chain(V.tensor_reduce(ln_sum[:, :], top8[:, :, :], AX_X, ALU.add))
            chain(V.tensor_scalar(ln_sum[:, :], ln_sum[:, :], 1e-9, None, ALU.add))
            chain(V.reciprocal(ln_mean[:, :], ln_sum[:, :]))
            dve.wait_ge(table_loaded, 32)
            chain(V.tensor_copy(parity[:, :, 1], par_row))
            V.tensor_scalar(parity[:, :, 0], par_row, -1.0, 1.0, ALU.mult, ALU.add).then_inc(parity_ready, 1)

            def weights_of(n, k):
                if not (isinstance(n, int) and n == 0 and k < 2):
                    dve.wait_ge(weights_done, n * TOPK1 + k - 1)
                V.scalar_tensor_tensor(out=junk[:, k % 2, :], in0=place[:, n, :], scalar=place8[:, n, k:k + 1],
                                       in1=comb[:, n, :], op0=ALU.is_equal, op1=ALU.mult,
                                       accum_out=w8[:, n, k:k + 1]).then_inc(weights_done, 1)

            def add_row(m, t4, k):
                n = m * 4 + t4
                dve.wait_ge(gathered[(t4 % 2) * 8 + k], 16 * (m * 2 + t4 // 2 + 1))
                row = rows_g[:, (t4 % 2) * 8 + k, :]
                if k == 0:
                    V.tensor_scalar(xn_tok[:, n, :], row, w8[:, n, 0:1], None, ALU.mult).then_inc(acc1_used, 1)
                else:
                    dve.wait_ge(acc1_used, m * 32 + t4 * 8 + k)
                    V.scalar_tensor_tensor(out=xn_tok[:, n, :], in0=row, scalar=w8[:, n, k:k + 1],
                                           in1=xn_tok[:, n, :], op0=ALU.mult, op1=ALU.add).then_inc(acc1_used, 1)

            def values_out(p, j, x, waits):
                dve.wait_ge(v_mm, p + 1 + x)
                if waits:
                    dve.wait_ge(pv_done, p * 2 - 2)
                V.tensor_tensor(v_sb[:, j % 2, :, :], ps_v[:, 0:2 * P].rearrange("p (i d) -> p i d", i=2),
                                arows[:, P * j:P * j + P].unsqueeze(1).to_broadcast([P, 2, P]), ALU.add) \
                    .then_inc(v_ready, 1)

            def probs_out(h, a, waits):
                dve.wait_ge(tr_done, h + 1)
                if waits:
                    dve.wait_ge(pv_done, h - 1)
                V.tensor_copy(probsT[:, a, :, :].rearrange("p c t -> p (c t)"), ps_y[:, a, :]).then_inc(pt_copied, 1)

            def normalise(p, j, waits):
                dve.wait_ge(pv_done, p * 2 + 2)
                V.reciprocal(rsums[:, :, :], sums[:, j % 4, :, :]).then_inc(recip_done, 1)
                dve.wait_ge(recip_done, p + 1)
                if waits:
                    dve.wait_ge(ctxt_done, p)
                V.tensor_tensor(ctx_sb[:, :, :].rearrange("p i (a d) -> p (i a) d", a=2),
                                ps_ctx[:, 0:2 * P].rearrange("p (k d) -> p k d", k=4),
                                rsums[:, :, :].rearrange("p i a -> p (i a)").unsqueeze(2).to_broadcast([P, 4, HD]),
                                ALU.mult).then_inc(normed, 1)

            def output_out(b):
                dve.wait_ge(out_done, b * PAIRS + PAIRS)
                V.tensor_tensor(att[:, bass.ds(b * 2, 2), :], ps_o[:, 0:2 * P].rearrange("p (i d) -> p i d", i=2),
                                arows[:, HEADS * HD:].unsqueeze(1).to_broadcast([P, 2, P]), ALU.add) \
                    .then_inc(o_evicted, 1)

            def attend(b, x, first):
                for j in range(PAIRS):
                    p = b * PAIRS + j
                    for a in range(2):
                        h = p * 2 + a
                        if a == 0 and not (first and j < 2):
                            normalise(p - 2, (j - 2) % PAIRS, not (first and j == 2))
                        dve.wait_ge(scores_done, h + 1)
                        V.tensor_reduce(negmax[:, a, :], ps_s[a][:, :].rearrange("p (i t) -> p i t", i=2), AX_X,
                                        ALU.max, negate=True).then_inc(max_ready, 1)
                        if not (first and j == 0 and a == 0):
                            probs_out(h - 1, 1 - a, not (first and 2 * j + a - 1 < 2))
                        if a == 1:
                            values_out(p + 1, (j + 1) % PAIRS, x, not (first and j == 0))
                            if j == 1 and not first:
                                output_out(b - 1)
                        t4, k = (2 * j + a) // 4, 2 * ((2 * j + a) % 4)
                        for kk in (k, k + 1):
                            if x == 0:
                                weights_of(b * 4 + t4, kk)
                            else:
                                add_row(b - HB, t4, kk)

            def attend_half(b0, x):
                values_out(b0 * PAIRS, 0, x, False)
                attend(b0, x, True)
                with dve.Fori(b0 + 1, b0 + HB) as b:
                    attend(b, x, False)
                p = (b0 + HB) * PAIRS
                probs_out(2 * p - 1, 1, True)
                normalise(p - 2, (p - 2) % PAIRS, True)
                normalise(p - 1, (p - 1) % PAIRS, True)
                output_out(b0 + HB - 1)

            attend_half(0, 0)
            dve.wait_ge(weights_done, NT * TOPK1)
            chain(V.tensor_tensor(w8[:, :, :], w8[:, :, :], across(ln_mean[:, :], [P, NT, TOPK1]), ALU.mult))
            chain(V.tensor_scalar(w8[:, :, :], w8[:, :, :], 2.5, None, ALU.mult))

            dve.wait_ge(parity_ready, 1)
            dve.sem_inc(y_out[1], 1)
            with dve.Fori(0, NBODY) as it:
                for h in range(2):
                    dve.wait_ge(silu1_done[h], it + 2)
                    hh = hid[:, h, :].rearrange("p (k i) -> p k i", i=F1)
                    pr = parity[:, :, :].rearrange("p n k -> p (n k)")[:, bass.ds(it * 16 + h * 8, 8)]
                    V.tensor_tensor(hh, hh, pr.unsqueeze(2).to_broadcast([P, 8, F1]), ALU.mult) \
                        .then_inc(masked[h], 1)
                for h in range(2):
                    dve.wait_ge(h_turned[h], it + 2)
                    V.tensor_copy(hidT[:, h, :], ps_y[:, h, :]).then_inc(hT_ready[h], 1)
                dve.wait_ge(down1_done[1], it + 1)
                dve.wait_ge(y_stored[1], 16 * (it + 1))
                V.tensor_copy(slots_y[:, 1, :], ps_t[1][:, :]).then_inc(y_out[1], 1)

            attend_half(HB, 1)
            for g in range(NG):
                q = slice(4 * g, 4 * g + 4)
                dve.wait_ge(shared_y, g + 1)
                dve.wait_ge(acc1_used, 32 * g + 32)
                V.tensor_tensor(xn_tok[:, q, :], xn_tok[:, q, :],
                                ps_y[:, g % 2, :].rearrange("p (n d) -> p n d", d=P), ALU.add).then_inc(y1_ready, 1)
            for g in range(NG):
                q = slice(4 * g, 4 * g + 4)
                dve.wait_ge(y1_silu, g + 1)
                chain(V.tensor_tensor(xn_tok[:, q, :], xn_tok[:, q, :], att[:, q, :], ALU.mult))
                V.tensor_tensor(x_tok[:, q, :], x_tok[:, q, :], xn_tok[:, q, :], ALU.add).then_inc(y1_done, 1)


def kernel(**inputs):
    import concourse.bacc as _bacc
    from concourse.bass_utils import run_bass_kernel_spmd as _run

    I = {k: np.asarray(v) for k, v in inputs.items()}
    f = np.float32
    z64 = np.zeros((P, 64), f)

    def padT(w):
        m = np.zeros((P, P), w.dtype)
        m[:w.shape[1], :w.shape[0]] = w.T
        return m

    wih, whh = I["L0_attn_W_ih"], I["L0_attn_W_hh"]
    gin_w = np.concatenate([wih[0:128].T, wih[128:256].T, padT(I["L0_attn_Bw"]), wih[256:384].T], 1)
    half_w = np.concatenate([whh[0:128].T, whh[128:256].T, whh[256:384].T, padT(I["L0_attn_A"]),
                             padT(I["L0_attn_Cw"]), I["L0_attn_proj_w"].T], 1)
    desc = np.tile(np.arange(8, 0, -1, dtype=f)[None], (P, 1))
    misc = np.concatenate([np.eye(P, dtype=f), np.triu(np.ones((P, P), f)), np.ones((P, P), f),
                           I["L0_attn_Dw"].T, desc, I["L0_ffn_Wr"], I["L0_attn_gate_w"].T], 1)
    bb = np.zeros((P, 1), f)
    bb[:64, 0] = I["L0_attn_Bb"]
    cols = np.concatenate([I["L0_attn_b_ih"].reshape(3, P).T, I["L0_attn_b_hh"].reshape(3, P).T, bb,
                           np.zeros((P, 1), f)], 1)
    rows = np.concatenate([I["L0_attn_Cb"], I["L0_attn_Db"], I["L0_attn_proj_b"], np.zeros(8, f),
                           I["L0_attn_gate_b"]])[None]
    b2b = np.zeros((16, 8, 16, P), f)
    for n in range(16):
        b2b[n, :, n, :] = I["L0_ffn_b2"]
    arrays = {
        "x": I["L0_attn_x"].reshape(NTOK, P), "gin_w": gin_w, "half_w": half_w, "misc_w": misc, "cols": cols,
        "rows": rows, "b2_blocks": b2b.reshape(P, 16 * P), "w1": I["L0_ffn_W1"],
        "b1": I["L0_ffn_b1"].reshape(E0 * FC, P).T, "w2": I["L0_ffn_W2"],
        "attn_w": np.concatenate([I["L1_attn_wq"].T, I["L1_attn_wk"].T, I["L1_attn_wv"].T,
                                  I["L1_attn_wo"].T.reshape(PAIRS, P, P).transpose(1, 0, 2).reshape(P, -1)], 1),
        "attn_cols": np.concatenate([I["L1_attn_bq"].reshape(PAIRS, P).T, I["L1_attn_bk"].reshape(PAIRS, P).T], 1),
        "attn_rows": np.concatenate([I["L1_attn_bv"], I["L1_attn_bo"]]),
        "router": I["L1_ffn_router_w"].T, "router_row": I["L1_ffn_expert_bias"][None],
        "w_gate": I["L1_ffn_w_gate"].transpose(2, 0, 1).reshape(P, -1),
        "w_down": I["L1_ffn_w_down"].reshape(E1 // 2, 2, P, F1).transpose(1, 3, 0, 2).reshape(P, -1),
        "shared_gate": I["L1_ffn_w_gate_shared"].T, "shared_down": I["L1_ffn_w_down_shared"].T,
        "jcols": np.arange(4 * P, dtype=f).reshape(P, 4), "sel_w": np.tile(np.eye(63, dtype=f)[31], (P, 1)),
    }
    arrays = {k: np.ascontiguousarray(v) for k, v in arrays.items()}
    nc = _bacc.Bacc("TRN2", target_bir_lowering=False, num_devices=1)
    aps = {k: nc.dram_tensor(k, v.shape, mybir.dt.from_np(v.dtype), kind="ExternalInput").ap()
           for k, v in arrays.items()}
    out = nc.dram_tensor("out", (NTOK, P), F32, kind="ExternalOutput").ap()
    build(nc, out=out, **aps)
    r = _run(nc, [arrays], core_ids=[0])
    return r.results[0]["out"].reshape(B, T, P)
```

```python
from contextlib import ExitStack

import numpy as np

import concourse.bass as bass
from concourse import mybir

ALU = mybir.AluOpType
ACT = mybir.ActivationFunctionType
F32 = mybir.dt.float32
BF16 = mybir.dt.bfloat16
I32 = mybir.dt.int32
F32R = mybir.dt.float32r
U8 = mybir.dt.uint8
AX_X = mybir.AxisListType.X

P = 128
B, T = 16, 256
NTOK = B * T
NT = NTOK // P
NG = NTOK // 512
E0, F0 = 8, 512
FC = F0 // P
CAP0 = int(NTOK * 1.25 / E0)
SLOTS0 = 2 * CAP0 * E0
UNITS0 = 2 * CAP0 // 256
STEPS_MOE = UNITS0 * E0 * 5
STEPS_BEFORE = (T - STEPS_MOE) // 8 * 4
EPS = 1e-5
HEADS, HD = 16, 64
PAIRS = HEADS // 2
E1, TOPK1, F1 = 160, 8, 64
SLOT_TILES = -(-(NTOK * TOPK1 // P + E1) // 8) * 8
SLOTS = SLOT_TILES * P
NBODY = SLOT_TILES // 8
HB = B // 2


class Count:

    def __init__(self, sem):
        self.sem, self.n = sem, 0

    def raised_by(self, ins):
        self.n += 1
        ins.then_inc(self.sem, 1)
        return self.n


def build(nc, x, gin_w, half_w, misc_w, cols, rows, b2, w1, b1, w2,
          attn_w, attn_cols, attn_rows, router, router_row, w_gate, w_down, shared_gate, shared_down,
          jcols, sel_w, out):
    with ExitStack() as ctx:
        def sb(name, shape, dt=F32):
            return ctx.enter_context(nc.sbuf_tensor(name, shape, dt))

        def bank(name):
            return ctx.enter_context(nc.psum_tensor(name, [P, 512], F32))

        def sem(name):
            return ctx.enter_context(nc.semaphore(name))

        x_tok = sb("x_tok", [P, NT, P])
        xn_tok = sb("xn_tok", [P, NT, P])
        xnT = sb("xnT", [P, NTOK])
        ln_sum = sb("ln_sum", [P, NT])
        ln_mean = sb("ln_mean", [P, NT])
        ln_sq = sb("ln_sq", [P, NT])
        ln_std = sb("ln_std", [P, NT])
        ln_rstd = sb("ln_rstd", [P, NT])
        eps_col = sb("eps_col", [P, 1])
        misc = sb("misc", [P, 610])
        ident, upper, ones = misc[:, 0:128], misc[:, 128:256], misc[:, 256:384]
        dwT, desc, rgT = misc[:, 384:512], misc[:, 512:520], misc[:, 520:530]
        slot_base = misc[:, 530:546]
        spare = misc[:, 546:610]
        rows_sb = sb("rows_sb", [1, 3 * 128 + 10])
        layer0 = ExitStack()

        def sb(name, shape, dt=F32, stack=layer0):
            return stack.enter_context(nc.sbuf_tensor(name, shape, dt))

        ginw = sb("ginw", [P, 4 * 128])
        halfw = sb("halfw", [P, 6 * 128])
        whr, whz, whn, aT, cwT, projT = (halfw[:, 128 * k:128 * k + 128] for k in range(6))
        cols_sb = sb("cols_sb", [P, 8])
        gin_bias = sb("gin_bias", [P, 4])
        gin = sb("gin", [P, 4, B, T])
        hist_g = sb("hist_g", [P, B, T + 1])
        hist_s = sb("hist_s", [P, B, T + 1])
        b2_sb = sb("b2_sb", [P, E0 * P])
        zeros = sb("zeros", [P, 1024])
        w1_sb = sb("w1_sb", [P, 2, F0])
        w2_sb = sb("w2_sb", [P, 2, FC, P])
        b1_sb = sb("b1_sb", [P, E0 * FC])
        h_sb = sb("h_sb", [P, 2, 256])
        slots0_x = sb("slots0_x", [P, 2, P])
        slots0_xT = sb("slots0_xT", [P, 256])
        slots0_y = sb("slots0_y", [P, 2, P])
        second = sb("second", [P, NT, P])
        slot_to = sb("slot_to", [P, NT, 2], I32)
        slot_from = sb("slot_from", [P, NT, 2], I32)
        w0 = sb("w0", [P, NT, 2])
        gate = sb("gate", [P, NT, 2])
        th_r = sb("th_r", [P, 16])
        th_zv = sb("th_zv", [P, 2, 16])
        cand = sb("cand", [P, 16])
        mixn = sb("mixn", [P, 16])
        pren = sb("pren", [P, 16])
        sumn = sb("sumn", [P, 16])
        zg = sb("zg", [P, 16])
        omz = sb("omz", [P, 16])
        newn = sb("newn", [P, 16])
        scr = hist_g[:, :, :].rearrange("p b t -> p (b t)")
        scr2 = hist_s[:, :, :].rearrange("p b t -> p (b t)")
        layer0.close()

        def sb(name, shape, dt=F32):
            return ctx.enter_context(nc.sbuf_tensor(name, shape, dt))

        def under(name, before, shape, dt):
            with ExitStack() as stack:
                if before:
                    stack.enter_context(nc.sbuf_tensor(name + "_before", [P, before], F32))
                return stack.enter_context(nc.sbuf_tensor(name, shape, dt))

        w_high1 = under("w_high1", NTOK, [P, 2 * HEADS * HD], F32R)
        gate1 = sb("gate1", [P, E1 * F1])
        down_stack = ExitStack()
        down1 = down_stack.enter_context(nc.sbuf_tensor("down1", [P, E1 // 2, P], F32))
        down_stack.close()
        comb = sb("comb", [P, NT, E1])
        place = sb("place", [P, NT, E1])
        w_high0 = under("w_high0", NTOK // 2, [P, 2 * HEADS * HD], F32R)
        att = sb("att", [P, NT, P])
        chosen = att[:, :, :].rearrange("p n d -> p (n d)")[:, 0:NT * E1 // 2].bitcast(BF16) \
            .rearrange("p (n e) -> p n e", e=E1)
        att_flat = att[:, :, :].rearrange("p n d -> p (n d)")
        w_qk_high = [w_high0[:, :], w_high1[:, :]]
        hsT = gate1[:, 0:NTOK]
        w_low = under("w_low", 0, [P, 2 * HEADS * HD], F32R)
        aw = sb("aw", [P, 4, HEADS * HD])
        acols = sb("acols", [P, 2, PAIRS])
        arows = sb("arows", [P, HEADS * HD + P])
        sg_w = sb("sg_w", [P, F1])
        sd_w = sb("sd_w", [F1, P])
        place8 = sb("place8", [P, NT, TOPK1])
        slot = sb("slot", [P, NT, TOPK1], I32)
        w8 = sb("w8", [P, NT, TOPK1])
        top8 = sb("top8", [P, NT, TOPK1])
        pair_row = sb("pair_row", [1, 4 * P], U8)
        of_pair = sb("of_pair", [P, 4 * P])
        jcol = sb("jcol", [P, 4])
        tile_e = sb("tile_e", [P, 4])
        tile_par = sb("tile_par", [P, 4])
        tile_i = sb("tile_i", [P, 4], I32)
        tile_u8 = sb("tile_u8", [P, 4], U8)
        rows_g = sb("rows_g", [P, 16, P])
        small = rows_g[:, :, :].rearrange("p n d -> p (n d)")
        rT, cnt_f, cnt_inc = (small[:, E1 * k:E1 * k + E1] for k in range(3))
        cnt_i = small[:, 3 * E1:4 * E1].bitcast(I32)
        rrow, offs = small[0:1, 4 * E1:5 * E1], small[:, 5 * E1:6 * E1]
        junk = small[:, 6 * E1:8 * E1].rearrange("p (k e) -> p k e", e=E1)
        par_row = small[:, 8 * E1:8 * E1 + 4 * P]
        bias_b = par_row[0:65, 0:E1 // 2].bitcast(BF16)
        bf = small[:, 8 * E1 + 4 * P:].bitcast(BF16)
        upper_b, ones_b, sel_b, tile_tot = bf[:, 0:P], bf[:, P:2 * P], bf[:, 2 * P:2 * P + 63], bf[0:NT, 320:320 + E1]
        attn_stack = ExitStack()

        def sb(name, shape, dt=F32, stack=attn_stack):
            return stack.enter_context(nc.sbuf_tensor(name, shape, dt))

        xb = sb("xb", [P, 2 * P])
        xr = sb("xr", [P, 2, T], F32R)
        qT = sb("qT", [P, 2, 2, T], F32R)
        kT = sb("kT", [P, 2, 2, T], F32R)
        v_sb = sb("v_sb", [P, 2, 2, P])
        probs = sb("probs", [P, 2, 2, T])
        probsT = sb("probsT", [P, 2, 2, T])
        negmax = sb("negmax", [P, 2, 2])
        sums = sb("sums", [P, 4, 2, 2])
        rsums = sb("rsums", [P, 2, 2])
        ctx_sb = sb("ctx_sb", [P, 2, P])
        ctxT = sb("ctxT", [P, 2 * P])
        attn_stack.close()

        def sb(name, shape, dt=F32):
            return ctx.enter_context(nc.sbuf_tensor(name, shape, dt))

        slots_x = sb("slots_x", [P, 2, 512])
        slots_xT = sb("slots_xT", [P, 2, 512])
        hid = sb("hid", [P, 2, 512])
        hidT = sb("hidT", [P, 2, 512])
        slots_y = sb("slots_y", [P, 2, 512])

        ps_rec = [bank("ps_rec0"), bank("ps_rec1")]
        ps_up = [bank("ps_up0"), bank("ps_up1")]
        ps_y = ctx.enter_context(nc.psum_tensor("ps_y", [P, 2, 512], F32))
        ps_t = [bank("ps_t0"), bank("ps_t1")]
        ps_r, ps_n, ps_zv, ps_rows = ps_rec[0], ps_rec[1], ps_t[0], ps_t[1]
        ps_qk, ps_v, ps_s, ps_ctx, ps_o = ps_rec[0], ps_rec[1], ps_up, ps_t[0], ps_t[1]

        x_loaded = [sem(f"x_loaded{c}") for c in range(4)]
        consts_loaded = sem("consts_loaded")
        w1_loaded = [sem("w1_loaded0"), sem("w1_loaded1")]
        w2_loaded = [sem("w2_loaded0"), sem("w2_loaded1")]
        dve_done = sem("dve_done")
        centred = sem("centred")
        squared = sem("squared")
        var_ready = sem("var_ready")
        std_ready = sem("std_ready")
        xn_ready = sem("xn_ready")
        turned = sem("turned")
        xnT_ready = sem("xnT_ready")
        gin_mm = sem("gin_mm")
        gin_act = sem("gin_act")
        gin_dve = sem("gin_dve")
        biases_ready = sem("biases_ready")
        bias_rows = sem("bias_rows")
        zeros_ready = sem("zeros_ready")
        logits_ready = sem("logits_ready")
        shifted = sem("shifted")
        exps_ready = sem("exps_ready")
        onehot_ready = sem("onehot_ready")
        ranks_ready = sem("ranks_ready")
        slots0_ready = sem("slots0_ready")
        zeroed0 = sem("zeroed0")
        first_scaled = sem("first_scaled")
        scattered0 = sem("scattered0")
        gathered0 = sem("rows0_gathered")
        rnn_ready = sem("rnn_ready")
        ssm_ready = sem("ssm_ready")
        r_done = sem("r_done")
        n_done = sem("n_done")
        zv_done = sem("zv_done")
        thr_ready = sem("thr_ready")
        thzv_ready = sem("thzv_ready")
        sumn_ready = sem("sumn_ready")
        cand_ready = sem("cand_ready")
        x0_in = sem("x0_in")
        x0_turned = sem("x0_turned")
        x0T_ready = sem("x0T_ready")
        y0_out = sem("y0_out")
        y0_stored = sem("y0_stored")
        up_ready = sem("up_ready")
        gelu_ready = sem("gelu_ready")
        down_done = sem("down_done")
        dve_step = sem("dve_step")
        silu_th = sem("silu_th")
        acc_final = sem("acc_final")
        y_ready = sem("y_ready")
        y_scaled = sem("y_scaled")
        y_used = sem("y_used")
        x1_ready = sem("x1_ready")
        stored = sem("stored")
        table_ready = sem("table_ready")
        attn_loaded = sem("attn_loaded")
        experts_loaded = sem("experts_loaded")
        probs1_mm = sem("probs1_mm")
        probs1_ready = sem("probs1_ready")
        chosen_ready = sem("chosen_ready")
        counts_mm = sem("counts_mm")
        tot_ready = sem("tot_ready")
        place_mm = sem("place_mm")
        place_ready = sem("place_ready")
        slots_ready = sem("slots_ready")
        scattered = sem("scattered")
        zeroed = sem("zeroed")
        table_stored = sem("table_stored")
        table_loaded = sem("table_loaded")
        bias_split = sem("bias_split")
        top_found = sem("top_found")
        marked = sem("marked")
        place_read = sem("place_read")
        xb_ready = sem("xb_ready")
        wq_scaled = sem("wq_scaled")
        w_split = sem("w_split")
        xr_high = sem("xr_high")
        xr_ready = sem("xr_ready")
        qk_high = sem("qk_high")
        q_mm = sem("q_mm")
        qk_ready = sem("qk_ready")
        v_mm = sem("v_mm")
        v_ready = sem("v_ready")
        scores_done = sem("scores_done")
        max_ready = sem("max_ready")
        exp_done = sem("exp_done")
        tr_done = sem("tr_done")
        pt_copied = [sem("pt_copied0"), sem("pt_copied1")]
        pv_done = sem("pv_done")
        normed = sem("normed")
        ctxt_done = sem("ctxt_done")
        ctxT_ready = sem("ctxT_ready")
        out_done = sem("out_done")
        o_evicted = sem("o_evicted")
        weights_done = sem("weights_done")
        acc1_used = sem("acc1_used")
        shared_mm = sem("shared_mm")
        shared_ready = sem("shared_ready")
        shared_y = sem("shared_y")
        y1_ready = sem("y1_ready")
        y1_silu = sem("y1_silu")
        y1_done = sem("y1_done")
        gathered = [sem(f"gathered{i}") for i in range(16)]
        x_in, x_turned, xT_ready, up1_done, silu1_done, h_turned, hT_ready, down1_done, y_out, y_stored = (
            [sem(f"{name}{h}") for h in range(2)] for name in
            ("x_in", "x_turned", "xT_ready", "up1_done", "silu1_done", "h_turned", "hT_ready",
             "down1_done", "y_out", "y_stored"))
        recip_done = sem("recip_done")

        xs_dram = nc.dram_tensor("xs_dram", (SLOTS, P), F32, kind="Internal").ap()
        ys_dram = nc.dram_tensor("ys_dram", (SLOTS, P), F32, kind="Internal").ap()
        xs0_dram = nc.dram_tensor("xs0_dram", (SLOTS0 + 2 * NTOK, P), F32, kind="Internal").ap()
        ys0_dram = nc.dram_tensor("ys0_dram", (SLOTS0 + P, P), F32, kind="Internal").ap()
        pair_dram = nc.dram_tensor("pair_dram", (4 * P,), U8, kind="Internal").ap()
        par_dram = nc.dram_tensor("par_dram", (4 * P,), F32, kind="Internal").ap()

        block = ctx.enter_context(nc.Block())

        @block.sync
        def _(sp):
            xd = x.rearrange("(n p) d -> p n d", p=P)
            for c in range(4):
                sp.dma_start(x_tok[:, 8 * c:8 * c + 8, :], xd[:, 8 * c:8 * c + 8, :]).then_inc(x_loaded[c], 16)
            sp.wait_ge(zeros_ready, 1)
            with sp.Fori(0, SLOTS0 // 1024) as i:
                sp.dma_start(xs0_dram[bass.ds(i * 1024, 1024), :].rearrange("(p r) d -> p (r d)", p=P), zeros[:, :]) \
                    .then_inc(zeroed0, 16)
            sp.dma_start(ys0_dram[SLOTS0:, :], zeros[:, 0:P]).then_inc(zeroed0, 16)
            with sp.Fori(0, SLOTS // 1024) as i:
                sp.dma_start(xs_dram[bass.ds(i * 1024, 1024), :].rearrange("(p r) d -> p (r d)", p=P), zeros[:, :]) \
                    .then_inc(zeroed, 16)

            def load_unit(g):
                sp.dma_start(slots0_x[:, :, :], xs0_dram[bass.ds(g * 256, 256), :].rearrange("(s p) d -> p s d", p=P)) \
                    .then_inc(x0_in, 16)

            sp.wait_ge(scattered0, 16 * NT * 2)
            load_unit(0)
            sp.sem_inc(y0_stored, 16)
            with sp.Fori(0, UNITS0 * E0) as g:
                sp.wait_ge(x0_turned, g + 1)
                load_unit((g + 1) % (UNITS0 * E0))
                sp.wait_ge(y0_out, g + 2)
                sp.dma_start(ys0_dram[bass.ds(g * 256, 256), :].rearrange("(s p) d -> p s d", p=P),
                             slots0_y[:, :, :]).then_inc(y0_stored, 16)
            sp.wait_ge(x1_ready, NG)
            sp.wait_ge(x0_in, 16 * (UNITS0 * E0 + 1))
            for dst, src in ((rT, router), (rrow, router_row), (sg_w[:, :], shared_gate),
                             (sd_w[:, :], shared_down), (aw[:, :, :], attn_w.rearrange("p (k n) -> p k n", k=4)),
                             (acols[:, :, :], attn_cols.rearrange("p (k n) -> p k n", k=2)),
                             (arows[:, :], attn_rows.partition_broadcast(P)), (jcol[:, :], jcols),
                             (cnt_f[:, 0:63], sel_w)):
                sp.dma_start(dst, src).then_inc(attn_loaded, 16)
            sp.dma_start(gate1[:, :], w_gate).then_inc(experts_loaded, 16)
            sp.wait_ge(table_ready, 2)
            sp.dma_start(pair_dram.rearrange("(p c) -> p c", p=P), tile_u8[:, :]).then_inc(table_stored, 16)
            sp.dma_start(par_dram.rearrange("(p c) -> p c", p=P), tile_par[:, :]).then_inc(table_stored, 16)
            sp.wait_ge(table_stored, 32)
            sp.dma_start(pair_row[:, :], pair_dram.rearrange("(a n) -> a n", a=1)).then_inc(table_loaded, 16)
            sp.dma_start(par_row, par_dram.partition_broadcast(P)).then_inc(table_loaded, 16)
            sp.wait_ge(weights_done, 2 * 128)
            sp.dma_start(down1[:, :, :], w_down.rearrange("p (k n) -> p k n", n=P)).then_inc(experts_loaded, 16)

            def load_slots(it, h):
                sp.dma_start(slots_x[:, h, :].rearrange("p (s d) -> p s d", d=P),
                             xs_dram[bass.ds(it * 1024 + h * 512, 512), :].rearrange("(s p) d -> p s d", p=P)) \
                    .then_inc(x_in[h], 16)

            sp.wait_ge(scattered, 16 * NT * TOPK1)
            sp.wait_ge(o_evicted, HB)
            for h in range(2):
                load_slots(0, h)
                sp.wait_ge(x_turned[h], 1)
                load_slots(1, h)
                sp.sem_inc(y_stored[h], 16)
            with sp.Fori(0, NBODY) as it:
                for h in range(2):
                    sp.wait_ge(x_turned[h], it + 2)
                    load_slots((it + 2) % NBODY, h)
                for h in range(2):
                    sp.wait_ge(y_out[h], it + 2)
                    sp.dma_start(ys_dram[bass.ds(it * 1024 + h * 512, 512), :].rearrange("(s p) d -> p s d", p=P),
                                 slots_y[:, h, :].rearrange("p (s d) -> p s d", d=P)).then_inc(y_stored[h], 16)
            outd = out.rearrange("(n p) d -> p n d", p=P)
            for g in range(NG):
                sp.wait_ge(y1_done, g + 1)
                sp.dma_start(outd[:, 4 * g:4 * g + 4, :], x_tok[:, 4 * g:4 * g + 4, :]).then_inc(stored, 16)
            sp.wait_ge(stored, 16 * NG)
            sp.wait_ge(zeroed, 16 * (SLOTS // 1024))
            for h in range(2):
                sp.wait_ge(x_in[h], 16 * (NBODY + 2))
                sp.wait_ge(y_stored[h], 16 * (NBODY + 1))

        @block.gpsimd
        def _(pool):
            nc.gpsimd.memset(zeros[:, :], 0.0).then_inc(zeros_ready, 1)

            def load_expert(e):
                pool.dma_start(w1_sb[:, e % 2, :], w1[e]).then_inc(w1_loaded[e % 2], 16)
                pool.dma_start(w2_sb[:, e % 2, :, :], w2[e].rearrange("(c p) d -> p c d", p=P)) \
                    .then_inc(w2_loaded[e % 2], 16)

            load_expert(0)
            load_expert(1)
            pool.wait_ge(slots0_ready, 1)
            pool.wait_ge(zeroed0, 16 * (SLOTS0 // 1024 + 1))
            for n in range(NT):
                for k in range(2):
                    nc.gpsimd.indirect_dma_start(xs0_dram, bass.IndirectOffsetOnAxis(ap=slot_to[:, n, k:k + 1], axis=0),
                                                 xn_tok[:, n, :], None).then_inc(scattered0, 16)
            for e in range(2, E0):
                pool.wait_ge(down_done, 4 * UNITS0 * (e - 1))
                load_expert(e)
            pool.wait_ge(scattered0, 16 * NT * 2)
            pool.wait_ge(y0_stored, 16 * (UNITS0 * E0 + 1))
            for n in range(NT):
                for k, dst in enumerate((xn_tok, second)):
                    nc.gpsimd.indirect_dma_start(dst[:, n, :], None, ys0_dram,
                                                 bass.IndirectOffsetOnAxis(ap=slot_from[:, n, k:k + 1], axis=0)) \
                        .then_inc(gathered0, 16)
            pool.wait_ge(slots_ready, 1)
            pool.wait_ge(zeroed, 16 * (SLOTS // 1024))
            for n in range(NT):
                for k in range(TOPK1):
                    nc.gpsimd.indirect_dma_start(xs_dram, bass.IndirectOffsetOnAxis(ap=slot[:, n, k:k + 1], axis=0),
                                                 xn_tok[:, n, :], None).then_inc(scattered, 16)
            for h in range(2):
                pool.wait_ge(y_stored[h], 16 * (NBODY + 1))
            for i in range(NT * TOPK1):
                if i >= 16:
                    pool.wait_ge(acc1_used, i - 15)
                nc.gpsimd.indirect_dma_start(rows_g[:, i % 16, :], None, ys_dram,
                                             bass.IndirectOffsetOnAxis(
                                                 ap=slot[:, i // TOPK1, i % TOPK1:i % TOPK1 + 1], axis=0)) \
                    .then_inc(gathered[i % 16], 16)

        @block.scalar
        def _(act):
            act.dma_start(misc[:, :], misc_w).then_inc(consts_loaded, 16)
            act.dma_start(ginw[:, :], gin_w).then_inc(consts_loaded, 16)
            act.dma_start(halfw[:, :], half_w).then_inc(consts_loaded, 16)
            act.dma_start(cols_sb[:, :], cols).then_inc(consts_loaded, 16)
            act.dma_start(rows_sb[:, :], rows).then_inc(consts_loaded, 16)
            act.dma_start(b2_sb[:, :], b2.partition_broadcast(P)).then_inc(consts_loaded, 16)
            act.dma_start(b1_sb[:, :], b1).then_inc(consts_loaded, 16)

            def layer_norm(layer, scratch):
                for c in range(4):
                    act.wait_ge(centred, 4 * layer + c + 1)
                    nc.scalar.activation(scratch[:, 1024 * c:1024 * c + 1024],
                                         xn_tok[:, 8 * c:8 * c + 8, :].rearrange("p n d -> p (n d)"),
                                         ACT.Square).then_inc(squared, 1)
                act.wait_ge(var_ready, layer + 1)
                nc.scalar.activation(ln_std[:, :], ln_sq[:, :], ACT.Sqrt, bias=eps_col[:, :], scale=1.0 / P) \
                    .then_inc(std_ready, 1)

            layer_norm(0, scr2)
            for g in range(NG):
                act.wait_ge(turned, g + 1)
                nc.scalar.copy(xnT[:, 512 * g:512 * g + 512], ps_t[g % 2][:, :]).then_inc(xnT_ready, 1)
                if g == 0:
                    act.wait_ge(biases_ready, 1)
                for k in range(2):
                    act.wait_ge(gin_mm, 4 * g + k + 1)
                    nc.scalar.activation(gin[:, k, 2 * g:2 * g + 2, :],
                                         ps_up[k][:, :].rearrange("p (b t) -> p b t", b=2),
                                         ACT.Identity, bias=gin_bias[:, k:k + 1]).then_inc(gin_act, 1)
            act.wait_ge(shifted, 1)
            nc.scalar.activation(scr[:, 0:256], scr[:, 0:256], ACT.Exp).then_inc(exps_ready, 1)
            nc.scalar.activation(gate[:, :, :], gate[:, :, :], ACT.Tanh, scale=0.5).then_inc(exps_ready, 1)

            def step(t):
                act.wait_ge(r_done, t + 1)
                nc.scalar.activation(th_r[:, :], ps_r[:, 0:16], ACT.Tanh, scale=0.5).then_inc(thr_ready, 1)
                act.wait_ge(zv_done, t + 1)
                nc.scalar.activation(th_zv[:, :, :].rearrange("p k b -> p (k b)"), ps_zv[:, 0:32], ACT.Tanh,
                                     scale=0.5).then_inc(thzv_ready, 1)
                act.wait_ge(sumn_ready, t + 1)
                nc.scalar.activation(cand[:, :], sumn[:, :], ACT.Tanh, scale=0.5).then_inc(cand_ready, 1)

            def rows_out(g):
                act.wait_ge(x0_turned, g + 1)
                nc.scalar.copy(slots0_xT[:, :], ps_rows[:, 0:256]).then_inc(x0T_ready, 1)

            def unit(e, g):
                for j in range(5):
                    step(STEPS_BEFORE + g * 5 + j)
                    if j < 4:
                        act.wait_ge(up_ready, g * 4 + j + 1)
                        nc.scalar.activation(h_sb[:, j % 2, :], ps_up[j % 2][:, 0:256], ACT.Gelu,
                                             bias=b1_sb[:, bass.ds(e * 4 + j, 1)]).then_inc(gelu_ready, 1)
                    else:
                        rows_out(g + 1)

            act.wait_ge(consts_loaded, 16 * 7)
            nc.scalar.activation(h_sb[:, 0, 0:16], ident[:, 0:16], ACT.Gelu)
            with act.Fori(0, STEPS_BEFORE // 4) as u:
                for j in range(4):
                    step(u * 4 + j)
            rows_out(0)
            with act.Fori(0, E0) as e:
                with act.Fori(0, UNITS0) as i:
                    unit(e, e * UNITS0 + i)
            with act.Fori((STEPS_BEFORE + STEPS_MOE) // 4, T // 4) as u:
                for j in range(4):
                    step(u * 4 + j)
            for n in range(NT):
                act.wait_ge(y_ready, n + 1)
                nc.scalar.mul(gin[:, 1, n // 2, 128 * (n % 2):128 * (n % 2) + 128], ps_up[n % 2][:, 0:128],
                              gate[:, n, 0:1]).then_inc(y_scaled, 1)
            for c in range(4):
                act.wait_ge(acc_final, c + 1)
                nc.scalar.activation(gin[:, 0, :, :].rearrange("p b t -> p (b t)")[:, 1024 * c:1024 * c + 1024],
                                     xn_tok[:, 8 * c:8 * c + 8, :].rearrange("p n d -> p (n d)"), ACT.Tanh, scale=0.5) \
                    .then_inc(silu_th, 1)

            layer_norm(1, att_flat)
            for g in range(NG):
                act.wait_ge(turned, NG + g + 1)
                nc.scalar.copy(xnT[:, 512 * g:512 * g + 512], ps_t[g % 2][:, :]).then_inc(xnT_ready, 1)
            act.wait_ge(attn_loaded, 16 * 9)
            nc.scalar.mul(acols[:, 0, :], acols[:, 0, :], HD ** -0.5).then_inc(wq_scaled, 1)
            nc.scalar.mul(aw[:, 0, :], aw[:, 0, :], HD ** -0.5).then_inc(wq_scaled, 1)
            for n in range(NT):
                act.wait_ge(probs1_mm, n + 1)
                nc.scalar.activation(comb[:, n, :], ps_rec[n % 2][:, 0:E1], ACT.Sigmoid).then_inc(probs1_ready, 1)

            def copy_inputs(b, x):
                nc.scalar.activation(xb[:, :], xnT[:, bass.ds((b % B) * T, T)], ACT.Identity).then_inc(xb_ready, 1)

            def inputs_high(b, x):
                nc.scalar.activation(xr[:, 0, :], xnT[:, bass.ds((b % B) * T, T)], ACT.Identity).then_inc(xr_high, 1)

            def qk_out(p, j, x, waits):
                act.wait_ge(q_mm, p + 1 + x)
                if waits:
                    act.wait_ge(scores_done, p * 2 - 2)
                nc.scalar.activation(qT[:, j % 2, 0, :], ps_qk[:, 0:T], ACT.Identity, bias=acols[:, 0, j:j + 1])
                nc.scalar.activation(kT[:, j % 2, 0, :], ps_qk[:, T:2 * T], ACT.Identity, bias=acols[:, 1, j:j + 1]) \
                    .then_inc(qk_high, 1)

            def probs_out(h, waits):
                act.wait_ge(tr_done, h + 1)
                if waits:
                    act.wait_ge(pv_done, h - 1)
                nc.scalar.copy(probsT[:, 1, :, :].rearrange("p c t -> p (c t)"), ps_y[:, 1, :]) \
                    .then_inc(pt_copied[1], 1)

            def ctx_out(p, waits):
                act.wait_ge(ctxt_done, p + 1)
                if waits:
                    act.wait_ge(out_done, p)
                nc.scalar.copy(ctxT[:, :], ps_v[:, T:2 * T]).then_inc(ctxT_ready, 1)

            def attend(b, x, first):
                for j in range(PAIRS):
                    p = b * PAIRS + j
                    for a in range(2):
                        h = p * 2 + a
                        act.wait_ge(max_ready, h + 1)
                        if not (first and j == 0):
                            act.wait_ge(tr_done, h - 1)
                        for i in range(2):
                            nc.scalar.activation(probs[:, a, i, :], ps_s[a][:, T * i:T * i + T], ACT.Exp,
                                                 bias=negmax[:, a, i:i + 1],
                                                 accum_out=sums[:, j % 4, i, a:a + 1]).then_inc(exp_done, 1)
                        if a == 0:
                            if not (first and j == 0):
                                probs_out(h - 1, not (first and j == 1))
                            if j == PAIRS - 1:
                                copy_inputs(b + 1, x)
                            if not (first and j < 2):
                                ctx_out(p - 2, not (first and j == 2))
                            qk_out(p + 1, (j + 1) % PAIRS, x, not (first and j == 0))
                        elif j == PAIRS - 2:
                            inputs_high(b + 1, x)

            def attend_half(b0, x):
                if x:
                    for h in range(2):
                        act.wait_ge(x_in[h], 16 * (NBODY + 2))
                        act.wait_ge(y_stored[h], 16 * (NBODY + 1))
                inputs_high(b0, x)
                if x:
                    act.wait_ge(q_mm, b0 * PAIRS + 1 + x)
                    nc.scalar.copy(xb[:, :], xnT[:, T * b0:T * b0 + T]).then_inc(xb_ready, 1)
                else:
                    copy_inputs(0, 0)
                qk_out(b0 * PAIRS, 0, x, False)
                attend(b0, x, True)
                with act.Fori(b0 + 1, b0 + HB) as b:
                    attend(b, x, False)
                probs_out((b0 + HB) * HEADS - 1, True)
                for p in (b0 * PAIRS + HB * PAIRS - 2, b0 * PAIRS + HB * PAIRS - 1):
                    ctx_out(p, True)

            attend_half(0, 0)

            for h in range(2):
                act.sem_inc(silu1_done[h], 1)
            act.sem_inc(y_out[0], 1)

            def xT_out(it, h):
                act.wait_ge(x_turned[h], it + 1)
                nc.scalar.copy(slots_xT[:, h, :], ps_rec[h][:, :]).then_inc(xT_ready[h], 1)

            def silu(it, h):
                act.wait_ge(up1_done[h], it + 1)
                act.wait_ge(h_turned[h], it + 1)
                nc.scalar.activation(hid[:, h, :], ps_up[h][:, :], ACT.Silu).then_inc(silu1_done[h], 1)

            for h in range(2):
                xT_out(0, h)
            nc.scalar.activation(ln_std[:, 0:1], ln_std[:, 0:1], ACT.Silu)
            with act.Fori(0, NBODY) as it:
                for h in range(2):
                    silu(it, h)
                for h in range(2):
                    xT_out(it + 1, h)
                act.wait_ge(down1_done[0], it + 1)
                act.wait_ge(y_stored[0], 16 * (it + 1))
                nc.scalar.copy(slots_y[:, 0, :], ps_t[0][:, :]).then_inc(y_out[0], 1)

            for g in range(NG):
                act.wait_ge(shared_mm, g + 1)
                nc.scalar.activation(hsT[0:F1, 512 * g:512 * g + 512], ps_y[0:F1, g % 2, :], ACT.Silu) \
                    .then_inc(shared_ready, 1)
            attend_half(HB, 1)
            for g in range(NG):
                act.wait_ge(y1_ready, g + 1)
                nc.scalar.activation(xn_tok[:, 4 * g:4 * g + 4, :], xn_tok[:, 4 * g:4 * g + 4, :], ACT.Silu) \
                    .then_inc(y1_silu, 1)

        @block.tensor
        def _(pe):
            pe.wait_ge(consts_loaded, 16 * 7)

            def turn(g, layer=0):
                pe.wait_ge(xn_ready, 4 * layer + g // 2 + 1)
                if g >= 2:
                    pe.wait_ge(xnT_ready, NG * layer + g - 1)
                for s in range(4):
                    last = nc.tensor.transpose(ps_t[g % 2][:, 128 * s:128 * s + 128], xn_tok[:, 4 * g + s, :], ident)
                last.then_inc(turned, 1)

            turn(0)
            for g in range(NG):
                if g + 1 < NG:
                    turn(g + 1)
                pe.wait_ge(xnT_ready, g + 1)
                for k, dst in enumerate((ps_up[0][:, :], ps_up[1][:, :], ps_y[:, 0, :], ps_y[:, 1, :])):
                    if g:
                        pe.wait_ge(gin_act if k < 2 else gin_dve, 2 * (g - 1) + k % 2 + 1)
                    nc.tensor.matmul(dst, ginw[:, 128 * k:128 * k + 128], xnT[:, 512 * g:512 * g + 512],
                                     start=True, stop=True).then_inc(gin_mm, 1)
                for s in range(4):
                    n = 4 * g + s
                    nc.tensor.matmul(ps_rec[0][:, 10 * n:10 * n + 10], xnT[:, 128 * n:128 * n + 128], rgT,
                                     start=True, stop=False)
                    last = nc.tensor.matmul(ps_rec[0][:, 10 * n:10 * n + 10], ones[0:1, :], rows_sb[0:1, 384:394],
                                            start=False, stop=True)
            last.then_inc(logits_ready, 1)
            pe.wait_ge(onehot_ready, 1)
            nc.tensor.matmul(ps_rec[1][:, :], upper, scr[:, 1024:1536], start=True, stop=True).then_inc(ranks_ready, 1)
            nc.tensor.matmul(ps_rec[0][:, :], ones, scr[:, 1024:1536], start=True, stop=True).then_inc(ranks_ready, 1)
            warm_b = zeros[:, :].bitcast(BF16)

            def keep_warm(n):
                for _ in range(n):
                    nc.tensor.matmul(ps_y[:, 1, :], warm_b[:, 0:P], warm_b[:, 0:512], start=True, stop=True)

            def input_r(t):
                nc.tensor.matmul(ps_r[:, 0:16], ident, gin[:, 0, :, t], start=True, stop=False, skip_group_check=True)

            def input_zv(t):
                nc.tensor.matmul(ps_zv[:, 0:32], ident, gin[:, 1:3, :, t], start=True, stop=False,
                                 skip_group_check=True)

            def step(t, early=None, late=None):
                pe.wait_ge(rnn_ready, t + 1)
                nc.tensor.matmul(ps_r[:, 0:16], whr, hist_g[:, :, t], start=False, stop=True,
                                 skip_group_check=True).then_inc(r_done, 1)
                nc.tensor.matmul(ps_n[:, 0:16], whn, hist_g[:, :, t], start=True, stop=True).then_inc(n_done, 1)
                nc.tensor.matmul(ps_zv[:, 0:16], whz, hist_g[:, :, t], start=False, stop=False, skip_group_check=True)
                pe.wait_ge(ssm_ready, t + 1)
                nc.tensor.matmul(ps_zv[:, 16:32], aT, hist_s[:, :, t], start=False, stop=True,
                                 skip_group_check=True).then_inc(zv_done, 1)
                if early:
                    early()
                keep_warm(4 if early is None else 2)
                pe.wait_ge(thr_ready, t + 1)
                input_r((t + 1) % T)
                if late:
                    late()
                keep_warm(2 if early is None else 1)
                pe.wait_ge(thzv_ready, t + 1)
                pe.wait_ge(ssm_ready, t + 2)
                input_zv((t + 1) % T)

            def turn_rows(g):
                pe.wait_ge(x0_in, 16 * (g + 1))
                if not isinstance(g, int):
                    pe.wait_ge(x0T_ready, g)
                for s in range(2):
                    last = nc.tensor.transpose(ps_rows[:, P * s:P * s + P], slots0_x[:, s, :], ident)
                last.then_inc(x0_turned, 1)

            def up(g, ep, wbuf, j):
                if j == 0:
                    pe.wait_ge(x0T_ready, g + 1)
                    pe.wait_ge(w1_loaded[wbuf], 16 * (ep + 1))
                nc.tensor.matmul(ps_up[j % 2][:, 0:256], w1_sb[:, wbuf, P * j:P * j + P], slots0_xT[:, :],
                                 start=True, stop=True).then_inc(up_ready, 1)

            def down(g, ep, wbuf, j):
                pe.wait_ge(gelu_ready, g * 4 + j + 1)
                if j == 0:
                    pe.wait_ge(w2_loaded[wbuf], 16 * (ep + 1))
                    pe.wait_ge(y0_out, g + 1)
                for s in range(2):
                    last = nc.tensor.matmul(ps_y[:, 0, P * s:P * s + P], h_sb[:, j % 2, P * s:P * s + P],
                                            w2_sb[:, wbuf, j, :], start=(j == 0 and s == 0), stop=(j == 3),
                                            skip_group_check=True)
                last.then_inc(down_done, 1)

            def unit(g, ep, wbuf):
                for j in range(5):
                    step(STEPS_BEFORE + g * 5 + j,
                         (lambda: up(g, ep, wbuf, j)) if j < 4 else (lambda: turn_rows(g + 1)),
                         (lambda: down(g, ep, wbuf, j - 1)) if j else None)

            pe.wait_ge(slots0_ready, 1)
            pe.wait_ge(gin_act, 2 * NG)
            pe.wait_ge(gin_dve, 2 * NG)
            pe.wait_ge(rnn_ready, 1)
            pe.wait_ge(zeros_ready, 1)
            input_r(0)
            input_zv(0)
            keep_warm(16)
            with pe.Fori(0, STEPS_BEFORE // 4) as u:
                for j in range(4):
                    step(u * 4 + j)
            turn_rows(0)
            with pe.Fori(0, E0 // 2) as ep:
                for half in range(2):
                    with pe.Fori(0, UNITS0) as i:
                        unit((ep * 2 + half) * UNITS0 + i, ep, half)
            with pe.Fori((STEPS_BEFORE + STEPS_MOE) // 4, T // 4) as u:
                for j in range(4):
                    step(u * 4 + j)
            pe.wait_ge(rnn_ready, T + 1)
            pe.wait_ge(ssm_ready, T + 1)
            pe.wait_ge(x0T_ready, UNITS0 * E0 + 1)
            pe.wait_ge(bias_rows, 1)
            for n in range(NT):
                b, h = n // 2, n % 2
                if n >= 2:
                    pe.wait_ge(y_scaled, n - 1)
                    pe.wait_ge(y_used, n - 1)
                nc.tensor.matmul(ps_up[n % 2][:, 0:128], xnT[:, 128 * n:128 * n + 128], dwT, start=True, stop=False)
                nc.tensor.matmul(ps_up[n % 2][:, 0:128], hist_s[:, b, 1 + 128 * h:129 + 128 * h], cwT,
                                 start=False, stop=True)
                nc.tensor.matmul(ps_t[n % 2][:, 0:128], hist_g[:, b, 1 + 128 * h:129 + 128 * h], projT,
                                 start=True, stop=False)
                nc.tensor.matmul(ps_t[n % 2][:, 0:128], ones[0:1, :], rows_sb[0:1, 256:384],
                                 start=False, stop=True).then_inc(y_ready, 1)

            for g in range(NG):
                turn(g, 1)
            pe.wait_ge(attn_loaded, 16 * 9)
            pe.wait_ge(bias_split, 1)
            for n in range(NT):
                pe.wait_ge(xnT_ready, NG + n // 4 + 1)
                if n >= 2:
                    pe.wait_ge(probs1_ready, n - 1)
                nc.tensor.matmul(ps_rec[n % 2][:, 0:E1], xnT[:, P * n:P * n + P], rT, start=True, stop=False)
                nc.tensor.matmul(ps_rec[n % 2][:, 0:E1], ones_b[0:65, :], bias_b[0:65, :], start=False, stop=True) \
                    .then_inc(probs1_mm, 1)
            for n in range(NT):
                pe.wait_ge(chosen_ready, n // 8 + 1)
                last = nc.tensor.matmul(ps_up[0][:, 0:E1], ones_b, chosen[:, n, :], start=(n == 0), stop=(n == NT - 1))
            last.then_inc(counts_mm, 1)
            for n in range(NT):
                last = nc.tensor.matmul(ps_up[1][0:NT, 0:E1], sel_b[:, 31 - n:63 - n], chosen[:, n, :],
                                        start=(n == 0), stop=(n == NT - 1))
            last.then_inc(counts_mm, 1)
            pe.wait_ge(tot_ready, 1)
            pe.wait_ge(probs1_ready, NT)
            for n in range(NT):
                dst = (ps_rec[n % 2])[:, 0:E1]
                if n >= 2:
                    pe.wait_ge(place_read, n - 1)
                if n:
                    nc.tensor.matmul(dst, upper_b[0:NT, n - 1:n].to_broadcast([NT, P]), tile_tot,
                                     start=True, stop=False)
                nc.tensor.matmul(dst, upper_b, chosen[:, n, :], start=(n == 0), stop=True).then_inc(place_mm, 1)
            pe.wait_ge(place_read, NT)

            def three_passes(dst, left, right):
                for k, (a_, b_) in enumerate(((0, 0), (0, 1), (1, 0))):
                    last = nc.tensor.matmul(dst, left[a_], right[b_], start=(k == 0), stop=(k == 2))
                return last

            def qk_mm(b, j, p, x):
                if not (isinstance(p, int) and p == 0):
                    pe.wait_ge(qk_ready, p + x)
                if j == 0:
                    pe.wait_ge(xr_ready, b + 1 + x)
                for k in range(2):
                    cols_k = slice(HEADS * HD * k + P * j, HEADS * HD * k + P * j + P)
                    last = three_passes(ps_qk[:, T * k:T * k + T],
                                        (w_qk_high[x][:, cols_k],
                                         w_low[:, cols_k]),
                                        (xr[:, 0, :], xr[:, 1, :]))
                last.then_inc(q_mm, 1)

            def v_mm_(b, j, p, x, ctx_before):
                pe.wait_ge(xb_ready, b + 1 + x)
                if not (isinstance(p, int) and p == 0):
                    pe.wait_ge(v_ready, p + x)
                if ctx_before:
                    pe.wait_ge(ctxT_ready, p - 2)
                for i in range(2):
                    last = nc.tensor.matmul(ps_v[:, P * i:P * i + P], xb[:, P * i:P * i + P],
                                            aw[:, 2, P * j:P * j + P], start=True, stop=True)
                last.then_inc(v_mm, 1)

            def turn_probs(h, p, a, waits):
                pe.wait_ge(exp_done, h * 2 + 2)
                if waits:
                    pe.wait_ge(pt_copied[a], p)
                for kc in range(2):
                    for i in range(2):
                        last = nc.tensor.transpose(ps_y[:, a, T * kc + P * i:T * kc + P * i + P],
                                                   probs[:, a, i, P * kc:P * kc + P], ident)
                last.then_inc(tr_done, 1)

            def values(h, p, j, a, x, waits):
                pe.wait_ge(pt_copied[a], p + 1)
                pe.wait_ge(v_ready, p + 1 + x)
                if a == 0 and waits:
                    pe.wait_ge(normed, p)
                for i in range(2):
                    for kc in range(2):
                        last = nc.tensor.matmul(ps_ctx[:, P * i + HD * a:P * i + HD * a + HD],
                                                probsT[:, a, kc, P * i:P * i + P],
                                                v_sb[:, j % 2, kc, HD * a:HD * a + HD],
                                                start=(kc == 0), stop=(kc == 1))
                last.then_inc(pv_done, 1)

            def turn_ctx(p, last_v):
                pe.wait_ge(normed, p + 1)
                pe.wait_ge(v_ready, last_v)
                for i in range(2):
                    last = nc.tensor.transpose(ps_v[:, T + P * i:T + P * i + P], ctx_sb[:, i, :], ident)
                last.then_inc(ctxt_done, 1)

            def project(p, j, b_out):
                pe.wait_ge(ctxT_ready, p + 1)
                if j == 0 and b_out is not None:
                    pe.wait_ge(o_evicted, b_out)
                for i in range(2):
                    last = nc.tensor.matmul(ps_o[:, P * i:P * i + P], ctxT[:, P * i:P * i + P],
                                            aw[:, 3, P * j:P * j + P], start=(j == 0 and i == 0), stop=(j == PAIRS - 1),
                                            skip_group_check=True)
                last.then_inc(out_done, 1)

            def attend(b, x, first):
                for j in range(PAIRS):
                    p = b * PAIRS + j
                    for a in range(2):
                        h = p * 2 + a
                        early = first and j == 0
                        pe.wait_ge(qk_ready, p + 1 + x)
                        if not early:
                            pe.wait_ge(exp_done, h * 2 - 2)
                        for i in range(2):
                            rows_a = slice(HD * a, HD * a + HD)
                            last = three_passes(ps_s[a][:, T * i:T * i + T],
                                                [qT[rows_a, j % 2, k, P * i:P * i + P] for k in range(2)],
                                                [kT[rows_a, j % 2, k, :] for k in range(2)])
                        last.then_inc(scores_done, 1)
                        if not (early and a == 0):
                            turn_probs(h - 1, p - 1 + a, 1 - a, not (first and 2 * j + a - 1 < 2))
                        if not early:
                            values(h - 2, p - 1, (j - 1) % PAIRS, a, x, not (first and j == 1))
                        if a == 0:
                            if not (first and j < 2):
                                turn_ctx(p - 2, p + 1 + x)
                            qk_mm(b + (j + 1) // PAIRS, (j + 1) % PAIRS, p + 1, x)
                        else:
                            v_mm_(b + (j + 1) // PAIRS, (j + 1) % PAIRS, p + 1, x, not (first and j < 2))
                            if not (first and j < 2):
                                jo = (j - 2) % PAIRS
                                project(p - 2, jo, None if first else b)

            def attend_half(b0, x):
                pe.wait_ge(w_split, x + 1)
                qk_mm(b0, 0, b0 * PAIRS, x)
                v_mm_(b0, 0, b0 * PAIRS, x, False)
                attend(b0, x, True)
                with pe.Fori(b0 + 1, b0 + HB) as b:
                    attend(b, x, False)
                p = (b0 + HB) * PAIRS
                turn_probs(2 * p - 1, p - 1, 1, True)
                values(2 * p - 2, p - 1, PAIRS - 1, 0, x, True)
                values(2 * p - 1, p - 1, PAIRS - 1, 1, x, True)
                for q in (p - 2, p - 1):
                    turn_ctx(q, p + 1 + x)
                    project(q, q % PAIRS, None)

            attend_half(0, 0)

            pe.wait_ge(experts_loaded, 32)
            pe.wait_ge(table_loaded, 32)
            pe.wait_ge(o_evicted, HB)
            pe.wait_ge(v_ready, HB * PAIRS + 1)
            pe.wait_ge(qk_ready, HB * PAIRS + 1)
            for h in range(2):
                pe.sem_inc(h_turned[h], 1)
            words = pair_row[:, :].bitcast(I32)

            def turn_slots(it, h):
                pe.wait_ge(x_in[h], 16 * (it + 1))
                if not isinstance(it, int):
                    pe.wait_ge(xT_ready[h], it)
                for s in range(4):
                    last = nc.tensor.transpose(ps_rec[h][:, P * s:P * s + P], slots_x[:, h, P * s:P * s + P], ident)
                last.then_inc(x_turned[h], 1)

            def turn_hidden(it, h):
                pe.wait_ge(silu1_done[h], it + 2)
                for s in range(4):
                    last = nc.tensor.transpose(ps_y[:, h, P * s:P * s + P], hid[:, h, P * s:P * s + P], ident)
                last.then_inc(h_turned[h], 1)

            for h in range(2):
                turn_slots(0, h)
            with pe.Fori(0, NBODY) as it:
                pairs = []
                for h in range(2):
                    word = pe.value_load(words[0:1, bass.ds(it * 2 + h, 1)], min_val=0, max_val=2 ** 31 - 1)
                    pairs.append([nc.s_assert_within((word // 256 ** s) % 128, 0, E1 // 2 - 1,
                                                     skip_runtime_bounds_check_because="the table holds pairs")
                                  for s in range(4)])
                    pe.wait_ge(xT_ready[h], it + 1)
                    pe.wait_ge(silu1_done[h], it + 1)
                    for s in range(4):
                        last = nc.tensor.matmul(ps_up[h][:, P * s:P * s + P], slots_xT[:, h, P * s:P * s + P],
                                                gate1[:, bass.ds(pairs[h][s] * P, P)], start=True, stop=True)
                    last.then_inc(up1_done[h], 1)
                turn_hidden(it, 0)
                turn_slots(it + 1, 0)
                turn_hidden(it, 1)
                turn_slots(it + 1, 1)
                for h in range(2):
                    pe.wait_ge(hT_ready[h], it + 1)
                    pe.wait_ge(y_out[h], it + 1)
                    for s in range(4):
                        last = nc.tensor.matmul(ps_t[h][:, P * s:P * s + P], hidT[:, h, P * s:P * s + P],
                                                down1[:, :, :].rearrange("p k n -> p (k n)")[
                                                    :, bass.ds(pairs[h][s] * P, P)], start=True, stop=True)
                    last.then_inc(down1_done[h], 1)
            for g in range(NG):
                if g >= 2:
                    pe.wait_ge(shared_ready, g - 1)
                nc.tensor.matmul(ps_y[0:F1, g % 2, :], sg_w[:, :], xnT[:, 512 * g:512 * g + 512],
                                 start=True, stop=True).then_inc(shared_mm, 1)
            pe.wait_ge(shared_ready, NG)
            for h in range(2):
                pe.wait_ge(y_stored[h], 16 * (NBODY + 1))
                pe.wait_ge(xT_ready[h], NBODY + 1)
                pe.wait_ge(y_out[h], NBODY + 1)
                pe.wait_ge(x_in[h], 16 * (NBODY + 2))
            attend_half(HB, 1)
            pe.wait_ge(o_evicted, B)
            for g in range(NG):
                if g >= 2:
                    pe.wait_ge(y1_ready, g - 1)
                for s in range(4):
                    n = 4 * g + s
                    last = nc.tensor.matmul(ps_y[:, g % 2, P * s:P * s + P], hsT[0:F1, P * n:P * n + P], sd_w[:, :],
                                            start=True, stop=True)
                last.then_inc(shared_y, 1)

        @block.vector
        def _(dve):
            steps = Count(dve_done)

            def chain(ins):
                dve.wait_ge(dve_done, steps.raised_by(ins))

            def across(col, shape):
                return col.unsqueeze(len(shape) - 1).to_broadcast(shape)

            V = nc.vector
            chain(V.memset(eps_col[:, :], EPS))

            def layer_norm(layer, scratch):
                for c in range(4):
                    s = slice(8 * c, 8 * c + 8)
                    if layer == 0:
                        dve.wait_ge(x_loaded[c], 16)
                    chain(V.tensor_reduce(ln_sum[:, s], x_tok[:, s, :], AX_X, ALU.add))
                    chain(V.tensor_scalar(ln_mean[:, s], ln_sum[:, s], 1.0 / P, None, ALU.mult))
                    V.tensor_tensor(xn_tok[:, s, :], x_tok[:, s, :], across(ln_mean[:, s], [P, 8, P]), ALU.subtract) \
                        .then_inc(centred, 1)
                for c in range(4):
                    s = slice(8 * c, 8 * c + 8)
                    dve.wait_ge(squared, 4 * layer + c + 1)
                    red = V.tensor_reduce(ln_sq[:, s],
                                          scratch[:, 1024 * c:1024 * c + 1024].rearrange("p (n d) -> p n d", d=P),
                                          AX_X, ALU.add)
                red.then_inc(var_ready, 1)
                dve.wait_ge(std_ready, layer + 1)
                chain(V.reciprocal(ln_rstd[:, :], ln_std[:, :]))
                for c in range(4):
                    s = slice(8 * c, 8 * c + 8)
                    V.tensor_tensor(xn_tok[:, s, :], xn_tok[:, s, :], across(ln_rstd[:, s], [P, 8, P]), ALU.mult) \
                        .then_inc(xn_ready, 1)

            layer_norm(0, scr2)
            dve.wait_ge(consts_loaded, 16 * 7)
            chain(V.tensor_scalar(halfw[:, :], halfw[:, :], 0.5, None, ALU.mult))
            chain(V.tensor_tensor(gin_bias[:, 0:2], cols_sb[:, 0:2], cols_sb[:, 3:5], ALU.add))
            chain(V.tensor_copy(gin_bias[:, 2:3], cols_sb[:, 6:7]))
            V.scalar_tensor_tensor(out=gin_bias[:, 3:4], in0=cols_sb[:, 2:3], scalar=2.0, in1=cols_sb[:, 5:6],
                                   op0=ALU.mult, op1=ALU.add).then_inc(biases_ready, 1)
            dve.wait_ge(biases_ready, 1)
            for g in range(NG):
                dve.wait_ge(gin_mm, 4 * g + 3)
                V.tensor_scalar(gin[:, 2, 2 * g:2 * g + 2, :], ps_y[:, 0, :].rearrange("p (b t) -> p b t", b=2),
                                gin_bias[:, 2:3], None, ALU.add).then_inc(gin_dve, 1)
                dve.wait_ge(gin_mm, 4 * g + 4)
                V.tensor_scalar(gin[:, 3, 2 * g:2 * g + 2, :], ps_y[:, 1, :].rearrange("p (b t) -> p b t", b=2),
                                2.0, gin_bias[:, 3:4], ALU.mult, ALU.add).then_inc(gin_dve, 1)

            def s3(a, k):
                return scr[:, a:a + NT * k].rearrange("p (n e) -> p n e", e=k)

            lg, eq = s3(0, 8), s3(256, 8)
            oh = s3(1024, 16)
            col = [scr[:, 2560 + NT * k:2560 + NT * k + NT] for k in range(8)]
            wide = [P, NT, 8]
            dve.wait_ge(logits_ready, 1)
            psl = ps_rec[0][:, 0:320].rearrange("p (n e) -> p n e", e=10)
            chain(V.tensor_copy(gate[:, :, :], psl[:, :, 8:10]))
            chain(V.tensor_reduce(col[0], psl[:, :, 0:8], AX_X, ALU.max))
            V.tensor_tensor(lg, psl[:, :, 0:8], across(col[0], wide), ALU.subtract).then_inc(shifted, 1)
            dve.wait_ge(exps_ready, 2)
            chain(V.tensor_scalar(gate[:, :, :], gate[:, :, :], 1.0, 0.25, ALU.add, ALU.mult))
            chain(V.tensor_reduce(col[0], lg, AX_X, ALU.add))
            chain(V.reciprocal(col[1], col[0]))
            chain(V.tensor_tensor(lg, lg, across(col[1], wide), ALU.mult))
            for k in range(2):
                ohk = oh[:, :, 8 * k:8 * k + 8]
                chain(V.tensor_reduce(col[2 + k], lg, AX_X, ALU.max))
                chain(V.tensor_tensor(eq, lg, across(col[2 + k], wide), ALU.is_equal))
                chain(V.tensor_tensor(eq, eq, desc.unsqueeze(1).to_broadcast(wide), ALU.mult))
                chain(V.tensor_reduce(col[4], eq, AX_X, ALU.max))
                chain(V.tensor_tensor(ohk, eq, across(col[4], wide), ALU.is_equal))
                if k == 0:
                    chain(V.scalar_tensor_tensor(out=lg, in0=ohk, scalar=-4.0, in1=lg, op0=ALU.mult, op1=ALU.add))
            V.tensor_tensor(col[5], col[2], col[3], ALU.add).then_inc(onehot_ready, 1)
            dve.wait_ge(onehot_ready, 1)
            chain(V.reciprocal(col[6], col[5]))
            for k in range(2):
                chain(V.tensor_tensor(col[2 + k], col[2 + k], col[6], ALU.mult))
            dve.wait_ge(ranks_ready, 2)
            a, b_ = scr[:, 3072:3584], scr[:, 3584:4096]
            chain(V.tensor_copy(a, ps_rec[0][:, :]))
            for k in (16, 32, 64, 128, 256):
                chain(V.tensor_copy(b_[:, 0:k], a[:, 0:k]))
                chain(V.tensor_tensor(b_[:, k:512], a[:, k:512], a[:, 0:512 - k], ALU.add))
                a, b_ = b_, a
            chain(V.tensor_tensor(a, a, ps_rec[0][:, :], ALU.subtract))
            chain(V.tensor_tensor(a, a, ps_rec[1][:, :], ALU.add))
            chain(V.scalar_tensor_tensor(out=b_, in0=a, scalar=float(CAP0), in1=scr[:, 1024:1536],
                                         op0=ALU.is_le, op1=ALU.mult))
            kept, slot_f, lost = (scr[:, 2048 + 64 * k:2112 + 64 * k] for k in range(3))
            a3 = a.rearrange("p (n e) -> p n e", e=16)
            chain(V.tensor_tensor(a3, a3, slot_base.unsqueeze(1).to_broadcast([P, NT, 16]), ALU.add))
            chain(V.tensor_tensor(a, a, b_, ALU.mult))
            chain(V.tensor_reduce(slot_f, a.rearrange("p (m e) -> p m e", e=8), AX_X, ALU.add))
            chain(V.tensor_reduce(kept, b_.rearrange("p (m e) -> p m e", e=8), AX_X, ALU.add))
            for k in range(2):
                chain(V.tensor_tensor(w0[:, :, k], col[2 + k], kept.rearrange("p (n k) -> p n k", k=2)[:, :, k],
                                      ALU.mult))
            chain(V.tensor_scalar(lost, kept, -1.0, 1.0, ALU.mult, ALU.add))
            chain(V.scalar_tensor_tensor(out=slot_from[:, :, :].rearrange("p n k -> p (n k)"), in0=lost,
                                         scalar=float(SLOTS0), in1=slot_f, op0=ALU.mult, op1=ALU.add))
            chain(V.tensor_tensor(lost, lost, spare, ALU.mult))
            V.tensor_tensor(slot_to[:, :, :].rearrange("p n k -> p (n k)"), lost, slot_f, ALU.add) \
                .then_inc(slots0_ready, 1)
            dve.wait_ge(slots0_ready, 1)
            V.memset(hist_s[:, :, 0], 0.0).then_inc(ssm_ready, 1)
            V.memset(hist_g[:, :, 0], 0.0).then_inc(rnn_ready, 1)
            dve.sem_inc(y0_out, 1)

            def step(t):
                dve.wait_ge(n_done, t + 1)
                dve.wait_ge(thr_ready, t + 1)
                V.scalar_tensor_tensor(out=mixn[:, :], in0=ps_n[:, 0:16], scalar=cols_sb[:, 5:6], in1=th_r[:, :],
                                       op0=ALU.add, op1=ALU.mult).then_inc(dve_step, 1)
                V.tensor_tensor(pren[:, :], ps_n[:, 0:16], gin[:, 3, :, t], ALU.add).then_inc(dve_step, 1)
                dve.wait_ge(dve_step, t * 5 + 2)
                V.tensor_tensor(sumn[:, :], mixn[:, :], pren[:, :], ALU.add).then_inc(sumn_ready, 1)
                dve.wait_ge(thzv_ready, t + 1)
                V.tensor_scalar(omz[:, :], th_zv[:, 0, :], -1.0, 1.0, ALU.mult, ALU.add).then_inc(dve_step, 1)
                V.scalar_tensor_tensor(out=zg[:, :], in0=th_zv[:, 0, :], scalar=1.0, in1=hist_g[:, :, t],
                                       op0=ALU.add, op1=ALU.mult).then_inc(dve_step, 1)
                V.scalar_tensor_tensor(out=hist_s[:, :, t + 1], in0=th_zv[:, 1, :], scalar=1.0,
                                       in1=ps_zv[:, 16:32], op0=ALU.add, op1=ALU.mult).then_inc(ssm_ready, 1)
                dve.wait_ge(cand_ready, t + 1)
                dve.wait_ge(dve_step, t * 5 + 3)
                V.tensor_tensor(newn[:, :], omz[:, :], cand[:, :], ALU.mult).then_inc(dve_step, 1)
                dve.wait_ge(dve_step, t * 5 + 5)
                V.scalar_tensor_tensor(out=hist_g[:, :, t + 1], in0=zg[:, :], scalar=0.5, in1=newn[:, :],
                                       op0=ALU.mult, op1=ALU.add).then_inc(rnn_ready, 1)
                dve.wait_ge(rnn_ready, t + 2)

            def unit(e, g):
                for j in range(5):
                    step(STEPS_BEFORE + g * 5 + j)
                dve.wait_ge(down_done, g * 4 + 4)
                dve.wait_ge(y0_stored, 16 * (g + 1))
                V.tensor_tensor(slots0_y[:, :, :], ps_y[:, 0, 0:256].rearrange("p (s d) -> p s d", d=P),
                                b2_sb[:, bass.ds(e * P, P)].unsqueeze(1).to_broadcast([P, 2, P]), ALU.add) \
                    .then_inc(y0_out, 1)

            with dve.Fori(0, STEPS_BEFORE // 4) as u:
                for j in range(4):
                    step(u * 4 + j)
            with dve.Fori(0, E0) as e:
                with dve.Fori(0, UNITS0) as i:
                    unit(e, e * UNITS0 + i)
            with dve.Fori((STEPS_BEFORE + STEPS_MOE) // 4, T // 4) as u:
                for j in range(4):
                    step(u * 4 + j)
            V.memset(hist_s[64:96, :, :], 2.0).then_inc(bias_rows, 1)
            for n in range(NT):
                dve.wait_ge(y_scaled, n + 1)
                V.scalar_tensor_tensor(out=gin[:, 2, n // 2, 128 * (n % 2):128 * (n % 2) + 128],
                                       in0=ps_t[n % 2][:, 0:128], scalar=gate[:, n, 1:2],
                                       in1=gin[:, 1, n // 2, 128 * (n % 2):128 * (n % 2) + 128],
                                       op0=ALU.mult, op1=ALU.add).then_inc(y_used, 1)
                if n >= NT // 2:
                    if n == NT // 2:
                        dve.wait_ge(gathered0, 16 * NT * 2)
                    for m in (2 * n - NT, 2 * n - NT + 1):
                        V.tensor_scalar(xn_tok[:, m, :], xn_tok[:, m, :], w0[:, m, 0:1], None, ALU.mult) \
                            .then_inc(first_scaled, 1)
                    for m in (2 * n - NT, 2 * n - NT + 1):
                        dve.wait_ge(first_scaled, m + 1)
                        last = V.scalar_tensor_tensor(out=xn_tok[:, m, :], in0=second[:, m, :], scalar=w0[:, m, 1:2],
                                                      in1=xn_tok[:, m, :], op0=ALU.mult, op1=ALU.add)
                    if n % 4 == 3:
                        last.then_inc(acc_final, 1)
            sil = gin[:, 0, :, :].rearrange("p b t -> p (b t)")
            moe = xn_tok[:, :, :].rearrange("p n d -> p (n d)")
            s_all = gin[:, 2, :, :].rearrange("p b t -> p (b t)")
            x_all = x_tok[:, :, :].rearrange("p n d -> p (n d)")
            quarters = [slice(1024 * c, 1024 * c + 1024) for c in range(4)]
            dve.wait_ge(y_used, NT)
            for c, q in enumerate(quarters):
                dve.wait_ge(silu_th, c + 1)
                chain(V.scalar_tensor_tensor(out=sil[:, q], in0=sil[:, q], scalar=1.0, in1=moe[:, q],
                                             op0=ALU.add, op1=ALU.mult))
                chain(V.tensor_tensor(sil[:, q], sil[:, q], s_all[:, q], ALU.mult))
                V.tensor_tensor(x_all[:, q], x_all[:, q], sil[:, q], ALU.add).then_inc(x1_ready, 2)

            dve.wait_ge(x1_ready, NG)
            layer_norm(1, att_flat)
            dve.wait_ge(attn_loaded, 16 * 9)
            chain(V.tensor_copy(upper_b, upper))
            chain(V.tensor_copy(ones_b, ones))
            chain(V.tensor_copy(sel_b, cnt_f[:, 0:63]))
            part_b = tile_tot[0:1, :]
            chain(V.memset(bias_b, 0.0))
            for k in range(3):
                chain(V.tensor_copy(part_b, rrow))
                last = V.tensor_copy(bias_b[32 * k:32 * k + 1, :], part_b)
                if k < 2:
                    chain(V.tensor_tensor(rrow, rrow, part_b, ALU.subtract))
            last.then_inc(bias_split, 1)
            def mark(n):
                dve.wait_ge(top_found, n + 1)
                V.match_replace(out=place[:, n, :], in_to_replace=top8[:, n, :], in_values=comb[:, n, :],
                                imm_value=-1.0).then_inc(marked, 1)

            for n in range(NT):
                dve.wait_ge(probs1_ready, n + 1)
                V.max(top8[:, n, :], comb[:, n, :]).then_inc(top_found, 1)
                if n:
                    mark(n - 1)
            mark(NT - 1)
            for c in range(4):
                dve.wait_ge(marked, 8 * c + 8)
                V.tensor_scalar(chosen[:, 8 * c:8 * c + 8, :], place[:, 8 * c:8 * c + 8, :], 0.0, None, ALU.is_lt) \
                    .then_inc(chosen_ready, 1)
            chain(V.memset(junk[:, 0, :], 1.0))
            dve.wait_ge(counts_mm, 1)
            chain(V.tensor_scalar(cnt_i, ps_up[0][:, 0:E1], float(P - 1), None, ALU.add))
            chain(V.tensor_scalar(cnt_i, cnt_i, 7, None, ALU.arith_shift_right))
            chain(V.tensor_copy(cnt_f, cnt_i))
            chain(V.tensor_tensor_scan(cnt_inc, junk[:, 0, :], cnt_f, 0.0, ALU.mult, ALU.add))
            dve.wait_ge(counts_mm, 2)
            V.tensor_copy(tile_tot, ps_up[1][0:NT, 0:E1]).then_inc(tot_ready, 1)
            chain(V.tensor_tensor(offs, cnt_inc, cnt_f, ALU.subtract))
            chain(V.tensor_scalar(offs, offs, float(P), None, ALU.mult))

            def placed(n):
                dve.wait_ge(place_read, n + 1)
                V.tensor_tensor(place[:, n, :], place[:, n, :], chosen[:, n, :], ALU.mult).then_inc(place_ready, 1)

            def places_of(n):
                dve.wait_ge(place_ready, n + 1)
                return V.max(place8[:, n, :], place[:, n, :])

            for n in range(NT):
                dve.wait_ge(place_mm, n + 1)
                V.tensor_tensor(place[:, n, :], ps_rec[n % 2][:, 0:E1], offs, ALU.add).then_inc(place_read, 1)
                if n >= 1:
                    placed(n - 1)
                if n >= 2:
                    places_of(n - 2)
            placed(NT - 1)
            places_of(NT - 2)
            chain(places_of(NT - 1))
            V.tensor_scalar(slot[:, :, :], place8[:, :, :], -1.0, None, ALU.add).then_inc(slots_ready, 1)
            w_qk = aw[:, 0:2, :].rearrange("p k n -> p (k n)")
            dve.wait_ge(wq_scaled, 2)
            chain(V.tensor_copy(w_qk_high[0], w_qk))
            V.tensor_tensor(w_low[:, :], w_qk, w_qk_high[0].bitcast(F32), ALU.subtract).then_inc(w_split, 1)
            for c in range(4):
                chain(V.tensor_scalar(junk[:, c % 2, :], cnt_inc, jcol[:, c:c + 1], None, ALU.is_le))
                last = V.tensor_reduce(tile_e[:, c:c + 1], junk[:, c % 2, :], AX_X, ALU.add)
            chain(last)
            chain(V.tensor_scalar(tile_e[:, :], tile_e[:, :], float(E1 - 1), None, ALU.min))
            chain(V.tensor_copy(tile_i[:, :], tile_e[:, :]))
            chain(V.tensor_scalar(tile_i[:, :], tile_i[:, :], 1, None, ALU.arith_shift_right))
            chain(V.tensor_copy(tile_par[:, :], tile_i[:, :]))
            V.tensor_copy(tile_u8[:, :], tile_par[:, :]).then_inc(table_ready, 1)
            dve.wait_ge(table_ready, 1)
            V.scalar_tensor_tensor(out=tile_par[:, :], in0=tile_par[:, :], scalar=-2.0, in1=tile_e[:, :],
                                   op0=ALU.mult, op1=ALU.add).then_inc(table_ready, 1)
            chain(V.tensor_reduce(ln_sum[:, :], top8[:, :, :], AX_X, ALU.add))
            chain(V.tensor_scalar(ln_sum[:, :], ln_sum[:, :], 1e-9, None, ALU.add))
            chain(V.reciprocal(ln_mean[:, :], ln_sum[:, :]))

            def weights_of(n, k):
                if not (isinstance(n, int) and n == 0 and k < 2):
                    dve.wait_ge(weights_done, n * TOPK1 + k - 1)
                V.scalar_tensor_tensor(out=junk[:, k % 2, :], in0=place[:, n, :], scalar=place8[:, n, k:k + 1],
                                       in1=comb[:, n, :], op0=ALU.is_equal, op1=ALU.mult,
                                       accum_out=w8[:, n, k:k + 1]).then_inc(weights_done, 1)

            def add_row(m, t4, k):
                n = m * 4 + t4
                dve.wait_ge(gathered[(t4 % 2) * 8 + k], 16 * (m * 2 + t4 // 2 + 1))
                row = rows_g[:, (t4 % 2) * 8 + k, :]
                if k == 0:
                    V.tensor_scalar(xn_tok[:, n, :], row, w8[:, n, 0:1], None, ALU.mult).then_inc(acc1_used, 1)
                else:
                    dve.wait_ge(acc1_used, m * 32 + t4 * 8 + k)
                    V.scalar_tensor_tensor(out=xn_tok[:, n, :], in0=row, scalar=w8[:, n, k:k + 1],
                                           in1=xn_tok[:, n, :], op0=ALU.mult, op1=ALU.add).then_inc(acc1_used, 1)

            def inputs_low(b, x):
                dve.wait_ge(xr_high, b + 1 + x)
                V.tensor_tensor(xr[:, 1, :], xnT[:, bass.ds((b % B) * T, T)], xr[:, 0, :].bitcast(F32), ALU.subtract) \
                    .then_inc(xr_ready, 1)

            def qk_low(p, j, x):
                dve.wait_ge(qk_high, p + 1 + x)
                for k, dst in enumerate((qT, kT)):
                    last = V.scalar_tensor_tensor(out=dst[:, j % 2, 1, :], in0=ps_qk[:, T * k:T * k + T],
                                                  scalar=acols[:, k, j:j + 1], in1=dst[:, j % 2, 0, :].bitcast(F32),
                                                  op0=ALU.add, op1=ALU.subtract)
                last.then_inc(qk_ready, 1)

            def values_out(p, j, x, waits):
                dve.wait_ge(v_mm, p + 1 + x)
                if waits:
                    dve.wait_ge(pv_done, p * 2 - 2)
                V.tensor_tensor(v_sb[:, j % 2, :, :], ps_v[:, 0:2 * P].rearrange("p (i d) -> p i d", i=2),
                                arows[:, P * j:P * j + P].unsqueeze(1).to_broadcast([P, 2, P]), ALU.add) \
                    .then_inc(v_ready, 1)

            def probs_out(h, waits):
                dve.wait_ge(tr_done, h + 1)
                if waits:
                    dve.wait_ge(pv_done, h - 1)
                V.tensor_copy(probsT[:, 0, :, :].rearrange("p c t -> p (c t)"), ps_y[:, 0, :]).then_inc(pt_copied[0], 1)

            def normalise(p, j, waits):
                dve.wait_ge(pv_done, p * 2 + 2)
                V.reciprocal(rsums[:, :, :], sums[:, j % 4, :, :]).then_inc(recip_done, 1)
                dve.wait_ge(recip_done, p + 1)
                if waits:
                    dve.wait_ge(ctxt_done, p)
                V.tensor_tensor(ctx_sb[:, :, :].rearrange("p i (a d) -> p (i a) d", a=2),
                                ps_ctx[:, 0:2 * P].rearrange("p (k d) -> p k d", k=4),
                                rsums[:, :, :].rearrange("p i a -> p (i a)").unsqueeze(2).to_broadcast([P, 4, HD]),
                                ALU.mult).then_inc(normed, 1)

            def output_out(b):
                dve.wait_ge(out_done, b * PAIRS + PAIRS)
                V.tensor_tensor(att[:, bass.ds(b * 2, 2), :], ps_o[:, 0:2 * P].rearrange("p (i d) -> p i d", i=2),
                                arows[:, HEADS * HD:].unsqueeze(1).to_broadcast([P, 2, P]), ALU.add) \
                    .then_inc(o_evicted, 1)

            def attend(b, x, first):
                for j in range(PAIRS):
                    p = b * PAIRS + j
                    for a in range(2):
                        h = p * 2 + a
                        if a == 0 and not (first and j < 2):
                            normalise(p - 2, (j - 2) % PAIRS, not (first and j == 2))
                        dve.wait_ge(scores_done, h + 1)
                        V.tensor_reduce(negmax[:, a, :], ps_s[a][:, :].rearrange("p (i t) -> p i t", i=2), AX_X,
                                        ALU.max, negate=True).then_inc(max_ready, 1)
                        if a == 1:
                            qk_low(p + 1, (j + 1) % PAIRS, x)
                            probs_out(h - 1, not (first and j == 0))
                            if j == PAIRS - 2:
                                inputs_low(b + 1, x)
                            values_out(p + 1, (j + 1) % PAIRS, x, not (first and j == 0))
                            if j == 1 and not first:
                                output_out(b - 1)
                        if a == 0:
                            for k in range(4):
                                if x == 0:
                                    weights_of(b * 4 + j // 2, j % 2 * 4 + k)
                                else:
                                    add_row(b - HB, j // 2, j % 2 * 4 + k)

            def attend_half(b0, x):
                inputs_low(b0, x)
                qk_low(b0 * PAIRS, 0, x)
                values_out(b0 * PAIRS, 0, x, False)
                attend(b0, x, True)
                with dve.Fori(b0 + 1, b0 + HB) as b:
                    attend(b, x, False)
                p = (b0 + HB) * PAIRS
                normalise(p - 2, (p - 2) % PAIRS, True)
                normalise(p - 1, (p - 1) % PAIRS, True)
                output_out(b0 + HB - 1)

            attend_half(0, 0)
            dve.wait_ge(weights_done, NT * TOPK1)
            chain(V.tensor_tensor(w8[:, :, :], w8[:, :, :], across(ln_mean[:, :], [P, NT, TOPK1]), ALU.mult))
            chain(V.tensor_scalar(w8[:, :, :], w8[:, :, :], 2.5, None, ALU.mult))

            dve.wait_ge(table_loaded, 32)
            chain(V.tensor_scalar(of_pair[0:F1, :], par_row[0:F1, :], -1.0, 1.0, ALU.mult, ALU.add))
            chain(V.tensor_copy(of_pair[F1:P, :], par_row[F1:P, :]))
            dve.sem_inc(y_out[1], 1)
            with dve.Fori(0, NBODY) as it:
                for h in range(2):
                    dve.wait_ge(h_turned[h], it + 2)
                    V.tensor_tensor(hidT[:, h, :].rearrange("p (s n) -> p s n", n=P),
                                    ps_y[:, h, :].rearrange("p (s n) -> p s n", n=P),
                                    of_pair[:, bass.ds(it * 8 + h * 4, 4)].unsqueeze(2).to_broadcast([P, 4, P]),
                                    ALU.mult).then_inc(hT_ready[h], 1)
                dve.wait_ge(down1_done[1], it + 1)
                dve.wait_ge(y_stored[1], 16 * (it + 1))
                V.tensor_copy(slots_y[:, 1, :], ps_t[1][:, :]).then_inc(y_out[1], 1)

            V.tensor_copy(w_qk_high[1], w_qk_high[0]).then_inc(w_split, 1)
            dve.wait_ge(w_split, 2)
            attend_half(HB, 1)
            for g in range(NG):
                q = slice(4 * g, 4 * g + 4)
                dve.wait_ge(shared_y, g + 1)
                dve.wait_ge(acc1_used, 32 * g + 32)
                V.tensor_tensor(xn_tok[:, q, :], xn_tok[:, q, :],
                                ps_y[:, g % 2, :].rearrange("p (n d) -> p n d", d=P), ALU.add).then_inc(y1_ready, 1)
            for g in range(NG):
                q = slice(4 * g, 4 * g + 4)
                dve.wait_ge(y1_silu, g + 1)
                chain(V.tensor_tensor(xn_tok[:, q, :], xn_tok[:, q, :], att[:, q, :], ALU.mult))
                V.tensor_tensor(x_tok[:, q, :], x_tok[:, q, :], xn_tok[:, q, :], ALU.add).then_inc(y1_done, 1)


def kernel(**inputs):
    import concourse.bacc as _bacc
    from concourse.bass_utils import run_bass_kernel_spmd as _run

    I = {k: np.asarray(v) for k, v in inputs.items()}
    f = np.float32

    def padT(w):
        m = np.zeros((P, P), w.dtype)
        m[:w.shape[1], :w.shape[0]] = w.T
        return m

    wih, whh = I["L0_attn_W_ih"], I["L0_attn_W_hh"]
    gin_w = np.concatenate([wih[0:128].T, wih[128:256].T, padT(I["L0_attn_Bw"]), wih[256:384].T], 1)
    cw = padT(I["L0_attn_Cw"])
    cw[64], cw[65] = I["L0_attn_Cb"], I["L0_attn_Db"]
    half_w = np.concatenate([whh[0:128].T, whh[128:256].T, whh[256:384].T, padT(I["L0_attn_A"]),
                             cw, I["L0_attn_proj_w"].T], 1)
    desc = np.tile(np.arange(8, 0, -1, dtype=f)[None], (P, 1))
    slot_base = np.tile(np.array([e * 2 * CAP0 + k * CAP0 - 1 for k in range(2) for e in range(E0)], f)[None], (P, 1))
    spare = np.array([[SLOTS0 + k * NTOK + n * P + p for n in range(NT) for k in range(2)] for p in range(P)], f)
    misc = np.concatenate([np.eye(P, dtype=f), np.triu(np.ones((P, P), f)), np.ones((P, P), f),
                           I["L0_attn_Dw"].T, desc, I["L0_ffn_Wr"], I["L0_attn_gate_w"].T, slot_base, spare], 1)
    bb = np.zeros((P, 1), f)
    bb[:64, 0] = I["L0_attn_Bb"]
    cols = np.concatenate([I["L0_attn_b_ih"].reshape(3, P).T, I["L0_attn_b_hh"].reshape(3, P).T, bb,
                           np.zeros((P, 1), f)], 1)
    rows = np.concatenate([I["L0_attn_Cb"], I["L0_attn_Db"], I["L0_attn_proj_b"], np.zeros(8, f),
                           I["L0_attn_gate_b"]])[None]
    arrays = {
        "x": I["L0_attn_x"].reshape(NTOK, P), "gin_w": gin_w, "half_w": half_w, "misc_w": misc, "cols": cols,
        "rows": rows, "b2": I["L0_ffn_b2"].reshape(-1), "w1": I["L0_ffn_W1"],
        "b1": I["L0_ffn_b1"].reshape(E0 * FC, P).T, "w2": I["L0_ffn_W2"],
        "attn_w": np.concatenate([I["L1_attn_wq"].T, I["L1_attn_wk"].T, I["L1_attn_wv"].T,
                                  I["L1_attn_wo"].T.reshape(PAIRS, P, P).transpose(1, 0, 2).reshape(P, -1)], 1),
        "attn_cols": np.concatenate([I["L1_attn_bq"].reshape(PAIRS, P).T, I["L1_attn_bk"].reshape(PAIRS, P).T], 1),
        "attn_rows": np.concatenate([I["L1_attn_bv"], I["L1_attn_bo"]]),
        "router": I["L1_ffn_router_w"].T, "router_row": I["L1_ffn_expert_bias"][None],
        "w_gate": I["L1_ffn_w_gate"].transpose(2, 0, 1).reshape(P, -1),
        "w_down": I["L1_ffn_w_down"].reshape(E1 // 2, 2, P, F1).transpose(1, 3, 0, 2).reshape(P, -1),
        "shared_gate": I["L1_ffn_w_gate_shared"].T, "shared_down": I["L1_ffn_w_down_shared"].T,
        "jcols": np.arange(4 * P, dtype=f).reshape(P, 4), "sel_w": np.tile(np.eye(63, dtype=f)[31], (P, 1)),
    }
    arrays = {k: np.ascontiguousarray(v) for k, v in arrays.items()}
    nc = _bacc.Bacc("TRN2", target_bir_lowering=False, num_devices=1)
    aps = {k: nc.dram_tensor(k, v.shape, mybir.dt.from_np(v.dtype), kind="ExternalInput").ap()
           for k, v in arrays.items()}
    out = nc.dram_tensor("out", (NTOK, P), F32, kind="ExternalOutput").ap()
    build(nc, out=out, **aps)
    r = _run(nc, [arrays], core_ids=[0])
    return r.results[0]["out"].reshape(B, T, P)
```
